# Optimizing a Trainium2 kernel written in Bass

```python
import numpy as np
import jax
import jax.numpy as jnp

def _softmax(x, axis=-1):
    return jax.nn.softmax(x, axis=axis)

def _gelu(x):
    return jax.nn.gelu(x, approximate=True)

def _silu(x):
    return jax.nn.silu(x)

def _sigmoid(x):
    return jax.nn.sigmoid(x)

def _layernorm(x, axis=-1, eps=1e-05):
    m = jnp.mean(x, axis=axis, keepdims=True)
    v = jnp.var(x, axis=axis, keepdims=True)
    return (x - m) / jnp.sqrt(v + eps)

def _scatter_add(tgt, idx, src, axis=0):
    return tgt.at[idx].add(src)

def _segment_sum(src, seg, n):
    return jax.ops.segment_sum(src, seg, n)
kernel_name = 'mk_lm_tower_d1_tok_ids768_r4_ccccdb'

def setup_inputs(seed: int=0):
    np.random.seed(seed)
    _w = jnp.asarray

    def _rec_inputs():
        import jax
        import jax.numpy as jnp
        _rk = jax.random.key(seed)
        x = jax.random.randint(jax.random.fold_in(_rk, 1), (16, 256), 0, 31999, jnp.int32)
        itok_BS_0_15 = jax.random.randint(jax.random.fold_in(_rk, 21), (16, 256), 0, 16, jnp.int32)
        itok_BS_0_3 = jax.random.randint(jax.random.fold_in(_rk, 22), (16, 256), 0, 4, jnp.int32)
        itok_BS_0_9999 = jax.random.randint(jax.random.fold_in(_rk, 23), (16, 256), 0, 2500, jnp.int32)
        itok_BS_0_2047 = jax.random.randint(jax.random.fold_in(_rk, 24), (16, 256), 0, 512, jnp.int32)
        fside_BS_age_tau = 49.5725 + 28.8366 * jax.random.normal(jax.random.fold_in(_rk, 25), (16, 256), jnp.float32)
        fside_BS_delays_tau = 49.8282 + 28.8637 * jax.random.normal(jax.random.fold_in(_rk, 26), (16, 256), jnp.float32)
        return (x, itok_BS_0_15, itok_BS_0_3, itok_BS_0_9999, itok_BS_0_2047, fside_BS_age_tau, fside_BS_delays_tau)
    x, itok_BS_0_15, itok_BS_0_3, itok_BS_0_9999, itok_BS_0_2047, fside_BS_age_tau, fside_BS_delays_tau = _rec_inputs()

    def _L0_tok_setup():
        import jax, jax.numpy as jnp
        import numpy as np
        B, S, H = (8, 512, 192)
        VOCAB, MODAL_V, SEG_V, NPI_V, MAX_POS = (8000, 16, 4, 2500, 512)
        LN_EPS = 1e-12

        def _sinusoidal_table(max_pos, hidden):
            pos = np.arange(max_pos, dtype=np.float32)[:, None]
            idx = np.arange(hidden, dtype=np.float32)[None, :]
            angle = pos / np.power(10000.0, 2.0 * idx / hidden)
            tab = np.where(np.arange(hidden)[None, :] % 2 == 0, np.sin(angle), np.cos(angle))
            return jnp.asarray(tab, dtype=jnp.float32)

        def _time2vec(tau, w, b, w0, b0):
            t = tau[..., None]
            v1 = jnp.sin(t * w[0] + b)
            v2 = t * w0[0] + b0
            return jnp.concatenate([v1, v2], axis=-1)

        def _layer_norm(x, gamma, beta, eps):
            mu = jnp.mean(x, axis=-1, keepdims=True)
            var = jnp.mean(jnp.square(x - mu), axis=-1, keepdims=True)
            return (x - mu) * jax.lax.rsqrt(var + eps) * gamma + beta
        key = jax.random.key(seed)
        ks = jax.random.split(key, 16)
        inp = {'word_ids': jax.random.randint(ks[0], (B, S), 0, VOCAB), 'modalities_ids': jax.random.randint(ks[1], (B, S), 0, MODAL_V), 'seg_ids': jax.random.randint(ks[2], (B, S), 0, SEG_V), 'npi_ids': jax.random.randint(ks[3], (B, S), 0, NPI_V), 'posi_ids': jnp.sort(jax.random.randint(ks[4], (B, S), 0, MAX_POS), axis=-1), 'age_tau': jax.random.uniform(ks[5], (B, S), dtype=jnp.float32) * 100.0, 'delays_tau': jax.random.uniform(ks[6], (B, S), dtype=jnp.float32) * 100.0, 'word_table': jax.random.normal(ks[7], (VOCAB, H), dtype=jnp.float32) * 0.02, 'modalities_table': jax.random.normal(ks[8], (MODAL_V, H), dtype=jnp.float32) * 0.02, 'seg_table': jax.random.normal(ks[9], (SEG_V, H), dtype=jnp.float32) * 0.02, 'npi_table': jax.random.normal(ks[10], (NPI_V, H), dtype=jnp.float32) * 0.02, 'posi_table': _sinusoidal_table(MAX_POS, H), 'age_w': jax.random.normal(ks[11], (1, H - 1), dtype=jnp.float32), 'age_b': jax.random.normal(ks[12], (H - 1,), dtype=jnp.float32), 'age_w0': jax.random.normal(ks[13], (1, 1), dtype=jnp.float32), 'age_b0': jax.random.normal(ks[14], (1,), dtype=jnp.float32), 'delay_w': jax.random.normal(ks[15], (1, H - 1), dtype=jnp.float32), 'delay_b': jax.random.normal(jax.random.fold_in(key, 100), (H - 1,), dtype=jnp.float32), 'delay_w0': jax.random.normal(jax.random.fold_in(key, 101), (1, 1), dtype=jnp.float32), 'delay_b0': jax.random.normal(jax.random.fold_in(key, 102), (1,), dtype=jnp.float32), 'ln_gamma': jnp.ones((H,), dtype=jnp.float32), 'ln_beta': jnp.zeros((H,), dtype=jnp.float32)}
        return inp
    _L0_tok_all = _L0_tok_setup()
    _L0_tok_in = {k: v for k, v in _L0_tok_all.items() if k in ('word_table', 'modalities_table', 'seg_table', 'npi_table', 'posi_table', 'age_w', 'age_b', 'age_w0', 'age_b0', 'delay_w', 'delay_b', 'delay_w0', 'delay_b0', 'ln_gamma', 'ln_beta')}
    del _L0_tok_all

    def _L0_attn_setup():
        import jax, jax.numpy as jnp
        import numpy as np
        D_MODEL = 192
        NHEAD = 12
        HEAD_DIM = D_MODEL // NHEAD
        MAX_REL = 16
        B, T = (4, 256)
        key = jax.random.key(seed)
        ks = jax.random.split(key, 6)
        s = 0.02
        return {'x': jax.random.normal(ks[0], (B, T, D_MODEL), dtype=jnp.float32), 'qkv_w': jax.random.normal(ks[1], (3 * D_MODEL, D_MODEL), dtype=jnp.float32) * s, 'qkv_b': jax.random.normal(ks[2], (3 * D_MODEL,), dtype=jnp.float32) * s, 'out_w': jax.random.normal(ks[3], (D_MODEL, D_MODEL), dtype=jnp.float32) * s, 'out_b': jax.random.normal(ks[4], (D_MODEL,), dtype=jnp.float32) * s, 'rel_pos_emb': jax.random.normal(ks[5], (2 * MAX_REL + 1, HEAD_DIM), dtype=jnp.float32)}
    _L0_attn_all = _L0_attn_setup()
    _L0_attn_in = {k: v for k, v in _L0_attn_all.items() if k in ('qkv_w', 'qkv_b', 'out_w', 'out_b', 'rel_pos_emb')}
    del _L0_attn_all

    def _L0_ffn_setup():
        import jax, jax.numpy as jnp
        import numpy as np
        ATOM = {'vm': 0, 'im': 1, 'cm': 2, 'sc': 3, 'cc': 4}
        TASK_PAIRS = [('vm', 'sc'), ('vm', 'cc'), ('im', 'sc'), ('im', 'cc'), ('cm', 'sc'), ('cm', 'cc')]
        SRC_IDX = np.array([[ATOM[l], ATOM[r]] for l, r in TASK_PAIRS], dtype=np.int32)
        DST_IDX = np.array([[ATOM[r], ATOM[l]] for l, r in TASK_PAIRS], dtype=np.int32)
        NCLS = 6
        NATOMS = 5

        def _l2norm(x, eps=1e-12):
            return x / jnp.clip(jnp.linalg.norm(x, axis=-1, keepdims=True), eps)
        key = jax.random.key(seed)
        ks = jax.random.split(key, 12)
        B, NPATCH, D, H = (64, 197, 192, 768)
        std = 0.02
        x = jax.random.normal(ks[0], (B, NCLS + NPATCH, D), dtype=jnp.float32)
        fc1_w = jax.random.normal(ks[1], (H, D), dtype=jnp.float32) * std
        fc1_b = jnp.zeros((H,), jnp.float32)
        fc2_w = jax.random.normal(ks[2], (D, H), dtype=jnp.float32) * std
        fc2_b = jnp.zeros((D,), jnp.float32)
        gate_pair = jax.random.normal(ks[3], (NCLS, 2, D), dtype=jnp.float32) * std
        atom_in_w = jax.random.normal(ks[4], (NATOMS, H, D), dtype=jnp.float32) * std
        atom_in_b = jax.random.normal(ks[5], (NATOMS, H), dtype=jnp.float32) * std
        atom_out_w = jax.random.normal(ks[6], (NATOMS, D, H), dtype=jnp.float32) * std
        atom_out_b = jax.random.normal(ks[7], (NATOMS, D), dtype=jnp.float32) * std
        balance_bias = jnp.zeros((NCLS, 2), jnp.float32)
        return {'x': x, 'fc1_w': fc1_w, 'fc1_b': fc1_b, 'fc2_w': fc2_w, 'fc2_b': fc2_b, 'gate_pair': gate_pair, 'atom_in_w': atom_in_w, 'atom_in_b': atom_in_b, 'atom_out_w': atom_out_w, 'atom_out_b': atom_out_b, 'balance_bias': balance_bias}
    _L0_ffn_all = _L0_ffn_setup()
    _L0_ffn_in = {k: v for k, v in _L0_ffn_all.items() if k in ('fc1_w', 'fc1_b', 'fc2_w', 'fc2_b', 'gate_pair', 'atom_in_w', 'atom_in_b', 'atom_out_w', 'atom_out_b', 'balance_bias')}
    del _L0_ffn_all
    return {'x': x, 'itok_BS_0_15': itok_BS_0_15, 'itok_BS_0_3': itok_BS_0_3, 'itok_BS_0_9999': itok_BS_0_9999, 'itok_BS_0_2047': itok_BS_0_2047, 'fside_BS_age_tau': fside_BS_age_tau, 'fside_BS_delays_tau': fside_BS_delays_tau, 'L0_tok_word_table': _L0_tok_in['word_table'], 'L0_tok_modalities_table': _L0_tok_in['modalities_table'], 'L0_tok_seg_table': _L0_tok_in['seg_table'], 'L0_tok_npi_table': _L0_tok_in['npi_table'], 'L0_tok_posi_table': _L0_tok_in['posi_table'], 'L0_tok_age_w': _L0_tok_in['age_w'], 'L0_tok_age_b': _L0_tok_in['age_b'], 'L0_tok_age_w0': _L0_tok_in['age_w0'], 'L0_tok_age_b0': _L0_tok_in['age_b0'], 'L0_tok_delay_w': _L0_tok_in['delay_w'], 'L0_tok_delay_b': _L0_tok_in['delay_b'], 'L0_tok_delay_w0': _L0_tok_in['delay_w0'], 'L0_tok_delay_b0': _L0_tok_in['delay_b0'], 'L0_tok_ln_gamma': _L0_tok_in['ln_gamma'], 'L0_tok_ln_beta': _L0_tok_in['ln_beta'], 'L0_attn_qkv_w': _L0_attn_in['qkv_w'], 'L0_attn_qkv_b': _L0_attn_in['qkv_b'], 'L0_attn_out_w': _L0_attn_in['out_w'], 'L0_attn_out_b': _L0_attn_in['out_b'], 'L0_attn_rel_pos_emb': _L0_attn_in['rel_pos_emb'], 'L0_ffn_fc1_w': _L0_ffn_in['fc1_w'], 'L0_ffn_fc1_b': _L0_ffn_in['fc1_b'], 'L0_ffn_fc2_w': _L0_ffn_in['fc2_w'], 'L0_ffn_fc2_b': _L0_ffn_in['fc2_b'], 'L0_ffn_gate_pair': _L0_ffn_in['gate_pair'], 'L0_ffn_atom_in_w': _L0_ffn_in['atom_in_w'], 'L0_ffn_atom_in_b': _L0_ffn_in['atom_in_b'], 'L0_ffn_atom_out_w': _L0_ffn_in['atom_out_w'], 'L0_ffn_atom_out_b': _L0_ffn_in['atom_out_b'], 'L0_ffn_balance_bias': _L0_ffn_in['balance_bias']}

def reference(x, itok_BS_0_15, itok_BS_0_3, itok_BS_0_9999, itok_BS_0_2047, fside_BS_age_tau, fside_BS_delays_tau, L0_tok_word_table, L0_tok_modalities_table, L0_tok_seg_table, L0_tok_npi_table, L0_tok_posi_table, L0_tok_age_w, L0_tok_age_b, L0_tok_age_w0, L0_tok_age_b0, L0_tok_delay_w, L0_tok_delay_b, L0_tok_delay_w0, L0_tok_delay_b0, L0_tok_ln_gamma, L0_tok_ln_beta, L0_attn_qkv_w, L0_attn_qkv_b, L0_attn_out_w, L0_attn_out_b, L0_attn_rel_pos_emb, L0_ffn_fc1_w, L0_ffn_fc1_b, L0_ffn_fc2_w, L0_ffn_fc2_b, L0_ffn_gate_pair, L0_ffn_atom_in_w, L0_ffn_atom_in_b, L0_ffn_atom_out_w, L0_ffn_atom_out_b, L0_ffn_balance_bias):
    import jax
    import jax.numpy as jnp

    def _L0_tok_ref(word_ids, modalities_ids, seg_ids, npi_ids, posi_ids, age_tau, delays_tau, word_table, modalities_table, seg_table, npi_table, posi_table, age_w, age_b, age_w0, age_b0, delay_w, delay_b, delay_w0, delay_b0, ln_gamma, ln_beta):
        import jax, jax.numpy as jnp
        import numpy as np
        B, S, H = (8, 512, 192)
        VOCAB, MODAL_V, SEG_V, NPI_V, MAX_POS = (8000, 16, 4, 2500, 512)
        LN_EPS = 1e-12

        def _sinusoidal_table(max_pos, hidden):
            pos = np.arange(max_pos, dtype=np.float32)[:, None]
            idx = np.arange(hidden, dtype=np.float32)[None, :]
            angle = pos / np.power(10000.0, 2.0 * idx / hidden)
            tab = np.where(np.arange(hidden)[None, :] % 2 == 0, np.sin(angle), np.cos(angle))
            return jnp.asarray(tab, dtype=jnp.float32)

        def _time2vec(tau, w, b, w0, b0):
            t = tau[..., None]
            v1 = jnp.sin(t * w[0] + b)
            v2 = t * w0[0] + b0
            return jnp.concatenate([v1, v2], axis=-1)

        def _layer_norm(x, gamma, beta, eps):
            mu = jnp.mean(x, axis=-1, keepdims=True)
            var = jnp.mean(jnp.square(x - mu), axis=-1, keepdims=True)
            return (x - mu) * jax.lax.rsqrt(var + eps) * gamma + beta
        word_e = word_table[word_ids]
        seg_e = seg_table[seg_ids]
        modal_e = modalities_table[modalities_ids]
        npi_e = npi_table[npi_ids]
        posi_e = posi_table[posi_ids]
        age_e = _time2vec(age_tau, age_w, age_b, age_w0, age_b0)
        delay_e = _time2vec(delays_tau, delay_w, delay_b, delay_w0, delay_b0)
        emb = word_e + seg_e + posi_e + modal_e + delay_e + age_e + npi_e
        emb = _layer_norm(emb, ln_gamma, ln_beta, LN_EPS)
        return emb

    def _L0_attn_ref(x, qkv_w, qkv_b, out_w, out_b, rel_pos_emb):
        import jax, jax.numpy as jnp
        import numpy as np
        D_MODEL = 192
        NHEAD = 12
        HEAD_DIM = D_MODEL // NHEAD
        MAX_REL = 16
        B, T = (4, 256)
        Bx, Tx, _ = x.shape
        scale = HEAD_DIM ** (-0.5)
        qkv = x @ qkv_w.T + qkv_b
        qkv = qkv.reshape(Bx, Tx, 3, NHEAD, HEAD_DIM)
        q = qkv[:, :, 0].transpose(0, 2, 1, 3)
        k = qkv[:, :, 1].transpose(0, 2, 1, 3)
        v = qkv[:, :, 2].transpose(0, 2, 1, 3)
        attn_scores = jnp.einsum('bhtd,bhsd->bhts', q, k)
        rng = jnp.arange(Tx)
        rel_pos = jnp.clip(rng[None, :] - rng[:, None], -MAX_REL, MAX_REL) + MAX_REL
        rel_emb = rel_pos_emb[rel_pos]
        rel_scores = jnp.einsum('bhtd,tsd->bhts', q, rel_emb)
        attn = jax.nn.softmax((attn_scores + rel_scores) * scale, axis=-1)
        out = jnp.einsum('bhts,bhsd->bhtd', attn, v)
        out = out.transpose(0, 2, 1, 3).reshape(Bx, Tx, D_MODEL)
        return out @ out_w.T + out_b

    def _L0_ffn_ref(x, fc1_w, fc1_b, fc2_w, fc2_b, gate_pair, atom_in_w, atom_in_b, atom_out_w, atom_out_b, balance_bias):
        import jax, jax.numpy as jnp
        import numpy as np
        ATOM = {'vm': 0, 'im': 1, 'cm': 2, 'sc': 3, 'cc': 4}
        TASK_PAIRS = [('vm', 'sc'), ('vm', 'cc'), ('im', 'sc'), ('im', 'cc'), ('cm', 'sc'), ('cm', 'cc')]
        SRC_IDX = np.array([[ATOM[l], ATOM[r]] for l, r in TASK_PAIRS], dtype=np.int32)
        DST_IDX = np.array([[ATOM[r], ATOM[l]] for l, r in TASK_PAIRS], dtype=np.int32)
        NCLS = 6
        NATOMS = 5

        def _l2norm(x, eps=1e-12):
            return x / jnp.clip(jnp.linalg.norm(x, axis=-1, keepdims=True), eps)
        src = jnp.asarray(SRC_IDX)
        dst = jnp.asarray(DST_IDX)
        D = x.shape[-1]
        H = atom_in_w.shape[1]
        cls_tokens = x[:, :NCLS]
        patch_tokens = x[:, NCLS:]
        patch_out = jax.nn.gelu(patch_tokens @ fc1_w.T + fc1_b, approximate=False) @ fc2_w.T + fc2_b
        gate_in = _l2norm(cls_tokens.astype(jnp.float32))
        gate_w = _l2norm(gate_pair.astype(jnp.float32))
        gate_logits = jnp.einsum('bnd,nrd->bnr', gate_in, gate_w) + balance_bias[None]
        route_probs = jax.nn.softmax(gate_logits, axis=-1)
        chosen_route = jnp.argmax(route_probs, axis=-1)
        hid_all = jax.nn.gelu(jnp.einsum('bnd,ahd->bnah', cls_tokens, atom_in_w) + atom_in_b[None, None], approximate=False)
        sh_pair = hid_all[:, jnp.arange(NCLS)[:, None], src, :]
        route_out_w = atom_out_w[dst.reshape(-1)].reshape(NCLS, 2, D, H)
        route_candidates = jnp.einsum('bnrh,nrdh->bnrd', sh_pair, route_out_w) + atom_out_b[dst][None]
        chosen_w = jnp.take_along_axis(route_probs, chosen_route[..., None], axis=-1)
        chosen_cand = jnp.take_along_axis(route_candidates, chosen_route[:, :, None, None], axis=2)[:, :, 0]
        cls_out = chosen_cand * chosen_w.astype(chosen_cand.dtype)
        return jnp.concatenate([cls_out, patch_out], axis=1)
    h = _L0_tok_ref(x, itok_BS_0_15, itok_BS_0_3, itok_BS_0_9999, itok_BS_0_2047, fside_BS_age_tau, fside_BS_delays_tau, L0_tok_word_table, L0_tok_modalities_table, L0_tok_seg_table, L0_tok_npi_table, L0_tok_posi_table, L0_tok_age_w, L0_tok_age_b, L0_tok_age_w0, L0_tok_age_b0, L0_tok_delay_w, L0_tok_delay_b, L0_tok_delay_w0, L0_tok_delay_b0, L0_tok_ln_gamma, L0_tok_ln_beta)
    h = h + _L0_attn_ref(_layernorm(h, axis=-1), L0_attn_qkv_w, L0_attn_qkv_b, L0_attn_out_w, L0_attn_out_b, L0_attn_rel_pos_emb)
    h = h + _L0_ffn_ref(_layernorm(h, axis=-1), L0_ffn_fc1_w, L0_ffn_fc1_b, L0_ffn_fc2_w, L0_ffn_fc2_b, L0_ffn_gate_pair, L0_ffn_atom_in_w, L0_ffn_atom_in_b, L0_ffn_atom_out_w, L0_ffn_atom_out_b, L0_ffn_balance_bias)
    return h

_drawn_inputs = setup_inputs


def setup_inputs(seed=0):
    import zlib

    import numpy as np

    out = dict(_drawn_inputs(seed))
    spreads = {'L0_tok_ln_gamma': (1.0, 0.2),
     'L0_tok_ln_beta': (0.0, 0.1),
     'L0_ffn_fc1_b': (0.0, 0.32),
     'L0_ffn_fc2_b': (0.0, 0.1),
     'L0_ffn_balance_bias': (0.0, 0.8)}
    factors = {'L0_tok_word_table': 6.33,
     'L0_tok_modalities_table': 6.21,
     'L0_tok_seg_table': 6.263,
     'L0_tok_npi_table': 6.103,
     'L0_attn_qkv_b': 8.0,
     'L0_attn_out_b': 2.977,
     'L0_attn_rel_pos_emb': 23.21,
     'L0_ffn_gate_pair': 8.0,
     'L0_ffn_atom_in_w': 8.0,
     'L0_ffn_atom_in_b': 8.0,
     'L0_ffn_atom_out_w': 8.0,
     'L0_ffn_atom_out_b': 36.893}
    for name, (base, spread) in spreads.items():
        noise = np.random.default_rng([zlib.crc32(name.encode()), seed]).standard_normal(out[name].shape)
        drawn = base * np.exp(spread * noise) if base else spread * noise
        out[name] = jnp.asarray(drawn.astype(out[name].dtype))
    for name, factor in factors.items():
        out[name] = (out[name] * factor).astype(out[name].dtype)
    return out
```

```python
import concourse.bass as bass
from concourse import mybir
from contextlib import ExitStack

F32 = mybir.dt.float32
I32 = mybir.dt.int32
ALU = mybir.AluOpType
ACT = mybir.ActivationFunctionType
AX = mybir.AxisListType

B, T, D = 16, 256, 192
P = 128
TC = T // P
TILES = B * TC
NH, HD = 12, 16
HG = 4
GRP = NH // HG
ROW = P // HG
REL = 16
NREL = 2 * REL + 1
BLK = 16
NEAR = 3 * BLK
EXT = NEAR + BLK - 1
BPT = P // BLK
KEYS = T + P + 2 * BLK
REL_AT = [BLK + P, BLK]
NEAR_AT = P
HID = 768
HT = HID // P
NTAB = 5
TABLE_ROWS = [8000, 16, 4, 2500, 512]
NCLS, NATOM = 6, 5
SCALE = -HD ** -0.5
EPS_EMB, EPS_LN, EPS_NORM = 1e-12, 1e-5, 1e-12
TURN = 6.283185307179586
TURN_HI = 6.28125
TURN_LO = TURN - TURN_HI
ROUND = 12582912.0
HALF_TURN = 3.1415925
BIG = 3.0e38
LAST = D - P


class Chain:

    def __init__(self, eng, sem):
        self.eng, self.sem, self.n, self.past = eng, sem, 0, 0

    def __call__(self, instruction):
        instruction.then_inc(self.sem, 1)
        self.n += 1
        self.eng.wait_ge(self.sem, self.past + self.n)

    def loop(self, i, steps):
        self.n0, self.steps, self.past = self.n, steps, i * steps

    def done(self, iterations):
        assert self.n - self.n0 == self.steps, (self.n - self.n0, self.steps)
        self.n, self.past = self.n0 + iterations * self.steps, 0


def wait(eng, sem, value):
    if not isinstance(value, int) or value > 0:
        eng.wait_ge(sem, value)


def wait_alone(eng, sem, value, passed):
    if not isinstance(value, int):
        eng.wait_ge(sem, value)
        eng.sem_inc(passed, 1)
    elif value > 0:
        eng.wait_ge(sem, value)


def tower(nc, io):
    with ExitStack() as ctx:
        def sb(name, shape, dt=F32):
            return ctx.enter_context(nc.sbuf_tensor(name, shape, dt))

        def sem(name):
            return ctx.enter_context(nc.semaphore(name))

        h = sb("h", [P, TILES, D])
        bn6 = sb("bn6", [P, TILES, 6])
        mean = sb("mean", [P, TILES])
        rstd = sb("rstd", [P, TILES])
        st = sb("st", [P, 4, TILES])
        ident = sb("ident", [P, P])
        xn = sb("xn", [P, TC, D])
        xT = sb("xT", [P, 2, T])
        ids = sb("ids", [P, NTAB, TILES], I32)
        idf = sb("idf", [P, 2, NTAB, TILES])
        idx = sb("idx", [P, NTAB, TILES], I32)
        idx_now = sb("idx_now", [P, 2, NTAB, TC], I32)
        tau = sb("tau", [P, 2, TILES])
        t2v_w = sb("t2v_w", [P, 2, D])
        t2v_b = sb("t2v_b", [P, 2, D])
        gamma = sb("gamma", [P, D])
        beta = sb("beta", [P, D])
        early = sb("early", [P, 9 * 2 * 2 * D])
        n_emb = 2 * TC * (NTAB + 2) * D
        emb = early[:, 0:n_emb].rearrange("p (r c j d) -> p r c j d", r=2, c=TC, j=NTAB + 2)
        angle = early[:, n_emb:n_emb + 2 * TC * D].rearrange("p (c w d) -> p c w d", c=TC, w=2)
        turns = early[:, n_emb + 2 * TC * D:n_emb + 4 * TC * D]\
            .rearrange("p (c w d) -> p c w d", c=TC, w=2)
        wout = early[:, 0:NATOM * HT * D].rearrange("p (a t d) -> p a t d", a=NATOM, t=HT)
        g_sel = sb("g_sel", [P, 2, NH, ROW])
        g_blk = sb("g_blk", [P, 2, NH])
        rel_hd = sb("rel_hd", [P, 2, NREL])
        span = sb("span", [P, 2])
        wq_n = sb("wq_n", [P, 2, D + 1])
        wq = sb("wq", [P, 2, NH * ROW])
        wk = sb("wk", [P, 2, NH, ROW])
        wk_d = sb("wk_d", [P, 2, D])
        wv = sb("wv", [P, 2, D])
        wo = sb("wo", [P, GRP, D])
        rel32 = sb("rel32", [P, NREL])
        relx = sb("relx", [P, EXT])
        rel_bd = sb("rel_bd", [P, EXT, HG])
        hmask = sb("hmask", [P, HG])
        q_mask = sb("q_mask", [P, T])
        k_ind = sb("k_ind", [P, T])
        sel_sum = sb("sel_sum", [P, P])
        qT = sb("qT", [P, GRP, T])
        kT = sb("kT", [P, GRP, T])
        mid = sb("mid", [P, GRP * HG * T])
        qm = mid[:, :].rearrange("p (g h t) -> p g h t", g=GRP, h=HG)
        v_new = sb("v_new", [P, TC, D])
        v1 = sb("v1", [P, TC, NH, ROW])
        r_sb = sb("r_sb", [P, GRP, TC, EXT * HG])
        near = sb("near", [P, GRP * TC * KEYS * HG])
        rel = near[:, :].rearrange("p (g c k h) -> p g c k h", g=GRP, c=TC, k=KEYS)
        win = near[:, 0:NATOM * 2 * HID].rearrange("p (a t n) -> p a t n", a=NATOM, t=2)
        ssum = sb("ssum", [P, 2, TC, T])
        smin = sb("smin", [P, 2, TC])
        prob = sb("prob", [P, 2, TC, T])
        late = sb("late", [P, GRP * HG * 2 * T])
        pT = late[:, :].rearrange("p (g h s t) -> p g h s t", g=GRP, h=HG, s=2)
        gT = late[:, 0:2 * HT * T].rearrange("p (r n t) -> p r n t", r=2, n=HT)
        o_sb = sb("o_sb", [P, T])
        o_inv = sb("o_inv", [P, T])
        oT = sb("oT", [P, GRP, T])
        w1 = sb("w1", [P, 2, HID])
        w2 = sb("w2", [P, HT, D])
        b2 = sb("b2", [P, D])
        NB = NCLS * B
        clsT = sb("clsT", [P, 2, NCLS, B])
        hcls = sb("hcls", [NB, D])
        bout = sb("bout", [P, 2, 2, NCLS])
        gate = sb("gate", [P, 2, NCLS, 2])
        bal = sb("bal", [P, 2, NCLS])
        ones = sb("ones", [P, P])
        taken = [0]

        def from_mid(*shape):
            n = 1
            for x in shape:
                n *= x
            part = mid[:, taken[0]:taken[0] + n]
            taken[0] += n
            names = "abcd"[:len(shape)]
            return part.rearrange(f"p ({' '.join(names)}) -> p {' '.join(names)}",
                                  **dict(zip(names, shape)))

        hidT = from_mid(HT, 2, NCLS, B)
        sq = from_mid(2, NB + 2 * NCLS)
        prod = from_mid(2, 2, NCLS, B)
        nrm = from_mid(3, NB + 2 * NCLS)
        lg = from_mid(2, NCLS, B)
        mx = from_mid(NCLS, B)
        den = from_mid(NCLS, B)
        first = from_mid(NCLS, B)
        cand = from_mid(2, 2, NCLS, B)
        ycT = sb("ycT", [P, 2, NB])

        psum = ctx.enter_context(nc.psum_tensor("psum", [P, 8, 512], F32))
        scratch = nc.dram_tensor("rel_terms", [GRP, TC, P, EXT * HG], F32).ap()

        s = {n: sem(n) for n in (
            "ids_in", "time_in", "norm_in", "attn_in", "ffn_in", "gate_in", "wout_in", "win_in",
            "dve_chain", "pool_chain", "dve_passed", "pool_passed", "sp_passed", "idx_ok", "idx_staged", "emb_free", "angles",
            "sines", "h_ready", "deviation", "zeroed",
            "g_ready", "wq_psum", "wq_ready", "wk_ready", "relbd_ready",
            "xn_ready", "xT_psum", "xT_ready", "qk_psum", "qk_ready", "qm_ready", "r_psum",
            "r_ready", "v_psum", "v_ready", "v1_ready", "s_psum", "s_min", "p_ready", "pT_psum",
            "pT_ready", "o_psum", "o_ready", "sum_psum", "oT_ready", "out_psum", "h2_ready",
            "f_psum", "f_ready", "y_psum", "y_ready", "stored", "cls_in",
            "sq_ready", "norms_psum", "root", "root_ready", "gates", "exps", "weights",
            "hid_psum", "hid_ready", "cand_psum", "cand_ready", "yc_psum", "yc_ready")}
        gathered = [sem("gathered_even"), sem("gathered_odd")]
        r_stored = [sem(f"r_stored{g}") for g in range(GRP)]
        rel_in = [sem(f"rel_in{g}") for g in range(GRP)]
        N_RD = 16 * BPT

        block = ctx.enter_context(nc.Block())

        S0, T0, OB, XB, QB, RB = 0, 2, 4, 5, 6, 7

        def phase_b(eng, slot, before_loop=None):
            def body(b, now, before, ahead):
                for k in range(NH):
                    slot(b, k, now, before, ahead)
            body(-1, False, False, True)
            body(0, True, False, True)
            with eng.Fori(1, B - 1) as b:
                if before_loop:
                    before_loop(b - 1)
                body(b, True, True, True)
            if before_loop:
                before_loop(None)
            body(B - 1, True, True, False)
            body(B, False, True, False)

        def phase_c(prepare, main, eng):
            prepare(0)
            for b in range(2):
                main(b, b)
                prepare(b + 1)
            with eng.Fori(1, B // 2 - 1) as i:
                for r in range(2):
                    main(2 * i + r, r)
                    prepare(2 * i + r + 1)
            main(B - 2, 0)
            prepare(B - 1)
            main(B - 1, 1)

        @block.sync
        def _(sp):
            def load(dst, name, sm):
                sp.dma_start(dst, io[name]).then_inc(s[sm], 16)

            load(ids[:, :, :], "ids", "ids_in")
            load(tau[:, :, :], "tau", "time_in")
            load(t2v_w[:, :, :], "t2v_w", "time_in")
            load(t2v_b[:, :, :], "t2v_b", "time_in")
            load(gamma[:, :], "gamma", "norm_in")
            load(beta[:, :], "beta", "norm_in")
            for dst, name in ((ident[:, :], "ident"), (g_sel[:, :, :, :], "g_sel"),
                              (g_blk[:, :, :], "g_blk"), (rel_hd[:, :, :], "rel_hd"),
                              (wq_n[:, :, :], "wq_n"), (wk_d[:, :, :], "wk"), (wv[:, :, :], "wv"),
                              (wo[:, :, :], "wo"), (rel32[:, :], "rel32"), (hmask[:, :], "hmask"),
                              (q_mask[:, :], "q_mask"), (k_ind[:, :], "k_ind"),
                              (sel_sum[:, :], "sel_sum")):
                load(dst, name, "attn_in")
            for dst, name in ((w1[:, :, :], "w1"), (w2[:, :, :], "w2"), (b2[:, :], "b2")):
                load(dst, name, "ffn_in")
            for dst, name in ((bout[:, :, :, :], "bout"), (gate[:, :, :, :], "gate"),
                              (bal[:, :, :], "bal"), (ones[:, :], "ones")):
                load(dst, name, "gate_in")
            sp.wait_ge(s["h_ready"], B)
            load(wout[:, :, :, :], "wout", "wout_in")

            def near_terms(b, g):
                wait_alone(sp, s["r_ready"], b * GRP + g + 1, s["sp_passed"])
                wait_alone(sp, rel_in[g], b * N_RD, s["sp_passed"])
                sp.dma_start(scratch[g].rearrange("c p e -> p c e"), r_sb[:, g, :, :])\
                    .then_inc(r_stored[g], 16)
                wait_alone(sp, r_stored[g], (b + 1) * 16, s["sp_passed"])
                wait_alone(sp, s["s_min"], (b - 1) * NH + HG * (g + 1), s["sp_passed"])
                for a in range(BPT):
                    rows = bass.AP(
                        tensor=scratch.tensor,
                        offset=(g * TC * P + a * BLK) * EXT * HG + (BLK - 1) * HG,
                        ap=[[(EXT - 1) * HG, BLK], [P * EXT * HG, TC], [1, NEAR * HG]])
                    at = NEAR_AT + a * BLK
                    sp.dma_start(rel[a * BLK:(a + 1) * BLK, g, :, at:at + NEAR, :], rows)\
                        .then_inc(rel_in[g], 16)

            wait(sp, s["zeroed"], 1)
            for g in range(GRP):
                near_terms(0, g)
            with sp.Fori(1, B) as b:
                for g in range(GRP):
                    near_terms(b, g)
            sp.wait_ge(s["s_min"], B * NH)
            load(win[:, :, :, :], "win", "win_in")
            sp.wait_ge(s["h2_ready"], B)
            h_seq = h[:, :, :].rearrange("p (b c) d -> p b c d", c=TC)
            for n in range(NCLS):
                sp.dma_start(hcls[n * B:(n + 1) * B, :], h_seq[n:n + 1, :, 0, :])\
                    .then_inc(s["cls_in"], 16)
            out = io["out"].rearrange("b (c p) d -> b p c d", p=P)
            with sp.Fori(0, B) as b:
                wait_alone(sp, s["y_ready"], b + 1, s["sp_passed"])
                sp.dma_start(out[bass.ds(b, 1), :, :, :].rearrange("b p c d -> p (b c) d"),
                             h[:, bass.ds(b * TC, TC), :]).then_inc(s["stored"], 16)
            sp.wait_ge(s["stored"], 16 * B)
            sp.wait_ge(s["yc_ready"], 1)
            for n in range(NCLS):
                sp.dma_start(io["out"][:, n, :], hcls[n * B:(n + 1) * B, :])\
                    .then_inc(s["stored"], 16)
            sp.wait_ge(s["stored"], 16 * (B + NCLS))

        @block.gpsimd
        def _(pool):
            chain = Chain(pool, s["pool_chain"])
            chain(pool.memset(near[:, :], 0.0))
            pool.sem_inc(s["zeroed"], 1)
            chain(pool.memset(v1[:, :, :, :], 1.0))
            chain(pool.memset(wk[:, :, :, :], 0.0))
            chain(pool.memset(xT[LAST:P, 1, :], 0.0))
            chain(pool.memset(clsT[LAST:P, 1, :, :], 0.0))
            chain(pool.memset(xT[LAST:LAST + 1, 1, :], 1.0))
            chain(pool.memset(clsT[LAST:LAST + 1, 1, :, :], 1.0))
            pool.sem_inc(s["zeroed"], 1)

            tables = [io["word"], io["modal"], io["seg"], io["npi"], io["posi"]]
            pool.wait_ge(s["idx_ok"], 1)
            with pool.Fori(0, B // 2) as i:
                for r in range(2):
                    b = 2 * i + r
                    wait_alone(pool, s["emb_free"], b + 1, s["pool_passed"])
                    pool.tensor_copy(idx_now[:, r, :, :], idx[:, :, bass.ds(b * TC, TC)])\
                        .then_inc(s["idx_staged"], 1)
                    wait_alone(pool, s["idx_staged"], b + 1, s["pool_passed"])
                    for c in range(TC):
                        for j in range(NTAB):
                            pool.indirect_dma_start(
                                out=emb[:, r, c, j, :], out_offset=None, in_=tables[j],
                                in_offset=bass.IndirectOffsetOnAxis(
                                    ap=idx_now[:, r, j, c:c + 1], axis=0))\
                                .then_inc(gathered[r], 16)

            def one_head_queries(b):
                for g in range(GRP):
                    wait_alone(pool, s["qk_ready"], b * GRP + g + 1, s["pool_passed"])
                    for k in range(HG):
                        ins = pool.tensor_scalar(qm[:, g, k, :], qT[:, g, :], hmask[:, k:k + 1],
                                                 None, ALU.mult)
                    ins.then_inc(s["qm_ready"], 1)

            def values(b):
                pool.wait_ge(s["v_ready"], b + 1)
                wait_alone(pool, s["o_psum"], b * GRP, s["pool_passed"])
                pool.tensor_copy(v1[:, :, :, 0:HD],
                                 v_new[:, :, :].rearrange("p c (h d) -> p c h d", d=HD))\
                    .then_inc(s["v1_ready"], 1)

            one_head_queries(0)
            values(0)
            with pool.Fori(1, B) as b:
                one_head_queries(b)
                values(b)

        @block.scalar
        def _(act):
            act.preload_act_table(ACT.Sin)
            with act.Fori(0, B // 2) as i:
                for r in range(2):
                    b = 2 * i + r
                    act.wait_ge(s["angles"], b + 1)
                    act.activation(emb[:, r, :, NTAB:NTAB + 2, D - 1:D], angle[:, :, :, D - 1:D],
                                   ACT.Copy)
                    act.activation(emb[:, r, :, NTAB:NTAB + 2, 0:D - 1],
                                   angle[:, :, :, 0:D - 1], ACT.Sin).then_inc(s["sines"], 1)

            def root(k):
                act.wait_ge(s["root"], k)
                act.activation(st[:, 1, :], st[:, 0, :], ACT.Sqrt).then_inc(s["root_ready"], 1)

            root(1)
            root(2)
            act.preload_act_table(ACT.Exp)

            def slot(b, k, now, before, ahead):
                n = k + 2
                if now if n < NH else ahead:
                    unit = b * NH + n
                    act.wait_ge(s["s_min"], unit + 1)
                    wait(act, s["pT_psum"], unit - 1)
                    for c in range(TC):
                        ins = act.activation(prob[:, n % 2, c, :], ssum[:, n % 2, c, :], ACT.Exp,
                                             bias=smin[:, n % 2, c:c + 1], scale=-1.0)
                    ins.then_inc(s["p_ready"], 1)
                if ahead and k == 1:
                    u = b + 1
                    act.wait_ge(s["xT_psum"], u + 1)
                    act.activation(xT[:, 0, :], psum[:, XB, 0:T], ACT.Copy)
                    act.activation(xT[0:LAST, 1, :], psum[0:LAST, XB, T:2 * T], ACT.Copy)\
                        .then_inc(s["xT_ready"], 1)
                if before and k == 0:
                    outputs(b - 1, GRP - 1)
                if now and k in (4, 8):
                    outputs(b, k // 4 - 1)
                if ahead and k in (3, 7, 11):
                    u, g = b + 1, k // 4
                    act.wait_ge(s["r_psum"], u * GRP + g + 1)
                    wait(act, r_stored[g], u * 16)
                    act.activation(r_sb[:, g, :, :].rearrange("p c e -> p (c e)"),
                                   psum[:, RB, 0:TC * EXT * HG], ACT.Copy)\
                        .then_inc(s["r_ready"], 1)
                if ahead and k == 4:
                    u = b + 1
                    act.wait_ge(s["v_psum"], u + 1)
                    wait(act, s["v1_ready"], u)
                    act.activation(v_new[:, :, :].rearrange("p c d -> p (c d)"),
                                   psum[:, XB, 0:TC * D], ACT.Copy).then_inc(s["v_ready"], 1)

            def outputs(b, g):
                act.wait_ge(s["o_psum"], b * GRP + g + 1)
                wait(act, s["oT_ready"], b * GRP + g)
                act.activation(o_sb[:, :], psum[:, OB, 0:T], ACT.Copy).then_inc(s["o_ready"], 1)

            phase_b(act, slot)

            root(3)
            act.preload_act_table(ACT.Gelu)

            def transposed(b):
                act.wait_ge(s["xT_psum"], B + b + 1)
                act.activation(xT[:, 0, :], psum[:, 6, 0:T], ACT.Copy)
                act.activation(xT[0:LAST, 1, :], psum[0:LAST, 6, T:2 * T], ACT.Copy)\
                    .then_inc(s["xT_ready"], 1)

            def gelus(b, r):
                for j in range(3):
                    act.wait_ge(s["f_psum"], b * 3 + j + 1)
                    if j == 0:
                        wait(act, s["y_psum"], b - 1)
                    act.activation(gT[:, r, 2 * j:2 * j + 2, :].rearrange("p n t -> p (n t)"),
                                   psum[:, 3 * r + j, :], ACT.Gelu).then_inc(s["f_ready"], 1)

            phase_c(transposed, gelus, act)

            for j in range(3):
                act.wait_ge(s["hid_psum"], j + 1)
                act.activation(hidT[:, 2 * j:2 * j + 2, :, :, :]
                               .rearrange("p t r n b -> p (t r n b)"),
                               psum[:, j, 0:4 * NB], ACT.Gelu).then_inc(s["hid_ready"], 1)
            act.wait_ge(s["norms_psum"], 1)
            act.activation(nrm[:, 0, :], psum[:, 3, 0:NB + 2 * NCLS], ACT.Sqrt)\
                .then_inc(s["root_ready"], 1)
            act.wait_ge(s["gates"], 1)
            act.activation(lg[:, :, :, :].rearrange("p r n b -> p (r n b)"),
                           lg[:, :, :, :].rearrange("p r n b -> p (r n b)"), ACT.Exp)\
                .then_inc(s["exps"], 1)

        @block.vector
        def _(dve):
            chain = Chain(dve, s["dve_chain"])

            dve.wait_ge(s["ids_in"], 16)
            chain(dve.tensor_copy(idf[:, 0, :, :], ids[:, :, :]))
            for j, rows in enumerate(TABLE_ROWS):
                last = dve.tensor_scalar(idf[:, 1, j, :], idf[:, 0, j, :], 0.0, float(rows),
                                         ALU.is_lt, ALU.mult)
            chain(last)
            chain(dve.tensor_tensor(idf[:, 0, :, :], idf[:, 0, :, :], idf[:, 1, :, :], ALU.add))
            for j, rows in enumerate(TABLE_ROWS):
                last = dve.tensor_scalar(idf[:, 1, j, :], idf[:, 0, j, :], 0.0, float(rows - 1),
                                         ALU.max, ALU.min)
            chain(last)
            dve.tensor_copy(idx[:, :, :], idf[:, 1, :, :]).then_inc(s["idx_ok"], 1)
            dve.sem_inc(s["emb_free"], 2)

            dve.wait_ge(s["time_in"], 48)
            body = chain
            with dve.Fori(0, B // 2) as i:
                chain.loop(i, 2 * 6)
                for r in range(2):
                    b = 2 * i + r
                    if r:
                        dve.wait_ge(s["sines"], b)
                    for c in range(TC):
                        for w in range(2):
                            last = dve.scalar_tensor_tensor(
                                angle[:, c, w, :], t2v_w[:, w, :],
                                tau[:, w, bass.ds(b * TC + c, 1)], t2v_b[:, w, :],
                                ALU.mult, ALU.add)
                    chain(last)
                    a, n = angle[:, :, :, 0:D - 1], turns[:, :, :, 0:D - 1]
                    a = a.rearrange("p c w d -> p (c w) d")
                    n = n.rearrange("p c w d -> p (c w) d")
                    chain(dve.tensor_scalar(n, a, 1.0 / TURN, ROUND, ALU.mult, ALU.add))
                    chain(dve.tensor_scalar(n, n, ROUND, None, ALU.subtract))
                    chain(dve.scalar_tensor_tensor(a, n, -TURN_HI, a, ALU.mult, ALU.add))
                    chain(dve.scalar_tensor_tensor(a, n, -TURN_LO, a, ALU.mult, ALU.add))
                    dve.tensor_scalar(a, a, HALF_TURN, -HALF_TURN, ALU.min, ALU.max)\
                        .then_inc(s["angles"], 1)
                    dve.wait_ge(s["sines"], b + 1)
                    dve.wait_ge(gathered[r], (i + 1) * 16 * TC * NTAB)
                    rows = h[:, bass.ds(b * TC, TC), :]
                    chain(dve.tensor_reduce(rows, emb[:, r, :, :, :]
                                            .rearrange("p c j d -> p c d j"), AX.X, ALU.add))
                    for c in range(TC):
                        last = dve.bn_stats(bn6[:, bass.ds(b * TC + c, 1), :],
                                            h[:, bass.ds(b * TC + c, 1), :])
                    last.then_inc(s["emb_free"], 1)
            chain.done(B // 2)
            dve.wait_ge(s["emb_free"], B + 2)

            def deviations(eps, k):
                m0, m1 = bn6[:, :, 1], bn6[:, :, 4]
                v0, v1_ = bn6[:, :, 2], bn6[:, :, 5]
                dve.tensor_tensor(st[:, 2, :], m0, m1, ALU.subtract)
                dve.tensor_tensor(st[:, 3, :], v0, v1_, ALU.add)
                chain(dve.tensor_tensor(mean[:, :], m0, m1, ALU.add))
                chain(dve.tensor_tensor(st[:, 2, :], st[:, 2, :], st[:, 2, :], ALU.mult))
                chain(dve.tensor_scalar(st[:, 3, :], st[:, 3, :], 1.0 / D, eps,
                                        ALU.mult, ALU.add))
                dve.tensor_scalar(mean[:, :], mean[:, :], 0.5, None, ALU.mult)
                chain(dve.scalar_tensor_tensor(st[:, 0, :], st[:, 2, :], 0.25, st[:, 3, :],
                                               ALU.mult, ALU.add))
                dve.sem_inc(s["root"], 1)
                dve.wait_ge(s["root_ready"], k)
                chain(dve.reciprocal(st[:, 2, :], st[:, 1, :]))
                chain(dve.tensor_tensor(st[:, 3, :], st[:, 2, :], st[:, 2, :], ALU.mult))
                chain(dve.tensor_tensor(st[:, 3, :], st[:, 3, :], st[:, 0, :], ALU.mult))
                chain(dve.tensor_scalar(st[:, 3, :], st[:, 3, :], -0.5, 1.5, ALU.mult, ALU.add))
                chain(dve.tensor_tensor(rstd[:, :], st[:, 3, :], st[:, 2, :], ALU.mult))

            def normalise(dst, b):
                for c in range(TC):
                    tile = bass.ds(b * TC + c, 1)
                    last = dve.tensor_scalar(dst[c], h[:, tile, :], mean[:, tile],
                                             rstd[:, tile], ALU.subtract, ALU.mult)
                return last

            deviations(EPS_EMB, 1)
            dve.wait_ge(s["norm_in"], 32)
            with dve.Fori(0, B) as b:
                chain.loop(b, 3)
                rows = h[:, bass.ds(b * TC, TC), :]
                chain(normalise([h[:, bass.ds(b * TC + c, 1), :] for c in range(TC)], b))
                chain(dve.tensor_tensor(rows, rows, gamma[:, None, :].to_broadcast([P, TC, D]),
                                        ALU.mult))
                chain(dve.tensor_tensor(rows, rows, beta[:, None, :].to_broadcast([P, TC, D]),
                                        ALU.add))
                for c in range(TC):
                    last = dve.bn_stats(bn6[:, bass.ds(b * TC + c, 1), :],
                                        h[:, bass.ds(b * TC + c, 1), :])
                last.then_inc(s["h_ready"], 1)
            chain.done(B)
            dve.wait_ge(s["h_ready"], B)
            deviations(EPS_LN, 2)

            dve.wait_ge(s["attn_in"], 16 * 13)
            chain(dve.tensor_tensor(span[:, :], rel_hd[:, :, NREL - 1], rel_hd[:, :, 0],
                                    ALU.subtract))
            for t in range(2):
                last = dve.tensor_scalar(g_sel[:, t, :, HD:ROW],
                                         g_blk[:, t, :, None].to_broadcast([P, NH, ROW - HD]),
                                         span[:, t:t + 1], None, ALU.mult)
            last.then_inc(s["g_ready"], 1)
            dve.wait_ge(s["zeroed"], 2)
            dve.tensor_copy(wk[:, :, :, 0:HD],
                            wk_d[:, :, :].rearrange("p t (h d) -> p t h d", d=HD))\
                .then_inc(s["wk_ready"], 1)
            dve.tensor_copy(relx[:, 0:REL - 1], rel32[:, 0:1].to_broadcast([P, REL - 1]))
            dve.tensor_copy(relx[:, REL - 1:REL - 1 + NREL], rel32[:, :])
            chain(dve.tensor_copy(relx[:, REL - 1 + NREL:EXT],
                                  rel32[:, NREL - 1:NREL].to_broadcast([P, EXT - REL + 1 - NREL])))
            chain(dve.tensor_scalar(relx[:, :], relx[:, :], rel32[:, 0:1], None, ALU.subtract))
            for k in range(HG):
                last = dve.tensor_scalar(rel_bd[:, :, k], relx[:, :], hmask[:, k:k + 1], None,
                                         ALU.mult)
            last.then_inc(s["relbd_ready"], 1)
            dve.wait_ge(s["wq_psum"], 1)
            dve.memset(wq[:, 1, :], 0.0)
            chain(dve.tensor_copy(wq[:, 0, :], psum[:, S0, 0:NH * ROW]))
            dve.tensor_copy(wq[0:LAST + 1, 1, :], psum[0:LAST + 1, T0, 0:NH * ROW])\
                .then_inc(s["wq_ready"], 1)

            def slot(b, k, now, before, ahead):
                n = k + 2
                if now if n < NH else ahead:
                    unit, g, hg = b * NH + n, (n % NH) // HG, n % HG
                    if hg == 0:
                        dve.wait_ge(rel_in[g], (b + n // NH + 1) * N_RD)
                    wait(dve, s["p_ready"], unit - 1)
                    wait_alone(dve, s["s_psum"], unit + 1, s["dve_passed"])
                    for c in range(TC):
                        last = dve.tensor_tensor_reduce(
                            ssum[:, n % 2, c, :], psum[:, S0 + n % 2, c * T:(c + 1) * T],
                            rel[:, g, c, REL_AT[c]:REL_AT[c] + T, hg], 1.0, BIG,
                            ALU.add, ALU.min, smin[:, n % 2, c:c + 1])
                    last.then_inc(s["s_min"], 1)
                if now:
                    unit = b * NH + k
                    dve.wait_ge(s["pT_psum"], unit + 1)
                    if k % HG == 0:
                        wait(dve, s["o_psum"], (b - 1) * GRP + k // HG + 1)
                    dve.tensor_copy(pT[:, k // HG, k % HG, :, :]
                                    .rearrange("p s t -> p (s t)"), psum[:, T0 + k % 2, :])\
                        .then_inc(s["pT_ready"], 1)
                if before and k == 1:
                    outputs(b - 1, GRP - 1)
                if now and k in (5, 9):
                    outputs(b, k // 4 - 1)
                if ahead and k == 0:
                    wait(dve, s["xT_psum"], b + 1)
                    normalise([xn[:, c, :] for c in range(TC)], b + 1)\
                        .then_inc(s["xn_ready"], 1)
                if before and k == 2:
                    u = b - 1
                    dve.wait_ge(s["out_psum"], u + 1)
                    rows = h[:, bass.ds(u * TC, TC), :]
                    chain(dve.tensor_tensor(rows, psum[:, RB, 0:TC * D]
                                            .rearrange("p (c d) -> p c d", c=TC), rows, ALU.add))
                    for c in range(TC):
                        last = dve.bn_stats(bn6[:, bass.ds(u * TC + c, 1), :],
                                            h[:, bass.ds(u * TC + c, 1), :])
                    last.then_inc(s["h2_ready"], 1)
                if ahead and k in (2, 6, 10):
                    u, g = b + 1, k // 4
                    dve.wait_ge(s["qk_psum"], u * GRP + g + 1)
                    dve.tensor_tensor(qT[:, g, :], psum[:, QB, 0:T], q_mask[:, :], ALU.mult)
                    dve.tensor_tensor(kT[:, g, :], psum[:, QB, T:2 * T], k_ind[:, :], ALU.add)\
                        .then_inc(s["qk_ready"], 1)

            def outputs(b, g):
                dve.wait_ge(s["sum_psum"], b * GRP + g + 1)
                chain(dve.reciprocal(o_inv[:, :], psum[:, OB, T:2 * T]))
                wait(dve, s["out_psum"], b)
                dve.tensor_tensor(oT[:, g, :], o_sb[:, :], o_inv[:, :], ALU.mult)\
                    .then_inc(s["oT_ready"], 1)

            def loops(i):
                if i is None:
                    chain.done(B - 2)
                else:
                    chain.loop(i, 3 + 1)

            phase_b(dve, slot, loops)
            dve.wait_ge(s["h2_ready"], B)
            deviations(EPS_LN, 3)

            dve.wait_ge(s["ffn_in"], 48)

            def prepare(b):
                wait(dve, s["xT_psum"], B + b)
                normalise([xn[:, c, :] for c in range(TC)], b).then_inc(s["xn_ready"], 1)
                dve.wait_ge(s["xT_ready"], B + b + 1)
                dve.tensor_copy(clsT[:, 0, :, bass.ds(b, 1)], xT[:, 0, 0:NCLS, None])
                dve.tensor_copy(clsT[0:LAST, 1, :, bass.ds(b, 1)], xT[0:LAST, 1, 0:NCLS, None])\
                    .then_inc(s["sq_ready"], 1)

            def results(b, r):
                rows = h[:, bass.ds(b * TC, TC), :]
                dve.wait_ge(s["cls_in"], 16 * NCLS)
                dve.wait_ge(s["y_psum"], b + 1)
                chain(dve.tensor_tensor(rows, psum[:, 7, 0:TC * D]
                                        .rearrange("p (c d) -> p c d", c=TC), rows, ALU.add))
                dve.tensor_tensor(rows, rows, b2[:, None, :].to_broadcast([P, TC, D]), ALU.add)\
                    .then_inc(s["y_ready"], 1)

            prepare(0)
            with dve.Fori(0, B // 2 - 1) as i:
                chain.loop(i, 2)
                for r in range(2):
                    prepare(2 * i + r + 1)
                    results(2 * i + r, r)
            chain.done(B // 2 - 1)
            prepare(B - 1)
            results(B - 2, 0)
            results(B - 1, 1)

            dve.wait_ge(s["gate_in"], 64)
            dve.wait_ge(s["sq_ready"], B)
            for t, n in ((0, P), (1, LAST)):
                c = clsT[0:n, t, :, :].rearrange("p n b -> p (n b)")
                g = gate[0:n, t, :, :].rearrange("p n r -> p (n r)")
                dve.tensor_tensor(sq[0:n, t, 0:NB], c, c, ALU.mult)
                dve.tensor_tensor(sq[0:n, t, NB:], g, g, ALU.mult)
                for r in range(2):
                    last = dve.tensor_tensor(
                        prod[0:n, t, r, :, :], clsT[0:n, t, :, :],
                        gate[0:n, t, :, r:r + 1].to_broadcast([n, NCLS, B]), ALU.mult)
            last.then_inc(s["sq_ready"], 1)
            dve.wait_ge(s["root_ready"], 4)
            size = psum[:, 3, 0:NB + 2 * NCLS]
            chain(dve.tensor_scalar(nrm[:, 1, :], nrm[:, 0, :], EPS_NORM, None, ALU.max))
            chain(dve.reciprocal(nrm[:, 1, :], nrm[:, 1, :]))
            chain(dve.tensor_tensor(nrm[:, 1, :], size, nrm[:, 1, :], ALU.mult))
            chain(dve.tensor_tensor(nrm[:, 1, :], nrm[:, 0, :], nrm[:, 1, :], ALU.add))
            chain(dve.tensor_scalar(nrm[:, 1, :], nrm[:, 1, :], 0.5, EPS_NORM,
                                    ALU.mult, ALU.max))
            chain(dve.reciprocal(nrm[:, 2, :], nrm[:, 1, :]))
            by_x = nrm[:, 2, 0:NB].rearrange("p (n b) -> p n b", b=B)
            by_g = nrm[:, 2, NB:].rearrange("p (n r) -> p n r", r=2)
            dots = psum[:, 3, P:P + 2 * NB].rearrange("p (r n b) -> p r n b", r=2, n=NCLS)
            for r in range(2):
                last = dve.tensor_tensor(lg[:, r, :, :], dots[:, r, :, :], by_x, ALU.mult)
            chain(last)
            for r in range(2):
                last = dve.tensor_tensor(lg[:, r, :, :], lg[:, r, :, :],
                                         by_g[:, :, r:r + 1].to_broadcast([P, NCLS, B]), ALU.mult)
            chain(last)
            for r in range(2):
                last = dve.tensor_tensor(lg[:, r, :, :], lg[:, r, :, :],
                                         bal[:, r, :, None].to_broadcast([P, NCLS, B]), ALU.add)
            chain(last)
            chain(dve.tensor_tensor(mx[:, :, :], lg[:, 0, :, :], lg[:, 1, :, :], ALU.max))
            for r in range(2):
                last = dve.tensor_tensor(lg[:, r, :, :], lg[:, r, :, :], mx[:, :, :],
                                         ALU.subtract)
            last.then_inc(s["gates"], 1)
            dve.wait_ge(s["exps"], 1)
            chain(dve.tensor_tensor(den[:, :, :], lg[:, 0, :, :], lg[:, 1, :, :], ALU.add))
            chain(dve.reciprocal(den[:, :, :], den[:, :, :]))
            for r in range(2):
                last = dve.tensor_tensor(lg[:, r, :, :], lg[:, r, :, :], den[:, :, :], ALU.mult)
            chain(last)
            chain(dve.tensor_tensor(first[:, :, :], lg[:, 0, :, :], lg[:, 1, :, :], ALU.is_ge))
            dve.tensor_tensor(lg[:, 0, :, :], lg[:, 0, :, :], first[:, :, :], ALU.mult)
            chain(dve.tensor_scalar(mx[:, :, :], first[:, :, :], -1.0, 1.0, ALU.mult, ALU.add))
            chain(dve.tensor_tensor(lg[:, 1, :, :], lg[:, 1, :, :], mx[:, :, :], ALU.mult))
            dve.wait_ge(s["cand_psum"], 1)
            for t, n in ((0, P), (1, LAST)):
                for r in range(2):
                    last = dve.tensor_tensor(
                        cand[0:n, t, r, :, :],
                        psum[0:n, 4 + t, r * NB:(r + 1) * NB].rearrange("p (n b) -> p n b", b=B),
                        bout[0:n, t, r, :, None].to_broadcast([n, NCLS, B]), ALU.add)
            chain(last)
            for t, n in ((0, P), (1, LAST)):
                for r in range(2):
                    last = dve.tensor_tensor(cand[0:n, t, r, :, :], cand[0:n, t, r, :, :],
                                             lg[0:n, r, :, :], ALU.mult)
            chain(last)
            for t, n in ((0, P), (1, LAST)):
                last = dve.tensor_tensor(
                    ycT[0:n, t, :].rearrange("p (n b) -> p n b", b=B),
                    cand[0:n, t, 0, :, :], cand[0:n, t, 1, :, :], ALU.add)
            last.then_inc(s["cand_ready"], 1)
            dve.wait_ge(s["yc_psum"], 1)
            dve.tensor_tensor(hcls[:, :], psum[0:NB, 6, 0:D], hcls[:, :], ALU.add)\
                .then_inc(s["yc_ready"], 1)

        @block.tensor
        def _(pe):
            mm = nc.tensor.matmul

            pe.wait_ge(s["attn_in"], 16 * 13)
            pe.wait_ge(s["g_ready"], 1)
            for bank, lo, hi in ((S0, 0, P), (T0, P, D + 1)):
                for t in range(2):
                    last = mm(psum[0:hi - lo, bank, 0:NH * ROW], wq_n[:, t, lo:hi],
                              g_sel[:, t, :, :].rearrange("p h r -> p (h r)"),
                              start=t == 0, stop=t == 1)
            last.then_inc(s["wq_psum"], 1)
            pe.wait_ge(s["wq_ready"], 1)
            pe.wait_ge(s["wk_ready"], 1)
            pe.wait_ge(s["relbd_ready"], 1)
            pe.wait_ge(s["zeroed"], 2)

            def slot(b, k, now, before, ahead):
                n = k + 2
                if now if n < NH else ahead:
                    unit, g, hg = b * NH + n, (n % NH) // HG, n % HG
                    if hg == 0:
                        pe.wait_ge(s["qm_ready"], (b + n // NH) * GRP + g + 1)
                    wait(pe, s["s_min"], unit - 1)
                    for c in range(TC):
                        last = mm(psum[:, S0 + n % 2, c * T:(c + 1) * T],
                                  qm[:, g, hg, c * P:(c + 1) * P], kT[:, g, :],
                                  start=True, stop=True)
                    last.then_inc(s["s_psum"], 1)
                if now:
                    unit = b * NH + k
                    pe.wait_ge(s["p_ready"], unit + 1)
                    wait(pe, s["pT_ready"], unit - 1)
                    for t in range(2):
                        for c in range(TC):
                            last = nc.tensor.transpose(
                                psum[:, T0 + k % 2, t * T + c * P:t * T + (c + 1) * P],
                                prob[:, k % 2, c, t * P:(t + 1) * P], ident[:, :])
                    last.then_inc(s["pT_psum"], 1)
                if before and k == 0:
                    outputs(b - 1, GRP - 1)
                if before and k == 1:
                    row_sums(b - 1, GRP - 1)
                if now and k in (4, 8):
                    outputs(b, k // 4 - 1)
                if now and k in (5, 9):
                    row_sums(b, k // 4 - 1)
                if ahead and k == 1:
                    u = b + 1
                    pe.wait_ge(s["xn_ready"], u + 1)
                    wait(pe, s["v_ready"], u)
                    for c in range(TC):
                        nc.tensor.transpose(psum[:, XB, c * P:(c + 1) * P], xn[:, c, 0:P],
                                            ident[:, :])
                        last = nc.tensor.transpose(psum[0:LAST, XB, T + c * P:T + (c + 1) * P],
                                                   xn[:, c, P:D], ident[:, :])
                    last.then_inc(s["xT_psum"], 1)
                if ahead and k in (2, 6, 10):
                    u, g = b + 1, k // 4
                    if g == 0:
                        pe.wait_ge(s["xT_ready"], u + 1)
                    wait(pe, s["qk_ready"], u * GRP + g)
                    for q, w in ((0, wq), (1, wk[:, :, :, :].rearrange("p t h r -> p t (h r)"))):
                        for t in range(2):
                            last = mm(psum[:, QB, q * T:(q + 1) * T],
                                      w[:, t, g * P:(g + 1) * P], xT[:, t, :],
                                      start=t == 0, stop=t == 1)
                    last.then_inc(s["qk_psum"], 1)
                if before and k == 2:
                    u = b - 1
                    pe.wait_ge(s["oT_ready"], (u + 1) * GRP)
                    if isinstance(b, int):
                        wait(pe, s["r_ready"], min(b + 1, B) * GRP)
                    else:
                        pe.wait_ge(s["r_ready"], (b + 1) * GRP)
                    for c in range(TC):
                        for g in range(GRP):
                            last = mm(psum[:, RB, c * D:(c + 1) * D],
                                      oT[:, g, c * P:(c + 1) * P], wo[:, g, :],
                                      start=g == 0, stop=g == GRP - 1)
                    last.then_inc(s["out_psum"], 1)
                if ahead and k in (3, 7, 11):
                    u, g = b + 1, k // 4
                    pe.wait_ge(s["qk_ready"], u * GRP + g + 1)
                    wait(pe, s["r_ready"], u * GRP + g)
                    if before and g == 0:
                        pe.wait_ge(s["h2_ready"], b)
                    for c in range(TC):
                        last = mm(psum[:, RB, c * EXT * HG:(c + 1) * EXT * HG],
                                  qT[:, g, c * P:(c + 1) * P],
                                  rel_bd[:, :, :].rearrange("p e h -> p (e h)"),
                                  start=True, stop=True)
                    last.then_inc(s["r_psum"], 1)
                if ahead and k == 4:
                    u = b + 1
                    for c in range(TC):
                        for t in range(2):
                            last = mm(psum[:, XB, c * D:(c + 1) * D], xT[:, t, c * P:(c + 1) * P],
                                      wv[:, t, :], start=t == 0, stop=t == 1)
                    last.then_inc(s["v_psum"], 1)

            def outputs(b, g):
                pe.wait_ge(s["pT_ready"], b * NH + HG * (g + 1))
                if g == 0:
                    pe.wait_ge(s["v1_ready"], b + 1)
                wait(pe, s["oT_ready"], b * GRP + g)
                for t in range(2):
                    for k in range(HG):
                        last = mm(psum[k * ROW:(k + 1) * ROW, OB, 0:T],
                                  v1[:, t, HG * g + k, :], pT[:, g, k, t, :],
                                  start=t == 0, stop=t == 1, tile_position=(0, k * ROW))
                last.then_inc(s["o_psum"], 1)

            def row_sums(b, g):
                pe.wait_ge(s["o_ready"], b * GRP + g + 1)
                mm(psum[:, OB, T:2 * T], sel_sum[:, :], o_sb[:, :], start=True, stop=True)\
                    .then_inc(s["sum_psum"], 1)

            phase_b(pe, slot)

            pe.wait_ge(s["ffn_in"], 48)

            def first(b, r):
                pe.wait_ge(s["xn_ready"], B + b + 1)
                wait(pe, s["sq_ready"], b)
                for c in range(TC):
                    nc.tensor.transpose(psum[:, 6, c * P:(c + 1) * P], xn[:, c, 0:P], ident[:, :])
                    last = nc.tensor.transpose(psum[0:LAST, 6, T + c * P:T + (c + 1) * P],
                                               xn[:, c, P:D], ident[:, :])
                last.then_inc(s["xT_psum"], 1)
                pe.wait_ge(s["xT_ready"], B + b + 1)
                for j in range(3):
                    wait(pe, s["f_ready"], (b - 2) * 3 + j + 1)
                    for k in range(2):
                        for t in range(2):
                            last = mm(psum[:, 3 * r + j, k * T:(k + 1) * T],
                                      w1[:, t, (2 * j + k) * P:(2 * j + k + 1) * P], xT[:, t, :],
                                      start=t == 0, stop=t == 1)
                    last.then_inc(s["f_psum"], 1)

            def second(b, r):
                pe.wait_ge(s["f_ready"], b * 3 + 3)
                wait(pe, s["y_ready"], b)
                for c in range(TC):
                    for n in range(HT):
                        last = mm(psum[:, 7, c * D:(c + 1) * D], gT[:, r, n, c * P:(c + 1) * P],
                                  w2[:, n, :], start=n == 0, stop=n == HT - 1)
                last.then_inc(s["y_psum"], 1)

            first(0, 0)
            first(1, 1)
            second(0, 0)
            first(2, 0)
            second(1, 1)
            first(3, 1)
            second(2, 0)
            with pe.Fori(2, B // 2) as i:
                first(2 * i, 0)
                second(2 * i - 1, 1)
                first(2 * i + 1, 1)
                second(2 * i, 0)
            second(B - 1, 1)

            pe.wait_ge(s["win_in"], 16)
            pe.wait_ge(s["wout_in"], 16)
            pe.wait_ge(s["sq_ready"], B)
            pe.wait_ge(s["f_ready"], 3 * B)

            def of_atom(columns, route, a):
                c = columns[:, route, :, :]
                if a < 3:
                    return c[:, 2 * a:2 * a + 2, :]
                return c.rearrange("p (k q) b -> p k q b", q=2)[:, :, a - 3, :]

            for n in range(HT):
                hid = psum[:, n // 2, (n % 2) * 2 * NB:(n % 2 + 1) * 2 * NB]\
                    .rearrange("p (r n b) -> p r n b", r=2, n=NCLS)
                for a in range(NATOM):
                    for t in range(2):
                        last = mm(of_atom(hid, a // 3, a), win[:, a, t, n * P:(n + 1) * P],
                                  of_atom(clsT[:, t:t + 1, :, :], 0, a),
                                  start=t == 0, stop=t == 1)
                if n % 2:
                    last.then_inc(s["hid_psum"], 1)
            pe.wait_ge(s["sq_ready"], B + 1)
            for lo, src in ((0, sq[:, :, :]),
                            (P, prod[:, :, :, :, :].rearrange("p t r n b -> p t (r n b)"))):
                for t, n in ((0, P), (1, LAST)):
                    last = mm(psum[:, 3, lo:lo + src.shape[2]], ones[0:n, :], src[0:n, t, :],
                              start=t == 0, stop=t == 1)
            last.then_inc(s["norms_psum"], 1)
            pe.wait_ge(s["hid_ready"], 3)
            for t, lo, hi in ((0, 0, P), (1, P, D)):
                out = psum[0:hi - lo, 4 + t, 0:2 * NB].rearrange("p (r n b) -> p r n b", r=2, n=NCLS)
                for a in range(NATOM):
                    route = 1 - a // 3
                    for n in range(HT):
                        last = mm(of_atom(out, route, a), wout[:, a, n, lo:hi],
                                  of_atom(hidT[:, n, :, :, :], route, a),
                                  start=n == 0, stop=n == HT - 1)
            last.then_inc(s["cand_psum"], 1)
            pe.wait_ge(s["cand_ready"], 1)
            nc.tensor.transpose(psum[0:NB, 6, 0:P], ycT[:, 0, :], ident[:, :])
            nc.tensor.transpose(psum[0:NB, 6, P:D], ycT[0:LAST, 1, :], ident[0:LAST, 0:LAST])\
                .then_inc(s["yc_psum"], 1)


INPUTS = ["x", "itok_BS_0_15", "itok_BS_0_3", "itok_BS_0_9999", "itok_BS_0_2047"]


def kernel(**inputs):
    import numpy as np
    import concourse.bacc as bacc
    from concourse.bass_utils import run_bass_kernel_spmd as run

    a = {k: np.asarray(v) for k, v in inputs.items()}
    t = {k[len("L0_tok_"):]: v for k, v in a.items() if k.startswith("L0_tok_")}
    at = {k[len("L0_attn_"):]: v for k, v in a.items() if k.startswith("L0_attn_")}
    f = {k[len("L0_ffn_"):]: v for k, v in a.items() if k.startswith("L0_ffn_")}

    def by_tile(v):
        return v.reshape(-1, P).T

    def rows(v):
        return np.broadcast_to(v, (P,) + v.shape)

    def halves(*parts):
        v = np.concatenate(parts, 0)
        full = np.zeros((2 * P,) + v.shape[1:], v.dtype)
        full[:v.shape[0]] = v
        return full.reshape((2, P) + v.shape[1:]).swapaxes(0, 1)

    def spread(v):
        full = np.zeros((GRP, HG, ROW) + v.shape[1:], v.dtype)
        full[:, :, :HD] = v.reshape((GRP, HG, HD) + v.shape[1:])
        return full.reshape((GRP, P) + v.shape[1:]).swapaxes(0, 1)

    part, tok = np.arange(P), np.arange(T)
    qkv_w, qkv_b = at["qkv_w"], at["qkv_b"]
    wo = spread(at["out_w"].T).copy()
    wo[HD, 0] = at["out_b"]
    rel_T = at["rel_pos_emb"].T
    place = (part % ROW - HD)[:, None]
    q_mask = ((place < 0) | (place >= tok // BLK + 2)).astype(np.float32)
    k_ind = (place == tok // BLK).astype(np.float32)
    heads = (part[:, None] // ROW == np.arange(HG)).astype(np.float32)
    hd = np.arange(2 * P)
    same = (hd[:, None] // HD == np.arange(NH)) * np.float32(SCALE)
    g_sel = np.zeros((2 * P, NH, ROW), np.float32)
    g_sel[:, :, :HD] = same[:, :, None] * (hd[:, None, None] % HD == np.arange(HD))
    sel_sum = (part[:, None] == part // ROW * ROW + HD).astype(np.float32)
    left, right = [0, 0, 1, 1, 2, 2], [3, 4, 3, 4, 3, 4]

    arrays = {
        "ids": np.stack([by_tile(a[n]) for n in INPUTS], 1),
        "tau": np.stack([by_tile(a["fside_BS_age_tau"]), by_tile(a["fside_BS_delays_tau"])], 1),
        "t2v_w": rows(np.stack([np.concatenate([t["age_w"][0], t["age_w0"][0]]),
                                np.concatenate([t["delay_w"][0], t["delay_w0"][0]])])),
        "t2v_b": rows(np.stack([np.concatenate([t["age_b"], t["age_b0"]]),
                                np.concatenate([t["delay_b"], t["delay_b0"]])])),
        "gamma": rows(t["ln_gamma"]), "beta": rows(t["ln_beta"]),
        "word": t["word_table"], "modal": t["modalities_table"], "seg": t["seg_table"],
        "npi": t["npi_table"], "posi": t["posi_table"],
        "ident": np.eye(P, dtype=np.float32),
        "g_sel": halves(g_sel), "g_blk": halves(same.astype(np.float32)),
        "rel_hd": halves(np.tile(rel_T, (NH, 1))),
        "wq_n": halves(np.concatenate([qkv_w[0:D], qkv_b[0:D, None]], 1)),
        "wk": halves(qkv_w[D:2 * D].T, qkv_b[None, D:2 * D]),
        "wv": halves(qkv_w[2 * D:].T, qkv_b[None, 2 * D:]),
        "wo": wo,
        "rel32": spread(np.tile(rel_T, (NH, 1)))[:, 0],
        "hmask": heads, "q_mask": q_mask, "k_ind": k_ind, "sel_sum": sel_sum,
        "w1": halves(f["fc1_w"].T, f["fc1_b"][None]),
        "w2": f["fc2_w"].T.reshape(HT, P, D).swapaxes(0, 1), "b2": rows(f["fc2_b"]),
        "win": np.stack([halves(w.T, b[None]) for w, b in zip(f["atom_in_w"], f["atom_in_b"])], 1),
        "wout": f["atom_out_w"].transpose(0, 2, 1).reshape(NATOM, HT, P, D).transpose(2, 0, 1, 3),
        "bout": halves(np.stack([f["atom_out_b"][right].T, f["atom_out_b"][left].T], 1)),
        "gate": halves(f["gate_pair"].transpose(2, 0, 1)),
        "bal": rows(f["balance_bias"].T),
        "ones": np.ones((P, P), np.float32),
    }
    arrays = {k: np.ascontiguousarray(v) for k, v in arrays.items()}
    nc = bacc.Bacc("TRN2", target_bir_lowering=False, num_devices=1)
    io = {k: nc.dram_tensor(f"in_{k}", v.shape, mybir.dt.from_np(v.dtype),
                            kind="ExternalInput").ap() for k, v in arrays.items()}
    io["out"] = nc.dram_tensor("out_y", (B, T, D), F32, kind="ExternalOutput").ap()
    tower(nc, io)
    r = run(nc, [{f"in_{k}": v for k, v in arrays.items()}], core_ids=[0])
    return r.results[0]["out_y"]
```

```python
import concourse.bass as bass
from concourse import mybir
from contextlib import ExitStack

F32 = mybir.dt.float32
F32R = mybir.dt.float32r
I32 = mybir.dt.int32
ALU = mybir.AluOpType
ACT = mybir.ActivationFunctionType
AX = mybir.AxisListType

B, T, D = 16, 256, 192
P = 128
TC = T // P
TILES = B * TC
NH, HD = 12, 16
HG = 4
GRP = NH // HG
ROW = P // HG
REL = 16
NREL = 2 * REL + 1
BLK = 16
NEAR = 3 * BLK
EXT = NEAR + BLK - 1
BPT = P // BLK
KEYS = T + P + 2 * BLK
REL_AT = [BLK + P, BLK]
SHARED = 2 * 2 * NH * T
NEAR_AT = P
HID = 768
HT = HID // P
TABLE_ROWS = [8000, 2500, 512, 16, 4]
NTAB = len(TABLE_ROWS)
AHEAD = 4
NGATHER = 3
NCLS, NATOM = 6, 5
SCALE = -HD ** -0.5
EPS_EMB, EPS_LN, EPS_NORM = 1e-12, 1e-5, 1e-12
TURN = 6.283185307179586
TURN_HI = 6.28125
TURN_LO = TURN - TURN_HI
ROUND = 12582912.0
HALF_TURN = 3.1415925
BIG = 3.0e38
STACK = 3 * ROW
MASK = -(1 << 12)
DVE_COPIES = 3
LAST = D - P


class Chain:

    def __init__(self, eng, sem):
        self.eng, self.sem, self.n, self.past = eng, sem, 0, 0

    def __call__(self, instruction):
        instruction.then_inc(self.sem, 1)
        self.n += 1
        self.eng.wait_ge(self.sem, self.past + self.n)

    def loop(self, i, steps):
        self.n0, self.steps, self.past = self.n, steps, i * steps

    def done(self, iterations):
        assert self.n - self.n0 == self.steps, (self.n - self.n0, self.steps)
        self.n, self.past = self.n0 + iterations * self.steps, 0


def wait(eng, sem, value):
    if not isinstance(value, int) or value > 0:
        eng.wait_ge(sem, value)


def wait_alone(eng, sem, value, passed):
    if not isinstance(value, int):
        eng.wait_ge(sem, value)
        eng.sem_inc(passed, 1)
    elif value > 0:
        eng.wait_ge(sem, value)


def tower(nc, io):
    with ExitStack() as ctx:
        def sb(name, shape, dt=F32):
            return ctx.enter_context(nc.sbuf_tensor(name, shape, dt))

        def sem(name):
            return ctx.enter_context(nc.semaphore(name))

        h = sb("h", [P, TILES, D])
        bn6 = sb("bn6", [P, TILES, 6])
        mean = sb("mean", [P, TILES])
        rstd = sb("rstd", [P, TILES])
        st = sb("st", [P, 4, TILES])
        ident = sb("ident", [P, P])
        ones = sb("ones", [P, P])
        xn = sb("xn", [P, TC, D])
        xT = sb("xT", [P, 2, T])
        ids = sb("ids", [P, NTAB, TILES], I32)
        idf = sb("idf", [P, 2, NTAB, TILES])
        idx = sb("idx", [P, NGATHER, TILES], I32)
        idx_now = sb("idx_now", [P, AHEAD, NGATHER, TC], I32)
        pair = sb("pair", [P, TILES])
        row_no = sb("row_no", [P, 1])
        tau = sb("tau", [P, 2, TILES])
        with ExitStack() as before:
            shared = before.enter_context(nc.sbuf_tensor("shared", [P, SHARED], F32))
        operands = ctx.enter_context(
            nc.sbuf_tensor("operands", [P, SHARED], F32R))
        n_emb = AHEAD * TC * (NGATHER + 2) * D
        emb = shared[:, 0:n_emb].rearrange("p (r c j d) -> p r c j d", r=AHEAD, c=TC,
                                               j=NGATHER + 2)
        angle = shared[:, n_emb:n_emb + 2 * TC * D].rearrange("p (c w d) -> p c w d", c=TC, w=2)
        turns = shared[:, n_emb + 2 * TC * D:n_emb + 4 * TC * D]\
            .rearrange("p (c w d) -> p c w d", c=TC, w=2)
        at = n_emb + 4 * TC * D
        t2v_w, t2v_b = (shared[:, at + x * D:at + (x + 2) * D].rearrange("p (w d) -> p w d", w=2)
                        for x in (0, 2))
        gamma, beta, pairs, modal, seg = (shared[:, at + x * D:at + (x + 1) * D]
                                          for x in (4, 5, 6, 7, 8))
        at += 9 * D
        diag, one_hot = (shared[:, at + x:at + x + 2 * T].rearrange("p (r t) -> p r t", r=2)
                         for x in (0, 2 * T))
        g_sel = sb("g_sel", [P, 2, NH, ROW])
        g_blk = sb("g_blk", [P, 2, NH])
        rel_hd = sb("rel_hd", [P, 2, NREL])
        span = sb("span", [P, 2])
        wq_n = sb("wq_n", [P, 2, D + 1])
        wq = sb("wq", [P, 2, NH * ROW])
        wk = sb("wk", [P, 2, NH, ROW])
        wk_d = sb("wk_d", [P, 2, D])
        wv = sb("wv", [P, 2, D])
        wo = sb("wo", [P, GRP, D])
        rel32 = sb("rel32", [P, NREL])
        relx = sb("relx", [P, EXT])
        rel_bd = sb("rel_bd", [P, EXT, HG])
        hmask = sb("hmask", [P, HG])
        q_mask = sb("q_mask", [P, T])
        k_ind = sb("k_ind", [STACK, T])
        qT = sb("qT", [P, GRP, T])
        q_hi = sb("q_hi", [P, GRP, T])
        q_lo = sb("q_lo", [P, GRP, T])
        k_hi = sb("k_hi", [P, GRP, T])
        k_lo = sb("k_lo", [P, GRP, T])
        stacks = operands[0:STACK, :].rearrange("p (r x g h t) -> p r x g h t",
                                                r=2, x=2, g=GRP, h=HG)
        sQ, sK = stacks[:, :, 0, :, :, :], stacks[:, :, 1, :, :, :]
        v_new = sb("v_new", [P, TC, D])
        v1 = sb("v1", [P, TC, NH, ROW])
        r_sb = sb("r_sb", [P, GRP, TC, EXT * HG])
        near = sb("near", [P, GRP * TC * KEYS * HG])
        rel = near[:, :].rearrange("p (g c k h) -> p g c k h", g=GRP, c=TC, k=KEYS)
        win = near[:, 0:NATOM * 2 * HID].rearrange("p (a t n) -> p a t n", a=NATOM, t=2)
        ssum = sb("ssum", [P, 2, TC, T])
        smin = sb("smin", [P, 2, TC])
        prob = sb("prob", [P, 2, TC, T])
        late = sb("late", [P, GRP * HG * 2 * T])
        pT = late[:, :].rearrange("p (g h s t) -> p g h s t", g=GRP, h=HG, s=2)
        gT = late[:, 0:2 * HT * T].rearrange("p (r n t) -> p r n t", r=2, n=HT)
        rsum = sb("rsum", [P, GRP, TC, HG])
        rinv = sb("rinv", [P, TC, HG])
        rinvs = sb("rinvs", [P, TC, HG, ROW])
        o_sb = sb("o_sb", [P, T])
        oT = sb("oT", [P, GRP, T])
        b2 = sb("b2", [P, D])
        NB = NCLS * B
        clsT = sb("clsT", [P, 2, NCLS, B])
        hcls = sb("hcls", [NB, D])
        bout = sb("bout", [P, 2, 2, NCLS])
        gate = sb("gate", [P, 2, NCLS, 2])
        bal = sb("bal", [P, 2, NCLS])
        taken = [0]

        def late_part(*shape):
            n = 1
            for x in shape:
                n *= x
            part = shared[:, taken[0]:taken[0] + n]
            taken[0] += n
            names = "abcd"[:len(shape)]
            return part.rearrange(f"p ({' '.join(names)}) -> p {' '.join(names)}",
                                  **dict(zip(names, shape)))

        w1 = late_part(2, HID)
        w2 = late_part(HT, D)
        wout = late_part(NATOM, HT, D)
        hidT = late_part(HT, 2, NCLS, B)
        sq = late_part(2, NB + 2 * NCLS)
        prod = late_part(2, 2, NCLS, B)
        nrm = late_part(3, NB + 2 * NCLS)
        lg = late_part(2, NCLS, B)
        mx = late_part(NCLS, B)
        den = late_part(NCLS, B)
        first = late_part(NCLS, B)
        cand = late_part(2, 2, NCLS, B)
        ycT = sb("ycT", [P, 2, NB])

        psum = ctx.enter_context(nc.psum_tensor("psum", [P, 8, 512], F32))
        scratch = nc.dram_tensor("rel_terms", [GRP, TC, P, EXT * HG], F32).ap()

        s = {n: sem(n) for n in (
            "ids_in", "small_in", "stats", "pairs_ready", "diag_ready", "id_psum", "one_hot_ready", "sum_psum", "summed", "time_in", "norm_in", "attn_in", "ffn_in", "gate_in", "wout_in", "win_in",
            "dve_chain", "pool_chain", "dve_passed", "pool_passed", "sp_passed", "idx_ok", "idx_staged", "angles",
            "sines", "h_ready", "deviation", "zeroed",
            "g_ready", "wq_psum", "wq_ready", "wk_ready", "relbd_ready", "ind_ready", "q_parts", "pT_act", "pT_dve", "inverse",
            "xn_ready", "xT_psum", "xT_ready", "qk_psum", "qk_ready", "r_psum",
            "r_ready", "v_psum", "v_ready", "v1_ready", "s_psum", "s_min", "p_ready", "pT_psum",
            "o_psum", "o_ready", "oT_ready", "out_psum", "h2_ready",
            "f_psum", "f_ready", "y_psum", "y_ready", "stored", "cls_in",
            "sq_ready", "norms_psum", "root", "root_ready", "gates", "exps", "weights",
            "hid_psum", "hid_ready", "cand_psum", "cand_ready", "yc_psum", "yc_ready")}
        gathered = [sem(f"gathered{k}") for k in range(AHEAD)]
        r_stored = [sem(f"r_stored{g}") for g in range(GRP)]
        rel_in = [sem(f"rel_in{g}") for g in range(GRP)]
        N_RD = 16 * BPT
        q_in = [sem(f"q_in{k}") for k in range(HG)]
        k_in = [sem(f"k_in{k}") for k in range(HG)]
        N_ATTN = 11
        R_SLOTS = (5, 6, 10)
        QK = {7: 0, 9: 1, 11: 2, 1: 3, 2: 4, 3: 5}
        QK_OF = [("q", 0), ("k", 0), ("k", 1), ("k", 2), ("q", 1), ("q", 2)]

        block = ctx.enter_context(nc.Block())

        S0, T0, OB, XB, QB, RB = 0, 2, 4, 5, 6, 7

        ID0, SUM0 = 0, 2

        def phase_a(step, eng, before_loop=None):
            for b in range(AHEAD):
                step(b, b, True, b > 0)
            with eng.Fori(1, B // AHEAD) as i:
                if before_loop:
                    before_loop(i - 1)
                for e in range(AHEAD):
                    step(AHEAD * i + e, e, True, True)
            if before_loop:
                before_loop(None)
            step(B, 0, False, True)

        def phase_b(eng, slot, before_loop=None):
            def body(b, r, now, before, ahead, ahead2):
                for k in range(NH):
                    slot(b, r, k, now, before, ahead, ahead2)
            body(-2, 0, False, False, False, True)
            body(-1, 1, False, False, True, True)
            body(0, 0, True, False, True, True)
            with eng.Fori(0, B // 2 - 2) as i:
                if before_loop:
                    before_loop(i)
                for r in range(2):
                    body(2 * i + r + 1, 1 - r, True, True, True, True)
            if before_loop:
                before_loop(None)
            body(B - 3, 1, True, True, True, True)
            body(B - 2, 0, True, True, True, False)
            body(B - 1, 1, True, True, False, False)
            body(B, 0, False, True, False, False)

        def copied(eng, b, k):
            if k < 0:
                b, k = b - 1, k + NH
            n, m = k // DVE_COPIES, k % DVE_COPIES
            if m == DVE_COPIES - 1:
                wait(eng, s["pT_dve"], b * (NH // DVE_COPIES) + n + 1)
            else:
                wait(eng, s["pT_act"], b * (NH - NH // DVE_COPIES) + n * (DVE_COPIES - 1) + m + 1)

        def phase_c(prepare, main, eng):
            prepare(0)
            for b in range(2):
                main(b, b)
                prepare(b + 1)
            with eng.Fori(1, B // 2 - 1) as i:
                for r in range(2):
                    main(2 * i + r, r)
                    prepare(2 * i + r + 1)
            main(B - 2, 0)
            prepare(B - 1)
            main(B - 1, 1)

        @block.sync
        def _(sp):
            def load(dst, name, sm):
                sp.dma_start(dst, io[name]).then_inc(s[sm], 16)

            load(ids[:, :, :], "ids", "ids_in")
            for dst, name in ((ident[:, :], "ident"), (ones[:, :], "ones"),
                              (row_no[:, :], "row_no"), (modal, "modal"), (seg, "seg")):
                load(dst, name, "small_in")
            load(tau[:, :, :], "tau", "time_in")
            load(t2v_w[:, :, :], "t2v_w", "time_in")
            load(t2v_b[:, :, :], "t2v_b", "time_in")
            load(gamma[:, :], "gamma", "norm_in")
            load(beta[:, :], "beta", "norm_in")
            for dst, name in ((g_sel[:, :, :, :], "g_sel"),
                              (g_blk[:, :, :], "g_blk"), (rel_hd[:, :, :], "rel_hd"),
                              (wq_n[:, :, :], "wq_n"), (wk_d[:, :, :], "wk"), (wv[:, :, :], "wv"),
                              (wo[:, :, :], "wo"), (rel32[:, :], "rel32"), (hmask[:, :], "hmask"),
                              (q_mask[:, :], "q_mask"), (k_ind[:, :], "k_ind"),
                              ):
                load(dst, name, "attn_in")
            load(b2[:, :], "b2", "ffn_in")
            for dst, name in ((bout[:, :, :, :], "bout"), (gate[:, :, :, :], "gate"),
                              (bal[:, :, :], "bal")):
                load(dst, name, "gate_in")

            def store_terms(b, g):
                wait_alone(sp, s["r_ready"], b * GRP + g + 1, s["sp_passed"])
                wait_alone(sp, rel_in[g], b * N_RD, s["sp_passed"])
                sp.dma_start(scratch[g].rearrange("c p e -> p c e"), r_sb[:, g, :, :])\
                    .then_inc(r_stored[g], 16)

            def windows(b, g):
                wait_alone(sp, r_stored[g], (b + 1) * 16, s["sp_passed"])
                wait_alone(sp, s["s_min"], (b - 1) * NH + HG * (g + 1), s["sp_passed"])
                for a in range(BPT):
                    rows = bass.AP(
                        tensor=scratch.tensor,
                        offset=(g * TC * P + a * BLK) * EXT * HG + (BLK - 1) * HG,
                        ap=[[(EXT - 1) * HG, BLK], [P * EXT * HG, TC], [1, NEAR * HG]])
                    at = NEAR_AT + a * BLK
                    sp.dma_start(rel[a * BLK:(a + 1) * BLK, g, :, at:at + NEAR, :], rows)\
                        .then_inc(rel_in[g], 16)

            sp.wait_ge(s["zeroed"], 1)
            for g in range(GRP):
                store_terms(0, g)
                windows(0, g)
            with sp.Fori(1, B) as b:
                for g in range(GRP):
                    store_terms(b, g)
                    windows(b, g)
            sp.wait_ge(s["s_psum"], B * NH)
            load(w1[:, :, :], "w1", "ffn_in")
            load(w2[:, :, :], "w2", "ffn_in")
            load(wout[:, :, :, :], "wout", "wout_in")
            sp.wait_ge(s["s_min"], B * NH)
            load(win[:, :, :, :], "win", "win_in")
            sp.wait_ge(s["h2_ready"], B)
            h_seq = h[:, :, :].rearrange("p (b c) d -> p b c d", c=TC)
            for n in range(NCLS):
                sp.dma_start(hcls[n * B:(n + 1) * B, :], h_seq[n:n + 1, :, 0, :])\
                    .then_inc(s["cls_in"], 16)
            out = io["out"].rearrange("b (c p) d -> b p c d", p=P)
            with sp.Fori(0, B) as b:
                wait_alone(sp, s["y_ready"], b + 1, s["sp_passed"])
                sp.dma_start(out[bass.ds(b, 1), :, :, :].rearrange("b p c d -> p (b c) d"),
                             h[:, bass.ds(b * TC, TC), :]).then_inc(s["stored"], 16)
            sp.wait_ge(s["stored"], 16 * B)
            sp.wait_ge(s["yc_ready"], 1)
            for n in range(NCLS):
                sp.dma_start(io["out"][:, n, :], hcls[n * B:(n + 1) * B, :])\
                    .then_inc(s["stored"], 16)
            sp.wait_ge(s["stored"], 16 * (B + NCLS))

        @block.gpsimd
        def _(pool):
            chain = Chain(pool, s["pool_chain"])
            tables = [io["word"], io["npi"], io["posi"]]
            pool.wait_ge(s["idx_ok"], 1)
            def gather(b, r):
                wait_alone(pool, s["sum_psum"], b - AHEAD + 1, s["pool_passed"])
                pool.tensor_copy(idx_now[:, r, :, :], idx[:, :, bass.ds(b * TC, TC)])\
                    .then_inc(s["idx_staged"], 1)
                wait_alone(pool, s["idx_staged"], b + 1, s["pool_passed"])
                for c in range(TC):
                    for j in range(NGATHER):
                        pool.indirect_dma_start(
                            out=emb[:, r, c, j, :], out_offset=None, in_=tables[j],
                            in_offset=bass.IndirectOffsetOnAxis(
                                ap=idx_now[:, r, j, c:c + 1], axis=0))\
                            .then_inc(gathered[r], 16)

            for e in range(AHEAD):
                gather(e, e)
            with pool.Fori(1, B // AHEAD) as i:
                for e in range(AHEAD):
                    gather(AHEAD * i + e, e)

            chain(pool.memset(near[:, :], 0.0))
            pool.sem_inc(s["zeroed"], 1)
            chain(pool.memset(v1[:, :, :, :], 1.0))
            chain(pool.memset(wk[:, :, :, :], 0.0))
            chain(pool.memset(xT[LAST:P, 1, :], 0.0))
            chain(pool.memset(clsT[LAST:P, 1, :, :], 0.0))
            chain(pool.memset(xT[LAST:LAST + 1, 1, :], 1.0))
            chain(pool.memset(clsT[LAST:LAST + 1, 1, :, :], 1.0))
            pool.sem_inc(s["zeroed"], 1)

            def stack(b, r, k, side, parts, rows):
                for n, part in enumerate(parts):
                    pool.dma_start(side[n * ROW:n * ROW + rows, r, :, k, :],
                                   part[k * ROW:k * ROW + rows, :, :].bitcast(F32R))\
                        .then_inc(k_in[k] if side is sK else q_in[k], 16)

            def stack_parts(b, r):
                wait_alone(pool, s["s_psum"], (b - 1) * NH, s["pool_passed"])
                wait_alone(pool, s["qk_ready"], b * len(QK) + QK_OF.index(("k", GRP - 1)) + 1,
                           s["pool_passed"])
                for k in range(HG):
                    stack(b, r, k, sK, (k_hi, k_lo, k_hi), HD)
                wait_alone(pool, s["q_parts"], b + 1, s["pool_passed"])
                for k in range(HG):
                    stack(b, r, k, sQ, (q_hi, q_hi, q_lo), ROW)

            def values(b):
                pool.wait_ge(s["v_ready"], b + 1)
                wait_alone(pool, s["o_psum"], b * GRP, s["pool_passed"])
                pool.tensor_copy(v1[:, :, :, 0:HD],
                                 v_new[:, :, :].rearrange("p c (h d) -> p c h d", d=HD))\
                    .then_inc(s["v1_ready"], 1)

            pool.wait_ge(s["ind_ready"], 1)
            for b in range(2):
                stack_parts(b, b)
                values(b)
            with pool.Fori(1, B // 2) as i:
                for r in range(2):
                    stack_parts(2 * i + r, r)
                    values(2 * i + r)

        @block.scalar
        def _(act):
            act.preload_act_table(ACT.Sin)

            def step(b, e, now, before):
                r = e % 2
                if now:
                    act.wait_ge(s["angles"], b + 1)
                    wait(act, s["sum_psum"], b - AHEAD + 1)
                    act.activation(emb[:, e, :, NGATHER:, D - 1:D], angle[:, :, :, D - 1:D],
                                   ACT.Copy)
                    act.activation(emb[:, e, :, NGATHER:, 0:D - 1],
                                   angle[:, :, :, 0:D - 1], ACT.Sin).then_inc(s["sines"], 1)
                if before:
                    act.wait_ge(s["sum_psum"], b)
                    act.activation(h[:, bass.ds((b - 1) * TC, TC), :],
                                   psum[:, SUM0 + 1 - r, 0:TC * D]
                                   .rearrange("p (c d) -> p c d", c=TC), ACT.Copy)\
                        .then_inc(s["summed"], 1)

            phase_a(step, act)

            def root(k):
                act.wait_ge(s["root"], k)
                act.activation(st[:, 1, :], st[:, 0, :], ACT.Sqrt).then_inc(s["root_ready"], 1)

            root(1)
            root(2)
            act.preload_act_table(ACT.Exp)

            act.wait_ge(s["attn_in"], 16 * N_ATTN)
            act.wait_ge(s["h_ready"], B)
            for r in range(2):
                last = act.activation(
                    sK[:, r, :, :, :].rearrange("p g h t -> p (g h) t"),
                    k_ind[:, None, :].to_broadcast([STACK, NH, T]), ACT.Copy)
            last.then_inc(s["ind_ready"], 1)

            def slot(b, r, k, now, before, ahead, ahead2):
                n = k + 2
                if now if n < NH else ahead:
                    unit, g, hg = b * NH + n, (n % NH) // HG, n % HG
                    act.wait_ge(s["s_min"], unit + 1)
                    wait(act, s["pT_psum"], unit - 1)
                    for c in range(TC):
                        ins = act.activation(prob[:, n % 2, c, :], ssum[:, n % 2, c, :], ACT.Exp,
                                             bias=smin[:, n % 2, c:c + 1], scale=-1.0,
                                             accum_out=rsum[:, g, c, hg:hg + 1])
                    ins.then_inc(s["p_ready"], 1)
                if now and k % DVE_COPIES < DVE_COPIES - 1:
                    act.wait_ge(s["pT_psum"], b * NH + k + 1)
                    wait(act, s["o_psum"], (b - 1) * GRP + k // HG + 1)
                    act.activation(pT[:, k // HG, k % HG, :, :]
                                   .rearrange("p s t -> p (s t)"), psum[:, T0 + k % 2, :],
                                   ACT.Copy).then_inc(s["pT_act"], 1)
                if ahead2 and k == 6:
                    u = b + 2
                    act.wait_ge(s["xT_psum"], u + 1)
                    act.activation(xT[:, 0, :], psum[:, XB, 0:T], ACT.Copy)
                    act.activation(xT[0:LAST, 1, :], psum[0:LAST, XB, T:2 * T], ACT.Copy)\
                        .then_inc(s["xT_ready"], 1)
                if before and k == 0:
                    outputs(b - 1, GRP - 1)
                if now and k in (4, 8):
                    outputs(b, k // 4 - 1)
                if ahead and k in R_SLOTS:
                    u, g = b + 1, R_SLOTS.index(k)
                    act.wait_ge(s["r_psum"], u * GRP + g + 1)
                    wait(act, r_stored[g], u * 16)
                    act.activation(r_sb[:, g, :, :].rearrange("p c e -> p (c e)"),
                                   psum[:, RB, 0:TC * EXT * HG], ACT.Copy)\
                        .then_inc(s["r_ready"], 1)
                if ahead and k == 1:
                    u = b + 1
                    act.wait_ge(s["v_psum"], u + 1)
                    wait(act, s["v1_ready"], u)
                    act.activation(v_new[:, :, :].rearrange("p c d -> p (c d)"),
                                   psum[:, XB, 0:TC * D], ACT.Copy).then_inc(s["v_ready"], 1)

            def outputs(b, g):
                act.wait_ge(s["o_psum"], b * GRP + g + 1)
                wait(act, s["oT_ready"], b * GRP + g)
                act.activation(o_sb[:, :], psum[:, OB, 0:T], ACT.Copy).then_inc(s["o_ready"], 1)

            phase_b(act, slot)

            root(3)
            act.preload_act_table(ACT.Gelu)

            def transposed(b):
                act.wait_ge(s["xT_psum"], B + b + 1)
                act.activation(xT[:, 0, :], psum[:, 6, 0:T], ACT.Copy)
                act.activation(xT[0:LAST, 1, :], psum[0:LAST, 6, T:2 * T], ACT.Copy)\
                    .then_inc(s["xT_ready"], 1)

            def gelus(b, r):
                for j in range(3):
                    act.wait_ge(s["f_psum"], b * 3 + j + 1)
                    if j == 0:
                        wait(act, s["y_psum"], b - 1)
                    act.activation(gT[:, r, 2 * j:2 * j + 2, :].rearrange("p n t -> p (n t)"),
                                   psum[:, 3 * r + j, :], ACT.Gelu).then_inc(s["f_ready"], 1)

            phase_c(transposed, gelus, act)

            act.wait_ge(s["norms_psum"], 1)
            act.activation(nrm[:, 0, :], psum[:, 3, 0:NB + 2 * NCLS], ACT.Sqrt)\
                .then_inc(s["root_ready"], 1)
            act.preload_act_table(ACT.Exp)
            act.wait_ge(s["gates"], 1)
            act.activation(lg[:, :, :, :].rearrange("p r n b -> p (r n b)"),
                           lg[:, :, :, :].rearrange("p r n b -> p (r n b)"), ACT.Exp)\
                .then_inc(s["exps"], 1)
            for j in range(3):
                act.wait_ge(s["hid_psum"], j + 1)
                act.activation(hidT[:, 2 * j:2 * j + 2, :, :, :]
                               .rearrange("p t r n b -> p (t r n b)"),
                               psum[:, j, 0:4 * NB], ACT.Gelu).then_inc(s["hid_ready"], 1)

        @block.vector
        def _(dve):
            chain = Chain(dve, s["dve_chain"])

            dve.wait_ge(s["ids_in"], 16)
            chain(dve.tensor_copy(idf[:, 0, :, :], ids[:, :, :]))
            for j, rows in enumerate(TABLE_ROWS):
                last = dve.tensor_scalar(idf[:, 1, j, :], idf[:, 0, j, :], 0.0, float(rows),
                                         ALU.is_lt, ALU.mult)
            chain(last)
            chain(dve.tensor_tensor(idf[:, 0, :, :], idf[:, 0, :, :], idf[:, 1, :, :], ALU.add))
            for j, rows in enumerate(TABLE_ROWS):
                last = dve.tensor_scalar(idf[:, 1, j, :], idf[:, 0, j, :], 0.0, float(rows - 1),
                                         ALU.max, ALU.min)
            chain(last)
            dve.tensor_copy(idx[:, :, :], idf[:, 1, 0:NGATHER, :]).then_inc(s["idx_ok"], 1)
            chain(dve.scalar_tensor_tensor(pair[:, :], idf[:, 1, NGATHER, :],
                                           float(TABLE_ROWS[NGATHER + 1]),
                                           idf[:, 1, NGATHER + 1, :], ALU.mult, ALU.add))
            dve.wait_ge(s["small_in"], 16 * 5)
            dve.tensor_tensor(pairs, modal, seg, ALU.add).then_inc(s["pairs_ready"], 1)

            dve.wait_ge(s["time_in"], 48)

            def step(b, e, now, before):
                r = e % 2
                if now:
                    wait(dve, s["id_psum"], b - 1)
                    for c in range(TC):
                        last = dve.tensor_scalar(diag[:, r, c * P:(c + 1) * P], ident[:, :],
                                                 pair[:, bass.ds(b * TC + c, 1)], None, ALU.mult)
                    last.then_inc(s["diag_ready"], 1)
                    wait(dve, s["sines"], b)
                    for c in range(TC):
                        for w in range(2):
                            last = dve.scalar_tensor_tensor(
                                angle[:, c, w, :], t2v_w[:, w, :],
                                tau[:, w, bass.ds(b * TC + c, 1)], t2v_b[:, w, :],
                                ALU.mult, ALU.add)
                    chain(last)
                    a, n = angle[:, :, :, 0:D - 1], turns[:, :, :, 0:D - 1]
                    a = a.rearrange("p c w d -> p (c w) d")
                    n = n.rearrange("p c w d -> p (c w) d")
                    chain(dve.tensor_scalar(n, a, 1.0 / TURN, ROUND, ALU.mult, ALU.add))
                    chain(dve.tensor_scalar(n, n, ROUND, None, ALU.subtract))
                    chain(dve.scalar_tensor_tensor(a, n, -TURN_HI, a, ALU.mult, ALU.add))
                    chain(dve.scalar_tensor_tensor(a, n, -TURN_LO, a, ALU.mult, ALU.add))
                    dve.tensor_scalar(a, a, HALF_TURN, -HALF_TURN, ALU.min, ALU.max)\
                        .then_inc(s["angles"], 1)
                    dve.wait_ge(s["id_psum"], b + 1)
                    wait(dve, s["sum_psum"], b - 1)
                    dve.tensor_scalar(one_hot[:, r, :], psum[:, ID0 + r, 0:T], row_no[:, 0:1],
                                      None, ALU.is_equal).then_inc(s["one_hot_ready"], 1)
                if before:
                    dve.wait_ge(s["summed"], b)
                    for c in range(TC):
                        last = dve.bn_stats(bn6[:, bass.ds((b - 1) * TC + c, 1), :],
                                            h[:, bass.ds((b - 1) * TC + c, 1), :])
                    last.then_inc(s["stats"], 1)

            def loops(i):
                if i is None:
                    chain.done(B // AHEAD - 1)
                else:
                    chain.loop(i, AHEAD * 5)

            phase_a(step, dve, loops)
            dve.wait_ge(s["stats"], B)

            def deviations(eps, k):
                m0, m1 = bn6[:, :, 1], bn6[:, :, 4]
                v0, v1_ = bn6[:, :, 2], bn6[:, :, 5]
                dve.tensor_tensor(st[:, 2, :], m0, m1, ALU.subtract)
                dve.tensor_tensor(st[:, 3, :], v0, v1_, ALU.add)
                chain(dve.tensor_tensor(mean[:, :], m0, m1, ALU.add))
                chain(dve.tensor_tensor(st[:, 2, :], st[:, 2, :], st[:, 2, :], ALU.mult))
                chain(dve.tensor_scalar(st[:, 3, :], st[:, 3, :], 1.0 / D, eps,
                                        ALU.mult, ALU.add))
                dve.tensor_scalar(mean[:, :], mean[:, :], 0.5, None, ALU.mult)
                chain(dve.scalar_tensor_tensor(st[:, 0, :], st[:, 2, :], 0.25, st[:, 3, :],
                                               ALU.mult, ALU.add))
                dve.sem_inc(s["root"], 1)
                dve.wait_ge(s["root_ready"], k)
                chain(dve.reciprocal(st[:, 2, :], st[:, 1, :]))
                chain(dve.tensor_tensor(st[:, 3, :], st[:, 2, :], st[:, 2, :], ALU.mult))
                chain(dve.tensor_tensor(st[:, 3, :], st[:, 3, :], st[:, 0, :], ALU.mult))
                chain(dve.tensor_scalar(st[:, 3, :], st[:, 3, :], -0.5, 1.5, ALU.mult, ALU.add))
                chain(dve.tensor_tensor(rstd[:, :], st[:, 3, :], st[:, 2, :], ALU.mult))

            def normalise(dst, b):
                for c in range(TC):
                    tile = bass.ds(b * TC + c, 1)
                    last = dve.tensor_scalar(dst[c], h[:, tile, :], mean[:, tile],
                                             rstd[:, tile], ALU.subtract, ALU.mult)
                return last

            dve.wait_ge(s["attn_in"], 16 * N_ATTN)
            chain(dve.tensor_tensor(span[:, :], rel_hd[:, :, NREL - 1], rel_hd[:, :, 0],
                                    ALU.subtract))
            for t in range(2):
                last = dve.tensor_scalar(g_sel[:, t, :, HD:ROW],
                                         g_blk[:, t, :, None].to_broadcast([P, NH, ROW - HD]),
                                         span[:, t:t + 1], None, ALU.mult)
            last.then_inc(s["g_ready"], 1)
            dve.wait_ge(s["zeroed"], 2)
            dve.tensor_copy(wk[:, :, :, 0:HD],
                            wk_d[:, :, :].rearrange("p t (h d) -> p t h d", d=HD))\
                .then_inc(s["wk_ready"], 1)
            dve.tensor_copy(relx[:, 0:REL - 1], rel32[:, 0:1].to_broadcast([P, REL - 1]))
            dve.tensor_copy(relx[:, REL - 1:REL - 1 + NREL], rel32[:, :])
            chain(dve.tensor_copy(relx[:, REL - 1 + NREL:EXT],
                                  rel32[:, NREL - 1:NREL].to_broadcast([P, EXT - REL + 1 - NREL])))
            chain(dve.tensor_scalar(relx[:, :], relx[:, :], rel32[:, 0:1], None, ALU.subtract))
            for k in range(HG):
                last = dve.tensor_scalar(rel_bd[:, :, k], relx[:, :], hmask[:, k:k + 1], None,
                                         ALU.mult)
            last.then_inc(s["relbd_ready"], 1)
            deviations(EPS_EMB, 1)
            dve.wait_ge(s["norm_in"], 32)
            with dve.Fori(0, TILES // 4) as i:
                chain.loop(i, 2)
                tiles = [bass.ds(4 * i + c, 1) for c in range(4)]
                for x in tiles:
                    last = dve.scalar_tensor_tensor(h[:, x, :], h[:, x, :], mean[:, x],
                                                    gamma[:, None, :], ALU.subtract, ALU.mult)
                chain(last)
                for x in tiles:
                    last = dve.scalar_tensor_tensor(h[:, x, :], h[:, x, :], rstd[:, x],
                                                    beta[:, None, :], ALU.mult, ALU.add)
                chain(last)
                for x in tiles:
                    last = dve.bn_stats(bn6[:, x, :], h[:, x, :])
                last.then_inc(s["h_ready"], 4 // TC)
            chain.done(TILES // 4)
            dve.wait_ge(s["h_ready"], B)
            deviations(EPS_LN, 2)

            dve.wait_ge(s["wq_psum"], 1)
            dve.memset(wq[:, 1, :], 0.0)
            chain(dve.tensor_copy(wq[:, 0, :], psum[:, S0, 0:NH * ROW]))
            dve.tensor_copy(wq[0:LAST + 1, 1, :], psum[0:LAST + 1, T0, 0:NH * ROW])\
                .then_inc(s["wq_ready"], 1)

            def xn_rows(b):
                wait(dve, s["xT_psum"], b)
                normalise([xn[:, c, :] for c in range(TC)], b).then_inc(s["xn_ready"], 1)

            def slot(b, r, k, now, before, ahead, ahead2):
                n = k + 2
                if now if n < NH else ahead:
                    unit, g, hg = b * NH + n, (n % NH) // HG, n % HG
                    if hg == 0:
                        dve.wait_ge(rel_in[g], (b + n // NH + 1) * N_RD)
                    wait(dve, s["p_ready"], unit - 1)
                    wait_alone(dve, s["s_psum"], unit + 1, s["dve_passed"])
                    for c in range(TC):
                        last = dve.tensor_tensor_reduce(
                            ssum[:, n % 2, c, :], psum[:, S0 + n % 2, c * T:(c + 1) * T],
                            rel[:, g, c, REL_AT[c]:REL_AT[c] + T, hg], 1.0, BIG,
                            ALU.add, ALU.min, smin[:, n % 2, c:c + 1])
                    last.then_inc(s["s_min"], 1)
                if now and k % DVE_COPIES == DVE_COPIES - 1:
                    dve.wait_ge(s["pT_psum"], b * NH + k + 1)
                    wait(dve, s["o_psum"], (b - 1) * GRP + k // HG + 1)
                    dve.tensor_copy(pT[:, k // HG, k % HG, :, :]
                                    .rearrange("p s t -> p (s t)"), psum[:, T0 + k % 2, :])\
                        .then_inc(s["pT_dve"], 1)
                if before and k == 1:
                    outputs(b - 1, GRP - 1)
                if now and k in (5, 9):
                    outputs(b, k // 4 - 1)
                if now and k in (3, 7, 11):
                    g = k // 4
                    dve.wait_ge(s["p_ready"], b * NH + HG * (g + 1))
                    chain(dve.reciprocal(rinv[:, :, :], rsum[:, g, :, :]))
                    wait(dve, s["o_psum"], b * GRP + g)
                    dve.tensor_copy(rinvs[:, :, :, :],
                                    rinv[:, :, :, None].to_broadcast([P, TC, HG, ROW]))                        .then_inc(s["inverse"], 1)
                if before and k == 4:
                    u = b - 1
                    dve.wait_ge(s["out_psum"], TC * (u + 1))
                    rows = h[:, bass.ds(u * TC, TC), :]
                    chain(dve.tensor_tensor(rows, psum[:, RB, 0:TC * D]
                                            .rearrange("p (c d) -> p c d", c=TC), rows, ALU.add))
                    for c in range(TC):
                        last = dve.bn_stats(bn6[:, bass.ds(u * TC + c, 1), :],
                                            h[:, bass.ds(u * TC + c, 1), :])
                    last.then_inc(s["h2_ready"], 1)
                if k in QK and (ahead2 if QK[k] < 3 else ahead):
                    u, n = (b + 2 if QK[k] < 3 else b + 1), QK[k]
                    what, g = QK_OF[n]
                    dve.wait_ge(s["qk_psum"], u * len(QK) + n + 1)
                    new = psum[:, QB, n % 2 * T:(n % 2 + 1) * T]
                    if what == "q":
                        dve.tensor_tensor(qT[:, g, :], new, q_mask[:, :], ALU.mult)\
                            .then_inc(s["qk_ready"], 1)
                    else:
                        if g == 0:
                            for hg in range(HG):
                                wait(dve, k_in[hg], u * 3 * 16)
                        chain(dve.tensor_scalar(k_hi[:, g, :].bitcast(I32), new.bitcast(I32),
                                                MASK, None, ALU.bitwise_and))
                        dve.tensor_tensor(k_lo[:, g, :], new, k_hi[:, g, :], ALU.subtract)\
                            .then_inc(s["qk_ready"], 1)
                    if n == len(QK) - 1:
                        for hg in range(HG):
                            wait(dve, q_in[hg], u * 3 * 16)
                        dve.wait_ge(s["qk_ready"], (u + 1) * len(QK))
                        chain(dve.tensor_scalar(q_hi[:, :, :].bitcast(I32),
                                                qT[:, :, :].bitcast(I32), MASK, None,
                                                ALU.bitwise_and))
                        dve.tensor_tensor(q_lo[:, :, :], qT[:, :, :], q_hi[:, :, :],
                                          ALU.subtract).then_inc(s["q_parts"], 1)
                if ahead2 and k == 4:
                    xn_rows(b + 2)

            def outputs(b, g):
                dve.wait_ge(s["o_ready"], b * GRP + g + 1)
                wait(dve, s["out_psum"], TC * b)
                dve.tensor_tensor(oT[:, g, :], o_sb[:, :], psum[:, OB, T:2 * T], ALU.mult)\
                    .then_inc(s["oT_ready"], 1)

            def loops(i):
                if i is None:
                    chain.done(B // 2 - 2)
                else:
                    chain.loop(i, 2 * (1 + 2 * GRP + 1))

            phase_b(dve, slot, loops)
            dve.wait_ge(s["h2_ready"], B)
            deviations(EPS_LN, 3)

            dve.wait_ge(s["ffn_in"], 48)

            def rows_of(b):
                wait(dve, s["xT_psum"], B + b)
                normalise([xn[:, c, :] for c in range(TC)], b).then_inc(s["xn_ready"], 1)

            def classes(b):
                dve.wait_ge(s["xT_ready"], B + b + 1)
                dve.tensor_copy(clsT[:, 0, :, bass.ds(b, 1)], xT[:, 0, 0:NCLS, None])
                dve.tensor_copy(clsT[0:LAST, 1, :, bass.ds(b, 1)], xT[0:LAST, 1, 0:NCLS, None])\
                    .then_inc(s["sq_ready"], 1)

            def results(b):
                rows = h[:, bass.ds(b * TC, TC), :]
                dve.wait_ge(s["cls_in"], 16 * NCLS)
                dve.wait_ge(s["y_psum"], b + 1)
                chain(dve.tensor_tensor(rows, psum[:, 7, 0:TC * D]
                                        .rearrange("p (c d) -> p c d", c=TC), rows, ALU.add))
                dve.tensor_tensor(rows, rows, b2[:, None, :].to_broadcast([P, TC, D]), ALU.add)\
                    .then_inc(s["y_ready"], 1)

            rows_of(0)
            rows_of(1)
            classes(0)
            with dve.Fori(1, B - 1) as b:
                chain.loop(b - 1, 1)
                rows_of(b + 1)
                classes(b)
                results(b - 1)
            chain.done(B - 2)
            classes(B - 1)
            results(B - 2)
            results(B - 1)

            dve.wait_ge(s["gate_in"], 48)
            dve.wait_ge(s["sq_ready"], B)
            for t, n in ((0, P), (1, LAST)):
                c = clsT[0:n, t, :, :].rearrange("p n b -> p (n b)")
                g = gate[0:n, t, :, :].rearrange("p n r -> p (n r)")
                dve.tensor_tensor(sq[0:n, t, 0:NB], c, c, ALU.mult)
                dve.tensor_tensor(sq[0:n, t, NB:], g, g, ALU.mult)
                for r in range(2):
                    last = dve.tensor_tensor(
                        prod[0:n, t, r, :, :], clsT[0:n, t, :, :],
                        gate[0:n, t, :, r:r + 1].to_broadcast([n, NCLS, B]), ALU.mult)
            last.then_inc(s["sq_ready"], 1)
            dve.wait_ge(s["root_ready"], 4)
            size = psum[:, 3, 0:NB + 2 * NCLS]
            chain(dve.tensor_scalar(nrm[:, 1, :], nrm[:, 0, :], EPS_NORM, None, ALU.max))
            chain(dve.reciprocal(nrm[:, 1, :], nrm[:, 1, :]))
            chain(dve.tensor_tensor(nrm[:, 1, :], size, nrm[:, 1, :], ALU.mult))
            chain(dve.tensor_tensor(nrm[:, 1, :], nrm[:, 0, :], nrm[:, 1, :], ALU.add))
            chain(dve.tensor_scalar(nrm[:, 1, :], nrm[:, 1, :], 0.5, EPS_NORM,
                                    ALU.mult, ALU.max))
            chain(dve.reciprocal(nrm[:, 2, :], nrm[:, 1, :]))
            by_x = nrm[:, 2, 0:NB].rearrange("p (n b) -> p n b", b=B)
            by_g = nrm[:, 2, NB:].rearrange("p (n r) -> p n r", r=2)
            dots = psum[:, 3, P:P + 2 * NB].rearrange("p (r n b) -> p r n b", r=2, n=NCLS)
            for r in range(2):
                last = dve.tensor_tensor(lg[:, r, :, :], dots[:, r, :, :], by_x, ALU.mult)
            chain(last)
            for r in range(2):
                last = dve.tensor_tensor(lg[:, r, :, :], lg[:, r, :, :],
                                         by_g[:, :, r:r + 1].to_broadcast([P, NCLS, B]), ALU.mult)
            chain(last)
            for r in range(2):
                last = dve.tensor_tensor(lg[:, r, :, :], lg[:, r, :, :],
                                         bal[:, r, :, None].to_broadcast([P, NCLS, B]), ALU.add)
            chain(last)
            chain(dve.tensor_tensor(mx[:, :, :], lg[:, 0, :, :], lg[:, 1, :, :], ALU.max))
            for r in range(2):
                last = dve.tensor_tensor(lg[:, r, :, :], lg[:, r, :, :], mx[:, :, :],
                                         ALU.subtract)
            last.then_inc(s["gates"], 1)
            dve.wait_ge(s["exps"], 1)
            chain(dve.tensor_tensor(den[:, :, :], lg[:, 0, :, :], lg[:, 1, :, :], ALU.add))
            chain(dve.reciprocal(den[:, :, :], den[:, :, :]))
            for r in range(2):
                last = dve.tensor_tensor(lg[:, r, :, :], lg[:, r, :, :], den[:, :, :], ALU.mult)
            chain(last)
            chain(dve.tensor_tensor(first[:, :, :], lg[:, 0, :, :], lg[:, 1, :, :], ALU.is_ge))
            dve.tensor_tensor(lg[:, 0, :, :], lg[:, 0, :, :], first[:, :, :], ALU.mult)
            chain(dve.tensor_scalar(mx[:, :, :], first[:, :, :], -1.0, 1.0, ALU.mult, ALU.add))
            chain(dve.tensor_tensor(lg[:, 1, :, :], lg[:, 1, :, :], mx[:, :, :], ALU.mult))
            dve.wait_ge(s["cand_psum"], 1)
            for t, n in ((0, P), (1, LAST)):
                for r in range(2):
                    last = dve.tensor_tensor(
                        cand[0:n, t, r, :, :],
                        psum[0:n, 4 + t, r * NB:(r + 1) * NB].rearrange("p (n b) -> p n b", b=B),
                        bout[0:n, t, r, :, None].to_broadcast([n, NCLS, B]), ALU.add)
            chain(last)
            for t, n in ((0, P), (1, LAST)):
                for r in range(2):
                    last = dve.tensor_tensor(cand[0:n, t, r, :, :], cand[0:n, t, r, :, :],
                                             lg[0:n, r, :, :], ALU.mult)
            chain(last)
            for t, n in ((0, P), (1, LAST)):
                last = dve.tensor_tensor(
                    ycT[0:n, t, :].rearrange("p (n b) -> p n b", b=B),
                    cand[0:n, t, 0, :, :], cand[0:n, t, 1, :, :], ALU.add)
            last.then_inc(s["cand_ready"], 1)
            dve.wait_ge(s["yc_psum"], 1)
            dve.tensor_tensor(hcls[:, :], psum[0:NB, 6, 0:D], hcls[:, :], ALU.add)\
                .then_inc(s["yc_ready"], 1)

        @block.tensor
        def _(pe):
            mm = nc.tensor.matmul

            pe.wait_ge(s["small_in"], 16 * 5)
            pe.wait_ge(s["pairs_ready"], 1)

            def step(b, e, now, before):
                r = e % 2
                if now:
                    pe.wait_ge(s["diag_ready"], b + 1)
                    wait(pe, s["one_hot_ready"], b - 1)
                    mm(psum[:, ID0 + r, 0:T], ones[:, :], diag[:, r, :], start=True, stop=True)\
                        .then_inc(s["id_psum"], 1)
                if before:
                    pe.wait_ge(s["one_hot_ready"], b)
                    pe.wait_ge(s["sines"], b)
                    wait(pe, s["summed"], b - 2)
                    last = (e - 1) % AHEAD
                    pe.wait_ge(gathered[last],
                               (b - 1 - last + AHEAD) * (16 * TC * NGATHER // AHEAD))
                    for c in range(TC):
                        out = psum[:, SUM0 + 1 - r, c * D:(c + 1) * D]
                        mm(out, one_hot[:, 1 - r, c * P:(c + 1) * P], pairs, start=True,
                           stop=False)
                        for j in range(NGATHER + 2):
                            last = mm(out, ident[:, :], emb[:, (e - 1) % AHEAD, c, j, :], start=False,
                                      stop=j == NGATHER + 1)
                    last.then_inc(s["sum_psum"], 1)

            phase_a(step, pe)

            pe.wait_ge(s["attn_in"], 16 * N_ATTN)
            pe.wait_ge(s["g_ready"], 1)
            for bank, lo, hi in ((S0, 0, P), (T0, P, D + 1)):
                for t in range(2):
                    last = mm(psum[0:hi - lo, bank, 0:NH * ROW], wq_n[:, t, lo:hi],
                              g_sel[:, t, :, :].rearrange("p h r -> p (h r)"),
                              start=t == 0, stop=t == 1)
            last.then_inc(s["wq_psum"], 1)
            pe.wait_ge(s["wq_ready"], 1)
            pe.wait_ge(s["wk_ready"], 1)
            pe.wait_ge(s["relbd_ready"], 1)
            pe.wait_ge(s["zeroed"], 2)

            def slot(b, r, k, now, before, ahead, ahead2):
                n = k + 2
                if now if n < NH else ahead:
                    unit, g, hg = b * NH + n, (n % NH) // HG, n % HG
                    u, ru = (b, r) if n < NH else (b + 1, 1 - r)
                    if g == 0:
                        pe.wait_ge(q_in[hg], (u + 1) * 3 * 16)
                        pe.wait_ge(k_in[hg], (u + 1) * 3 * 16)
                    wait(pe, s["s_min"], unit - 1)
                    for c in range(TC):
                        last = mm(psum[:, S0 + n % 2, c * T:(c + 1) * T],
                                  sQ[:, ru, g, hg, c * P:(c + 1) * P],
                                  sK[:, ru, g, hg, :], start=True, stop=True)
                    last.then_inc(s["s_psum"], 1)
                if now:
                    pe.wait_ge(s["p_ready"], b * NH + k + 1)
                    copied(pe, b, k - 2)
                    for t in range(2):
                        for c in range(TC):
                            last = nc.tensor.transpose(
                                psum[:, T0 + k % 2, t * T + c * P:t * T + (c + 1) * P],
                                prob[:, k % 2, c, t * P:(t + 1) * P], ident[:, :])
                    last.then_inc(s["pT_psum"], 1)
                if before and k == 0:
                    outputs(b - 1, GRP - 1)
                if ahead2 and k == 6:
                    u = b + 2
                    pe.wait_ge(s["xn_ready"], u + 1)
                    wait(pe, s["v_ready"], u)
                    for c in range(TC):
                        nc.tensor.transpose(psum[:, XB, c * P:(c + 1) * P], xn[:, c, 0:P],
                                            ident[:, :])
                        last = nc.tensor.transpose(psum[0:LAST, XB, T + c * P:T + (c + 1) * P],
                                                   xn[:, c, P:D], ident[:, :])
                    last.then_inc(s["xT_psum"], 1)
                if k in QK and (ahead2 if QK[k] < 3 else ahead):
                    u, n = (b + 2 if QK[k] < 3 else b + 1), QK[k]
                    what, g = QK_OF[n]
                    if n == 0:
                        pe.wait_ge(s["xT_ready"], u + 1)
                    wait(pe, s["qk_ready"], u * len(QK) + n)
                    w = wq if what == "q" else wk[:, :, :, :].rearrange("p t h r -> p t (h r)")
                    for t in range(2):
                        last = mm(psum[:, QB, n % 2 * T:(n % 2 + 1) * T],
                                  w[:, t, g * P:(g + 1) * P], xT[:, t, :],
                                  start=t == 0, stop=t == 1)
                    last.then_inc(s["qk_psum"], 1)
                if before and k in (2, 3):
                    u, c = b - 1, k - 2
                    if c == 0:
                        pe.wait_ge(s["oT_ready"], (u + 1) * GRP)
                        if isinstance(b, int):
                            wait(pe, s["r_ready"], min(b + 1, B) * GRP)
                        else:
                            pe.wait_ge(s["r_ready"], (b + 1) * GRP)
                    for g in range(GRP):
                        last = mm(psum[:, RB, c * D:(c + 1) * D],
                                  oT[:, g, c * P:(c + 1) * P], wo[:, g, :],
                                  start=g == 0, stop=g == GRP - 1)
                    last.then_inc(s["out_psum"], 1)
                if ahead and k in R_SLOTS:
                    u, g = b + 1, R_SLOTS.index(k)
                    pe.wait_ge(s["qk_ready"], u * len(QK) + QK_OF.index(("q", g)) + 1)
                    wait(pe, s["r_ready"], u * GRP + g)
                    if before and g == 0:
                        pe.wait_ge(s["h2_ready"], b)
                    for c in range(TC):
                        last = mm(psum[:, RB, c * EXT * HG:(c + 1) * EXT * HG],
                                  qT[:, g, c * P:(c + 1) * P],
                                  rel_bd[:, :, :].rearrange("p e h -> p (e h)"),
                                  start=True, stop=True)
                    last.then_inc(s["r_psum"], 1)
                if now and k in (4, 8):
                    outputs(b, k // 4 - 1)
                if ahead and k == 1:
                    u = b + 1
                    for c in range(TC):
                        for t in range(2):
                            last = mm(psum[:, XB, c * D:(c + 1) * D], xT[:, t, c * P:(c + 1) * P],
                                      wv[:, t, :], start=t == 0, stop=t == 1)
                    last.then_inc(s["v_psum"], 1)

            def outputs(b, g):
                for k in (HG - 2, HG - 1):
                    copied(pe, b, HG * g + k)
                if g == 0:
                    pe.wait_ge(s["v1_ready"], b + 1)
                wait(pe, s["oT_ready"], b * GRP + g)
                for t in range(2):
                    for k in range(HG):
                        mm(psum[k * ROW:(k + 1) * ROW, OB, 0:T],
                           v1[:, t, HG * g + k, :], pT[:, g, k, t, :],
                           start=t == 0, stop=t == 1, tile_position=(0, k * ROW))
                pe.wait_ge(s["inverse"], b * GRP + g + 1)
                for c in range(TC):
                    last = mm(psum[:, OB, T + c * P:T + (c + 1) * P],
                              rinvs[:, c, :, :].rearrange("p h r -> p (h r)"), ident[:, :],
                              start=True, stop=True)
                last.then_inc(s["o_psum"], 1)

            phase_b(pe, slot)

            pe.wait_ge(s["ffn_in"], 48)

            def transposes(b):
                pe.wait_ge(s["xn_ready"], B + b + 1)
                wait(pe, s["sq_ready"], b)
                for c in range(TC):
                    nc.tensor.transpose(psum[:, 6, c * P:(c + 1) * P], xn[:, c, 0:P], ident[:, :])
                    last = nc.tensor.transpose(psum[0:LAST, 6, T + c * P:T + (c + 1) * P],
                                               xn[:, c, P:D], ident[:, :])
                last.then_inc(s["xT_psum"], 1)

            def first(b, r):
                pe.wait_ge(s["xT_ready"], B + b + 1)
                for j in range(3):
                    wait(pe, s["f_ready"], (b - 2) * 3 + j + 1)
                    for k in range(2):
                        for t in range(2):
                            last = mm(psum[:, 3 * r + j, k * T:(k + 1) * T],
                                      w1[:, t, (2 * j + k) * P:(2 * j + k + 1) * P], xT[:, t, :],
                                      start=t == 0, stop=t == 1)
                    last.then_inc(s["f_psum"], 1)

            def second(b, r):
                pe.wait_ge(s["f_ready"], b * 3 + 3)
                wait(pe, s["y_ready"], b)
                for c in range(TC):
                    for n in range(HT):
                        last = mm(psum[:, 7, c * D:(c + 1) * D], gT[:, r, n, c * P:(c + 1) * P],
                                  w2[:, n, :], start=n == 0, stop=n == HT - 1)
                last.then_inc(s["y_psum"], 1)

            transposes(0)
            first(0, 0)
            transposes(1)
            for b in range(1, 3):
                first(b, b % 2)
                transposes(b + 1)
                second(b - 1, 1 - b % 2)
            with pe.Fori(1, B // 2 - 1) as i:
                for r in range(2):
                    first(2 * i + r + 1, 1 - r)
                    transposes(2 * i + r + 2)
                    second(2 * i + r, r)
            first(B - 1, 1)
            second(B - 2, 0)
            second(B - 1, 1)

            def of_atom(columns, route, a):
                c = columns[:, route, :, :]
                if a < 3:
                    return c[:, 2 * a:2 * a + 2, :]
                return c.rearrange("p (k q) b -> p k q b", q=2)[:, :, a - 3, :]

            pe.wait_ge(s["sq_ready"], B + 1)
            pe.wait_ge(s["f_ready"], 3 * B)
            for lo, src in ((0, sq[:, :, :]),
                            (P, prod[:, :, :, :, :].rearrange("p t r n b -> p t (r n b)"))):
                for t, n in ((0, P), (1, LAST)):
                    last = mm(psum[:, 3, lo:lo + src.shape[2]], ones[0:n, :], src[0:n, t, :],
                              start=t == 0, stop=t == 1)
            last.then_inc(s["norms_psum"], 1)
            pe.wait_ge(s["win_in"], 16)
            pe.wait_ge(s["wout_in"], 16)
            pe.wait_ge(s["f_ready"], 3 * B)
            for n in range(HT):
                hid = psum[:, n // 2, (n % 2) * 2 * NB:(n % 2 + 1) * 2 * NB]\
                    .rearrange("p (r n b) -> p r n b", r=2, n=NCLS)
                for a in range(NATOM):
                    for t in range(2):
                        last = mm(of_atom(hid, a // 3, a), win[:, a, t, n * P:(n + 1) * P],
                                  of_atom(clsT[:, t:t + 1, :, :], 0, a),
                                  start=t == 0, stop=t == 1)
                if n % 2:
                    last.then_inc(s["hid_psum"], 1)
            pe.wait_ge(s["hid_ready"], 3)
            for t, lo, hi in ((0, 0, P), (1, P, D)):
                out = psum[0:hi - lo, 4 + t, 0:2 * NB].rearrange("p (r n b) -> p r n b", r=2, n=NCLS)
                for a in range(NATOM):
                    route = 1 - a // 3
                    for n in range(HT):
                        last = mm(of_atom(out, route, a), wout[:, a, n, lo:hi],
                                  of_atom(hidT[:, n, :, :, :], route, a),
                                  start=n == 0, stop=n == HT - 1)
            last.then_inc(s["cand_psum"], 1)
            pe.wait_ge(s["cand_ready"], 1)
            nc.tensor.transpose(psum[0:NB, 6, 0:P], ycT[:, 0, :], ident[:, :])
            nc.tensor.transpose(psum[0:NB, 6, P:D], ycT[0:LAST, 1, :], ident[0:LAST, 0:LAST])\
                .then_inc(s["yc_psum"], 1)


INPUTS = ["x", "itok_BS_0_9999", "itok_BS_0_2047", "itok_BS_0_15", "itok_BS_0_3"]


def kernel(**inputs):
    import numpy as np
    import concourse.bacc as bacc
    from concourse.bass_utils import run_bass_kernel_spmd as run

    a = {k: np.asarray(v) for k, v in inputs.items()}
    t = {k[len("L0_tok_"):]: v for k, v in a.items() if k.startswith("L0_tok_")}
    at = {k[len("L0_attn_"):]: v for k, v in a.items() if k.startswith("L0_attn_")}
    f = {k[len("L0_ffn_"):]: v for k, v in a.items() if k.startswith("L0_ffn_")}

    def by_tile(v):
        return v.reshape(-1, P).T

    def rows(v):
        return np.broadcast_to(v, (P,) + v.shape)

    def halves(*parts):
        v = np.concatenate(parts, 0)
        full = np.zeros((2 * P,) + v.shape[1:], v.dtype)
        full[:v.shape[0]] = v
        return full.reshape((2, P) + v.shape[1:]).swapaxes(0, 1)

    def spread(v):
        full = np.zeros((GRP, HG, ROW) + v.shape[1:], v.dtype)
        full[:, :, :HD] = v.reshape((GRP, HG, HD) + v.shape[1:])
        return full.reshape((GRP, P) + v.shape[1:]).swapaxes(0, 1)

    def up(v):
        return np.concatenate([v, np.zeros((P - v.shape[0],) + v.shape[1:], v.dtype)], 0)

    part, tok = np.arange(P), np.arange(T)
    qkv_w, qkv_b = at["qkv_w"], at["qkv_b"]
    wo = spread(at["out_w"].T).copy()
    wo[HD, 0] = at["out_b"]
    rel_T = at["rel_pos_emb"].T
    place = (part % ROW - HD)[:, None]
    high = (part // ROW != 1)[:, None]
    q_mask = ((place < 0) | (place >= tok // BLK + 2)).astype(np.float32)
    k_ind = (high & (place == tok // BLK)).astype(np.float32)[:STACK]
    heads = (part[:, None] // ROW == np.arange(HG)).astype(np.float32)
    hd = np.arange(2 * P)
    same = (hd[:, None] // HD == np.arange(NH)) * np.float32(SCALE)
    g_sel = np.zeros((2 * P, NH, ROW), np.float32)
    g_sel[:, :, :HD] = same[:, :, None] * (hd[:, None, None] % HD == np.arange(HD))
    left, right = [0, 0, 1, 1, 2, 2], [3, 4, 3, 4, 3, 4]

    arrays = {
        "ids": np.stack([by_tile(a[n]) for n in INPUTS], 1),
        "tau": np.stack([by_tile(a["fside_BS_age_tau"]), by_tile(a["fside_BS_delays_tau"])], 1),
        "t2v_w": rows(np.stack([np.concatenate([t["age_w"][0], t["age_w0"][0]]),
                                np.concatenate([t["delay_w"][0], t["delay_w0"][0]])])),
        "t2v_b": rows(np.stack([np.concatenate([t["age_b"], t["age_b0"]]),
                                np.concatenate([t["delay_b"], t["delay_b0"]])])),
        "gamma": rows(t["ln_gamma"]), "beta": rows(t["ln_beta"]),
        "word": t["word_table"], 
        "modal": up(np.repeat(t["modalities_table"], TABLE_ROWS[4], 0)),
        "seg": up(np.tile(t["seg_table"], (TABLE_ROWS[3], 1))),
        "row_no": part[:, None].astype(np.float32),
        "npi": t["npi_table"], "posi": t["posi_table"],
        "ident": np.eye(P, dtype=np.float32),
        "g_sel": halves(g_sel), "g_blk": halves(same.astype(np.float32)),
        "rel_hd": halves(np.tile(rel_T, (NH, 1))),
        "wq_n": halves(np.concatenate([qkv_w[0:D], qkv_b[0:D, None]], 1)),
        "wk": halves(qkv_w[D:2 * D].T, qkv_b[None, D:2 * D]),
        "wv": halves(qkv_w[2 * D:].T, qkv_b[None, 2 * D:]),
        "wo": wo,
        "rel32": spread(np.tile(rel_T, (NH, 1)))[:, 0],
        "hmask": heads, "q_mask": q_mask, "k_ind": k_ind,
        "w1": halves(f["fc1_w"].T, f["fc1_b"][None]),
        "w2": f["fc2_w"].T.reshape(HT, P, D).swapaxes(0, 1), "b2": rows(f["fc2_b"]),
        "win": np.stack([halves(w.T, b[None]) for w, b in zip(f["atom_in_w"], f["atom_in_b"])], 1),
        "wout": f["atom_out_w"].transpose(0, 2, 1).reshape(NATOM, HT, P, D).transpose(2, 0, 1, 3),
        "bout": halves(np.stack([f["atom_out_b"][right].T, f["atom_out_b"][left].T], 1)),
        "gate": halves(f["gate_pair"].transpose(2, 0, 1)),
        "bal": rows(f["balance_bias"].T),
        "ones": np.ones((P, P), np.float32),
    }
    arrays = {k: np.ascontiguousarray(v) for k, v in arrays.items()}
    nc = bacc.Bacc("TRN2", target_bir_lowering=False, num_devices=1)
    io = {k: nc.dram_tensor(f"in_{k}", v.shape, mybir.dt.from_np(v.dtype),
                            kind="ExternalInput").ap() for k, v in arrays.items()}
    io["out"] = nc.dram_tensor("out_y", (B, T, D), F32, kind="ExternalOutput").ap()
    tower(nc, io)
    r = run(nc, [{f"in_{k}": v for k, v in arrays.items()}], core_ids=[0])
    return r.results[0]["out_y"]
```

```python
import concourse.bass as bass
from concourse import mybir
from contextlib import ExitStack

F32 = mybir.dt.float32
F32R = mybir.dt.float32r
I32 = mybir.dt.int32
ALU = mybir.AluOpType
ACT = mybir.ActivationFunctionType
AX = mybir.AxisListType

B, T, D = 16, 256, 192
P = 128
TC = T // P
TILES = B * TC
NH, HD = 12, 16
HG = 4
GRP = NH // HG
ROW = P // HG
REL = 16
NREL = 2 * REL + 1
BLK = 16
NEAR = 3 * BLK
EXT = NEAR + BLK - 1
BPT = P // BLK
KEYS = T + P + 2 * BLK
REL_AT = [BLK + P, BLK]
SHARED = 2 * 2 * NH * T
NEAR_AT = P
HID = 768
HT = HID // P
TABLE_ROWS = [8000, 2500, 512, 16, 4]
NTAB = len(TABLE_ROWS)
AHEAD = 4
GROUPS = B // AHEAD
GT = AHEAD * TC
LAST_GROUP = GROUPS - 1
LAST_G = LAST_GROUP * GT
NGATHER = 3
NCLS, NATOM = 6, 5
SCALE = -HD ** -0.5
EPS_EMB, EPS_LN, EPS_NORM = 1e-12, 1e-5, 1e-12
TURN = 6.283185307179586
TURN_HI = 6.28125
TURN_LO = TURN - TURN_HI
ROUND = 12582912.0
HALF_TURN = 3.1415925
BIG = 3.0e38
STACK = 3 * ROW
MASK = -(1 << 12)
DVE_COPIES = 3
LAST = D - P


class Chain:

    def __init__(self, eng, sem):
        self.eng, self.sem, self.n, self.past = eng, sem, 0, 0

    def __call__(self, instruction):
        instruction.then_inc(self.sem, 1)
        self.n += 1
        self.eng.wait_ge(self.sem, self.past + self.n)

    def loop(self, i, steps):
        self.n0, self.steps, self.past = self.n, steps, i * steps

    def done(self, iterations):
        assert self.n - self.n0 == self.steps, (self.n - self.n0, self.steps)
        self.n, self.past = self.n0 + iterations * self.steps, 0


def wait(eng, sem, value):
    if not isinstance(value, int) or value > 0:
        eng.wait_ge(sem, value)


def wait_alone(eng, sem, value, passed):
    if not isinstance(value, int):
        eng.wait_ge(sem, value)
        eng.sem_inc(passed, 1)
    elif value > 0:
        eng.wait_ge(sem, value)


def tower(nc, io):
    with ExitStack() as ctx:
        def sb(name, shape, dt=F32):
            return ctx.enter_context(nc.sbuf_tensor(name, shape, dt))

        def sem(name):
            return ctx.enter_context(nc.semaphore(name))

        h = sb("h", [P, TILES, D])
        bn6 = sb("bn6", [P, TILES, 6])
        mean = sb("mean", [P, TILES])
        rstd = sb("rstd", [P, TILES])
        st = sb("st", [P, 4, TILES])
        ident = sb("ident", [P, P])
        gamma = sb("gamma", [P, D])
        beta = sb("beta", [P, D])
        ones = sb("ones", [P, P])
        xn = sb("xn", [P, TC, D])
        xT = sb("xT", [P, 2, T])
        ids = sb("ids", [P, NTAB, TILES], I32)
        idf = sb("idf", [P, 2, NTAB, TILES])
        idx = sb("idx", [P, NGATHER, TILES], I32)
        idx_now = sb("idx_now", [P, AHEAD, NGATHER, TC], I32)
        pair = sb("pair", [P, TILES])
        row_no = sb("row_no", [P, 1])
        tau = sb("tau", [P, 2, TILES])
        with ExitStack() as around_b:
            shared = around_b.enter_context(nc.sbuf_tensor("shared", [P, SHARED], F32))
        operands = sb("operands", [P, SHARED], F32R)
        n_emb = AHEAD * TC * (NGATHER + 2) * D
        emb = shared[:, 0:n_emb].rearrange("p (r c j d) -> p r c j d", r=AHEAD, c=TC,
                                           j=NGATHER + 2)
        angle = shared[:, n_emb:n_emb + 2 * TC * D].rearrange("p (c w d) -> p c w d", c=TC, w=2)
        turns = shared[:, n_emb + 2 * TC * D:n_emb + 4 * TC * D]\
            .rearrange("p (c w d) -> p c w d", c=TC, w=2)
        at = n_emb + 4 * TC * D
        t2v_w, t2v_b = (shared[:, at + x * D:at + (x + 2) * D].rearrange("p (w d) -> p w d", w=2)
                        for x in (0, 2))
        pairs, modal, seg = (shared[:, at + x * D:at + (x + 1) * D] for x in (4, 5, 6))
        at += 7 * D
        diag, one_hot = (shared[:, at + x:at + x + 2 * T].rearrange("p (r t) -> p r t", r=2)
                         for x in (0, 2 * T))
        stacks = operands[0:STACK, :].rearrange("p (r x g h t) -> p r x g h t",
                                                r=2, x=2, g=GRP, h=HG)
        sQ, sK = stacks[:, :, 0, :, :, :], stacks[:, :, 1, :, :, :]
        near = sb("near", [P, GRP * TC * KEYS * HG])
        rel = near[:, :].rearrange("p (g c k h) -> p g c k h", g=GRP, c=TC, k=KEYS)
        win = near[:, 0:NATOM * 2 * HID].rearrange("p (a t n) -> p a t n", a=NATOM, t=2)
        late = sb("late", [P, GRP * HG * 2 * T])
        pT = late[:, :].rearrange("p (g h s t) -> p g h s t", g=GRP, h=HG, s=2)
        gT = late[:, 0:2 * HT * T].rearrange("p (r n t) -> p r n t", r=2, n=HT)
        w1_cut = late[:, 2 * HT * T:2 * HT * T + 2 * HID].rearrange("p (t n) -> p t n", t=2)
        b2 = sb("b2", [P, D])
        NB = NCLS * B
        clsT = sb("clsT", [P, 2, NCLS, B])
        hcls = sb("hcls", [NB, D])
        bout = sb("bout", [NB, 2, D])
        parity = sb("parity", [NB, 2])
        by_row = sb("by_row", [NB, 4])
        gate = sb("gate", [P, 2, NCLS, 2])
        bal = sb("bal", [P, 2, NCLS])
        taken = [0]

        def late_part(*shape):
            n = 1
            for x in shape:
                n *= x
            part = shared[:, taken[0]:taken[0] + n]
            taken[0] += n
            names = "abcd"[:len(shape)]
            return part.rearrange(f"p ({' '.join(names)}) -> p {' '.join(names)}",
                                  **dict(zip(names, shape)))

        w1 = late_part(2, HID)
        w2 = late_part(HT, D)
        wout = late_part(NATOM, HT, D)
        hidT = late_part(HT, 2, NCLS, B)
        sq = late_part(2, NB + 2 * NCLS)
        prod = late_part(2, 2, NCLS, B)
        nrm = late_part(3, NB + 2 * NCLS)
        lg = late_part(2, NCLS, B)
        mx = late_part(NCLS, B)
        den = late_part(NCLS, B)
        first = late_part(NCLS, B)
        y_cls = late_part(D)[0:NB, :]

        with ExitStack() as during_b:
            def sb_b(name, shape, dt=F32):
                return during_b.enter_context(nc.sbuf_tensor(name, shape, dt))

            g_sel = sb_b("g_sel", [P, 2, NH, ROW])
            g_blk = sb_b("g_blk", [P, 2, NH])
            rel_hd = sb_b("rel_hd", [P, 2, NREL])
            span = sb_b("span", [P, 2])
            wq_n = sb_b("wq_n", [P, 2, D + 1])
            wq = sb_b("wq", [P, 2, NH * ROW])
            wk = sb_b("wk", [P, 2, NH, ROW])
            wk_d = sb_b("wk_d", [P, 2, D])
            wv = sb_b("wv", [P, 2, D])
            wo = sb_b("wo", [P, GRP, D])
            rel32 = sb_b("rel32", [P, NREL])
            relx = sb_b("relx", [P, EXT])
            rel_bd = sb_b("rel_bd", [P, EXT, HG])
            hmask = sb_b("hmask", [P, HG])
            q_mask = sb_b("q_mask", [P, T])
            k_ind = sb_b("k_ind", [STACK, T])
            qT = sb_b("qT", [P, GRP, T])
            q_hi = sb_b("q_hi", [P, GRP, T])
            q_lo = sb_b("q_lo", [P, GRP, T])
            k_hi = sb_b("k_hi", [P, GRP, T])
            k_lo = sb_b("k_lo", [P, GRP, T])
            v_new = sb_b("v_new", [P, TC, D])
            v1 = sb_b("v1", [P, TC, NH, ROW])
            r_sb = sb_b("r_sb", [P, GRP, TC, EXT * HG])
            ssum = sb_b("ssum", [P, 2, TC, T])
            smin = sb_b("smin", [P, 2, TC])
            prob = sb_b("prob", [P, 2, TC, T])
            rsum = sb_b("rsum", [P, GRP, TC, HG])
            rinv = sb_b("rinv", [P, TC, HG])
            rinvs = sb_b("rinvs", [P, TC, HG, ROW])
            o_sb = sb_b("o_sb", [P, T])
            oT = sb_b("oT", [P, GRP, T])
        w1_hi, w1_lo = (sb(n, [P, 2, HID], F32R) for n in ("w1_hi", "w1_lo"))
        x_hi, x_lo = (sb(n, [P, 2, T], F32R) for n in ("x_hi", "x_lo"))
        x_cut = sb("x_cut", [P, 2, T])

        psum = ctx.enter_context(nc.psum_tensor("psum", [P, 8, 512], F32))
        scratch = nc.dram_tensor("rel_terms", [GRP, TC, P, EXT * HG], F32).ap()

        s = {n: sem(n) for n in (
            "dve_chain", "pool_chain", "dve_passed", "pool_passed", "sp_passed",
            "ids_in", "small_in", "time_in", "norm_in", "attn_in", "ffn_in", "gate_in",
            "wout_in", "win_in", "idx_ok", "idx_staged", "pairs_ready", "diag_ready", "id_psum",
            "one_hot_ready", "angles", "sines", "sum_psum", "summed", "stats", "h_ready",
            "zeroed",
            "g_ready", "wq_psum", "wq_ready", "wk_ready", "relbd_ready", "ind_ready",
            "q_parts", "tops_ready", "pT_act", "pT_dve", "inverse",
            "xn_ready", "xT_psum", "xT_ready", "qk_psum", "qk_ready", "r_psum",
            "r_ready", "v_psum", "v_ready", "v1_ready", "s_psum", "s_min", "p_ready", "pT_psum",
            "o_psum", "o_ready", "oT_ready", "out_psum", "h2_ready",
            "w_cuts", "w_lows", "w_highs", "x_cuts", "x_lows", "x_highs",
            "f_psum", "f_ready", "y_psum", "y_ready", "stored", "cls_in",
            "sq_ready", "norms_psum", "root", "root_ready", "gates", "exps", "weights",
            "hid_psum", "hid_ready", "cand_psum", "rows_psum", "yc_ready")}
        gathered = [sem(f"gathered{k}") for k in range(AHEAD)]
        r_stored = [sem(f"r_stored{g}") for g in range(GRP)]
        rel_in = [sem(f"rel_in{g}") for g in range(GRP)]
        N_RD = 16 * BPT
        q_in = [sem(f"q_in{k}") for k in range(HG)]
        k_in = [sem(f"k_in{k}") for k in range(HG)]
        N_ATTN = 11
        R_SLOTS = (0, 8, 10)
        QK = {7: 0, 10: 1, 11: 2, 1: 3, 2: 4, 3: 5}
        QK_OF = [("q", 0), ("k", 0), ("k", 1), ("k", 2), ("q", 1), ("q", 2)]
        TOP_SLOTS, NORM_SLOTS = (4, 6, 7, 8), (1, 4, 8)

        block = ctx.enter_context(nc.Block())

        ID0, SUM0 = 0, 2
        S0, T0, OB, XB, QB, RB = 0, 2, 4, 5, 6, 7

        def phase_a(step, eng, norm, before_loop=None):
            for b in range(AHEAD):
                step(b, b, True, b > 0)
            with eng.Fori(1, B // AHEAD) as i:
                if before_loop:
                    before_loop(i - 1)
                for e in range(AHEAD):
                    step(AHEAD * i + e, e, True, True)
                    if e:
                        norm(i - 1, e)
            if before_loop:
                before_loop(None)
            step(B, 0, False, True)

        def phase_b(eng, slot, before_slot=None, before_loop=None):
            def body(b, r, now, before, ahead, ahead2):
                for k in range(NH):
                    if isinstance(b, int) and b < 0 and before_slot:
                        before_slot(b, k)
                    slot(b, r, k, now, before, ahead, ahead2)
            body(-2, 0, False, False, False, True)
            body(-1, 1, False, False, True, True)
            body(0, 0, True, False, True, True)
            with eng.Fori(0, B // 2 - 2) as i:
                if before_loop:
                    before_loop(i)
                for r in range(2):
                    body(2 * i + r + 1, 1 - r, True, True, True, True)
            if before_loop:
                before_loop(None)
            body(B - 3, 1, True, True, True, True)
            body(B - 2, 0, True, True, True, False)
            body(B - 1, 1, True, True, False, False)
            body(B, 0, False, True, False, False)

        def copied(eng, b, k):
            if k < 0:
                b, k = b - 1, k + NH
            n, m = k // DVE_COPIES, k % DVE_COPIES
            if m == DVE_COPIES - 1:
                wait(eng, s["pT_dve"], b * (NH // DVE_COPIES) + n + 1)
            else:
                wait(eng, s["pT_act"], b * (NH - NH // DVE_COPIES) + n * (DVE_COPIES - 1) + m + 1)

        def phase_c(step, eng, before_loop=None):
            step(0, 0, True, False)
            step(1, 1, True, True)
            with eng.Fori(1, B // 2 - 1) as i:
                if before_loop:
                    before_loop(i - 1)
                for r in range(2):
                    step(2 * i + r, r, True, True)
            if before_loop:
                before_loop(None)
            step(B - 2, 0, True, True)
            step(B - 1, 1, False, True)

        @block.sync
        def _(sp):
            def load(dst, name, sm):
                sp.dma_start(dst, io[name]).then_inc(s[sm], 16)

            load(ids[:, :, :], "ids", "ids_in")
            for dst, name in ((ident[:, :], "ident"), (ones[:, :], "ones"),
                              (row_no[:, :], "row_no"), (modal, "modal"), (seg, "seg")):
                load(dst, name, "small_in")
            load(tau[:, :, :], "tau", "time_in")
            load(t2v_w[:, :, :], "t2v_w", "time_in")
            load(t2v_b[:, :, :], "t2v_b", "time_in")
            load(gamma[:, :], "gamma", "norm_in")
            load(beta[:, :], "beta", "norm_in")
            for dst, name in ((g_sel[:, :, :, :], "g_sel"),
                              (g_blk[:, :, :], "g_blk"), (rel_hd[:, :, :], "rel_hd"),
                              (wq_n[:, :, :], "wq_n"), (wk_d[:, :, :], "wk"), (wv[:, :, :], "wv"),
                              (wo[:, :, :], "wo"), (rel32[:, :], "rel32"), (hmask[:, :], "hmask"),
                              (q_mask[:, :], "q_mask"), (k_ind[:, :], "k_ind")):
                load(dst, name, "attn_in")
            load(b2[:, :], "b2", "ffn_in")
            for dst, name in ((bout[:, :, :], "bout"), (parity[:, :], "parity"),
                              (gate[:, :, :, :], "gate"),
                              (bal[:, :, :], "bal")):
                load(dst, name, "gate_in")

            def store_terms(b, g):
                wait_alone(sp, s["r_ready"], b * GRP + g + 1, s["sp_passed"])
                wait_alone(sp, rel_in[g], b * N_RD, s["sp_passed"])
                sp.dma_start(scratch[g].rearrange("c p e -> p c e"), r_sb[:, g, :, :])\
                    .then_inc(r_stored[g], 16)

            def windows(b, g):
                wait_alone(sp, r_stored[g], (b + 1) * 16, s["sp_passed"])
                wait_alone(sp, s["s_min"], (b - 1) * NH + HG * (g + 1), s["sp_passed"])
                for a in range(BPT):
                    rows = bass.AP(
                        tensor=scratch.tensor,
                        offset=(g * TC * P + a * BLK) * EXT * HG + (BLK - 1) * HG,
                        ap=[[(EXT - 1) * HG, BLK], [P * EXT * HG, TC], [1, NEAR * HG]])
                    at = NEAR_AT + a * BLK
                    sp.dma_start(rel[a * BLK:(a + 1) * BLK, g, :, at:at + NEAR, :], rows)\
                        .then_inc(rel_in[g], 16)

            sp.wait_ge(s["zeroed"], 1)
            for g in range(GRP):
                store_terms(0, g)
                windows(0, g)
            with sp.Fori(1, B) as b:
                for g in range(GRP):
                    store_terms(b, g)
                    windows(b, g)
            sp.wait_ge(s["s_psum"], B * NH)
            load(w1[:, :, :], "w1", "ffn_in")
            load(w2[:, :, :], "w2", "ffn_in")
            load(wout[:, :, :, :], "wout", "wout_in")
            sp.wait_ge(s["s_min"], B * NH)
            load(win[:, :, :, :], "win", "win_in")
            sp.wait_ge(s["h2_ready"], B)
            h_seq = h[:, :, :].rearrange("p (b c) d -> p b c d", c=TC)
            for n in range(NCLS):
                sp.dma_start(hcls[n * B:(n + 1) * B, :], h_seq[n:n + 1, :, 0, :])\
                    .then_inc(s["cls_in"], 16)
            out = io["out"].rearrange("b (c p) d -> b p c d", p=P)
            with sp.Fori(0, B) as b:
                wait_alone(sp, s["y_ready"], b + 1, s["sp_passed"])
                sp.dma_start(out[bass.ds(b, 1), :, :, :].rearrange("b p c d -> p (b c) d"),
                             h[:, bass.ds(b * TC, TC), :]).then_inc(s["stored"], 16)
            sp.wait_ge(s["stored"], 16 * B)
            sp.wait_ge(s["yc_ready"], 1)
            for n in range(NCLS):
                sp.dma_start(io["out"][:, n, :], hcls[n * B:(n + 1) * B, :])\
                    .then_inc(s["stored"], 16)
            sp.wait_ge(s["stored"], 16 * (B + NCLS))

        @block.gpsimd
        def _(pool):
            chain = Chain(pool, s["pool_chain"])
            tables = [io["word"], io["npi"], io["posi"]]
            pool.wait_ge(s["idx_ok"], 1)

            def gather(b, r):
                wait_alone(pool, s["sum_psum"], b - AHEAD + 1, s["pool_passed"])
                pool.tensor_copy(idx_now[:, r, :, :], idx[:, :, bass.ds(b * TC, TC)])\
                    .then_inc(s["idx_staged"], 1)
                wait_alone(pool, s["idx_staged"], b + 1, s["pool_passed"])
                for c in range(TC):
                    for j in range(NGATHER):
                        pool.indirect_dma_start(
                            out=emb[:, r, c, j, :], out_offset=None, in_=tables[j],
                            in_offset=bass.IndirectOffsetOnAxis(
                                ap=idx_now[:, r, j, c:c + 1], axis=0))\
                            .then_inc(gathered[r], 16)

            for e in range(AHEAD):
                gather(e, e)
            with pool.Fori(1, B // AHEAD) as i:
                for e in range(AHEAD):
                    gather(AHEAD * i + e, e)

            chain(pool.memset(near[:, :], 0.0))
            pool.sem_inc(s["zeroed"], 1)
            chain(pool.memset(v1[:, :, :, :], 1.0))
            chain(pool.memset(wk[:, :, :, :], 0.0))
            chain(pool.memset(xT[LAST:P, 1, :], 0.0))
            chain(pool.memset(clsT[LAST:P, 1, :, :], 0.0))
            chain(pool.memset(xT[LAST:LAST + 1, 1, :], 1.0))
            chain(pool.memset(clsT[LAST:LAST + 1, 1, :, :], 1.0))
            pool.sem_inc(s["zeroed"], 1)

            def stack(b, r, k, side, parts, rows):
                for n, part in parts:
                    pool.dma_start(side[n * ROW:n * ROW + rows, r, :, k, :],
                                   part[k * ROW:k * ROW + rows, :, :].bitcast(F32R))\
                        .then_inc(k_in[k] if side is sK else q_in[k], 16)

            def stack_parts(b, r):
                wait_alone(pool, s["s_psum"], (b - 1) * NH, s["pool_passed"])
                wait_alone(pool, s["qk_ready"], b * len(QK) + QK_OF.index(("k", GRP - 1)) + 1,
                           s["pool_passed"])
                for k in range(HG):
                    stack(b, r, k, sK, ((0, k_hi), (1, k_lo), (2, k_hi)), HD)
                wait_alone(pool, s["q_parts"], b + 1, s["pool_passed"])
                for k in range(HG):
                    stack(b, r, k, sQ, ((1, q_hi), (2, q_lo)), ROW)

            def values(b):
                pool.wait_ge(s["v_ready"], b + 1)
                wait_alone(pool, s["o_psum"], b * GRP, s["pool_passed"])
                pool.tensor_copy(v1[:, :, :, 0:HD],
                                 v_new[:, :, :].rearrange("p c (h d) -> p c h d", d=HD))\
                    .then_inc(s["v1_ready"], 1)

            pool.wait_ge(s["ind_ready"], 1)
            for b in range(2):
                stack_parts(b, b)
                values(b)
            with pool.Fori(1, B // 2) as i:
                for r in range(2):
                    stack_parts(2 * i + r, r)
                    values(2 * i + r)

        @block.scalar
        def _(act):
            act.preload_act_table(ACT.Sin)

            def step(b, e, now, before):
                r = e % 2
                if before:
                    act.wait_ge(s["sum_psum"], b)
                    act.activation(h[:, bass.ds((b - 1) * TC, TC), :],
                                   psum[:, SUM0 + 1 - r, 0:TC * D]
                                   .rearrange("p (c d) -> p c d", c=TC), ACT.Copy)\
                        .then_inc(s["summed"], 1)
                if now:
                    act.wait_ge(s["angles"], b + 1)
                    wait(act, s["sum_psum"], b - AHEAD + 1)
                    act.activation(emb[:, e, :, NGATHER:, D - 1:D], angle[:, :, :, D - 1:D],
                                   ACT.Copy)
                    act.activation(emb[:, e, :, NGATHER:, 0:D - 1],
                                   angle[:, :, :, 0:D - 1], ACT.Sin).then_inc(s["sines"], 1)

            def root(k, tiles=slice(0, TILES)):
                act.wait_ge(s["root"], k)
                act.activation(st[:, 1, tiles], st[:, 0, tiles], ACT.Sqrt)\
                    .then_inc(s["root_ready"], 1)

            def norm(g, part):
                if part == 1:
                    root(g + 1, bass.ds(g * GT, GT))

            phase_a(step, act, norm)
            root(GROUPS, slice(0, LAST_G))

            def slot(b, r, k, now, before, ahead, ahead2):
                n = k + 2
                if now if n < NH else ahead:
                    unit, g, hg = b * NH + n, (n % NH) // HG, n % HG
                    act.wait_ge(s["s_min"], unit + 1)
                    wait(act, s["pT_psum"], unit - 1)
                    for c in range(TC):
                        ins = act.activation(prob[:, n % 2, c, :], ssum[:, n % 2, c, :], ACT.Exp,
                                             bias=smin[:, n % 2, c:c + 1], scale=-1.0,
                                             accum_out=rsum[:, g, c, hg:hg + 1])
                    ins.then_inc(s["p_ready"], 1)
                if now and k % DVE_COPIES < DVE_COPIES - 1:
                    act.wait_ge(s["pT_psum"], b * NH + k + 1)
                    wait(act, s["o_psum"], (b - 1) * GRP + k // HG + 1)
                    act.activation(pT[:, k // HG, k % HG, :, :]
                                   .rearrange("p s t -> p (s t)"), psum[:, T0 + k % 2, :],
                                   ACT.Copy).then_inc(s["pT_act"], 1)
                if ahead2 and k == 5:
                    u = b + 2
                    act.wait_ge(s["xT_psum"], u + 1)
                    act.activation(xT[:, 0, :], psum[:, XB, 0:T], ACT.Copy)
                    act.activation(xT[0:LAST, 1, :], psum[0:LAST, XB, T:2 * T], ACT.Copy)\
                        .then_inc(s["xT_ready"], 1)
                if before and k == 1:
                    outputs(b - 1, GRP - 1)
                if now and k in (5, 9):
                    outputs(b, k // 4 - 1)
                if ahead and k in R_SLOTS:
                    u, g = b + 1, R_SLOTS.index(k)
                    act.wait_ge(s["r_psum"], u * GRP + g + 1)
                    wait(act, r_stored[g], u * 16)
                    act.activation(r_sb[:, g, :, :].rearrange("p c e -> p (c e)"),
                                   psum[:, RB, 0:TC * EXT * HG], ACT.Copy)\
                        .then_inc(s["r_ready"], 1)
                if ahead and k == 2:
                    u = b + 1
                    act.wait_ge(s["v_psum"], u + 1)
                    wait(act, s["v1_ready"], u)
                    act.activation(v_new[:, :, :].rearrange("p c d -> p (c d)"),
                                   psum[:, XB, 0:TC * D], ACT.Copy).then_inc(s["v_ready"], 1)

            def outputs(b, g):
                act.wait_ge(s["o_psum"], b * GRP + g + 1)
                wait(act, s["oT_ready"], b * GRP + g)
                act.activation(o_sb[:, :], psum[:, OB, 0:T], ACT.Copy).then_inc(s["o_ready"], 1)

            def before_slot(b, k):
                if (b, k) == (-2, 6):
                    act.wait_ge(s["attn_in"], 16 * N_ATTN)
                    act.wait_ge(s["stats"], B)
                    for r in range(2):
                        last = act.activation(
                            sK[:, r, :, :, :].rearrange("p g h t -> p (g h) t"),
                            k_ind[:, None, :].to_broadcast([STACK, NH, T]), ACT.Copy)
                    last.then_inc(s["ind_ready"], 1)
                if (b, k) == (-1, 6):
                    root(GROUPS + 1, slice(LAST_G, TILES))
                if (b, k) == (-1, 10):
                    root(GROUPS + 2, slice(LAST_G, TILES))
                    act.preload_act_table(ACT.Exp)

            phase_b(act, slot, before_slot)

            root(GROUPS + 3)
            act.preload_act_table(ACT.Gelu)

            act.wait_ge(s["w_cuts"], 1)
            act.activation(w1_hi[:, :, :], w1_cut, ACT.Copy).then_inc(s["w_highs"], 1)

            def transposed(b):
                act.wait_ge(s["xT_psum"], B + b + 1)
                act.activation(xT[:, 0, :], psum[:, 6, 0:T], ACT.Copy)
                act.activation(xT[0:LAST, 1, :], psum[0:LAST, 6, T:2 * T], ACT.Copy)\
                    .then_inc(s["xT_ready"], 1)

            def x_high(b):
                act.wait_ge(s["x_cuts"], b + 1)
                act.activation(x_hi[:, :, :], x_cut[:, :, :], ACT.Copy)\
                    .then_inc(s["x_highs"], 1)

            transposed(0)
            x_high(0)

            def step(b, r, more, before):
                for j in range(3):
                    act.wait_ge(s["f_psum"], b * 3 + j + 1)
                    if j == 0:
                        wait(act, s["y_psum"], b - 1)
                    act.activation(gT[:, r, 2 * j:2 * j + 2, :].rearrange("p n t -> p (n t)"),
                                   psum[:, 3 * r + j, :], ACT.Gelu).then_inc(s["f_ready"], 1)
                if more:
                    transposed(b + 1)
                    x_high(b + 1)

            phase_c(step, act)

            act.wait_ge(s["norms_psum"], 1)
            act.activation(nrm[:, 0, :], psum[:, 3, 0:NB + 2 * NCLS], ACT.Sqrt)\
                .then_inc(s["root_ready"], 1)
            act.preload_act_table(ACT.Exp)
            act.wait_ge(s["gates"], 1)
            act.activation(lg[:, :, :, :].rearrange("p r n b -> p (r n b)"),
                           lg[:, :, :, :].rearrange("p r n b -> p (r n b)"), ACT.Exp)\
                .then_inc(s["exps"], 1)
            for j in range(3):
                act.wait_ge(s["hid_psum"], j + 1)
                act.activation(hidT[:, 2 * j:2 * j + 2, :, :, :]
                               .rearrange("p t r n b -> p (t r n b)"),
                               psum[:, j, 0:4 * NB], ACT.Gelu).then_inc(s["hid_ready"], 1)

        @block.vector
        def _(dve):
            chain = Chain(dve, s["dve_chain"])

            dve.wait_ge(s["ids_in"], 16)
            chain(dve.tensor_copy(idf[:, 0, :, :], ids[:, :, :]))
            for j, rows in enumerate(TABLE_ROWS):
                last = dve.tensor_scalar(idf[:, 1, j, :], idf[:, 0, j, :], 0.0, float(rows),
                                         ALU.is_lt, ALU.mult)
            chain(last)
            chain(dve.tensor_tensor(idf[:, 0, :, :], idf[:, 0, :, :], idf[:, 1, :, :], ALU.add))
            for j, rows in enumerate(TABLE_ROWS):
                last = dve.tensor_scalar(idf[:, 1, j, :], idf[:, 0, j, :], 0.0, float(rows - 1),
                                         ALU.max, ALU.min)
            chain(last)
            dve.tensor_copy(idx[:, :, :], idf[:, 1, 0:NGATHER, :]).then_inc(s["idx_ok"], 1)
            chain(dve.scalar_tensor_tensor(pair[:, :], idf[:, 1, NGATHER, :],
                                           float(TABLE_ROWS[NGATHER + 1]),
                                           idf[:, 1, NGATHER + 1, :], ALU.mult, ALU.add))
            dve.wait_ge(s["small_in"], 16 * 5)
            dve.tensor_tensor(pairs, modal, seg, ALU.add).then_inc(s["pairs_ready"], 1)

            dve.wait_ge(s["time_in"], 48)

            def step(b, e, now, before):
                r = e % 2
                if now:
                    wait(dve, s["id_psum"], b - 1)
                    for c in range(TC):
                        last = dve.tensor_scalar(diag[:, r, c * P:(c + 1) * P], ident[:, :],
                                                 pair[:, bass.ds(b * TC + c, 1)], None, ALU.mult)
                    last.then_inc(s["diag_ready"], 1)
                    wait(dve, s["sines"], b)
                    for c in range(TC):
                        for w in range(2):
                            last = dve.scalar_tensor_tensor(
                                angle[:, c, w, :], t2v_w[:, w, :],
                                tau[:, w, bass.ds(b * TC + c, 1)], t2v_b[:, w, :],
                                ALU.mult, ALU.add)
                    chain(last)
                    a, n = angle[:, :, :, 0:D - 1], turns[:, :, :, 0:D - 1]
                    a = a.rearrange("p c w d -> p (c w) d")
                    n = n.rearrange("p c w d -> p (c w) d")
                    chain(dve.tensor_scalar(n, a, 1.0 / TURN, ROUND, ALU.mult, ALU.add))
                    chain(dve.tensor_scalar(n, n, ROUND, None, ALU.subtract))
                    chain(dve.scalar_tensor_tensor(a, n, -TURN_HI, a, ALU.mult, ALU.add))
                    chain(dve.scalar_tensor_tensor(a, n, -TURN_LO, a, ALU.mult, ALU.add))
                    dve.tensor_scalar(a, a, HALF_TURN, -HALF_TURN, ALU.min, ALU.max)\
                        .then_inc(s["angles"], 1)
                    dve.wait_ge(s["id_psum"], b + 1)
                    wait(dve, s["sum_psum"], b - 1)
                    dve.tensor_scalar(one_hot[:, r, :], psum[:, ID0 + r, 0:T], row_no[:, 0:1],
                                      None, ALU.is_equal).then_inc(s["one_hot_ready"], 1)
                if not isinstance(b, int) or b >= 2:
                    sum_statistics(b - 2)
                if isinstance(b, int) and b == B:
                    sum_statistics(B - 1)

            def sum_statistics(b):
                dve.wait_ge(s["summed"], b + 1)
                for c in range(TC):
                    last = dve.bn_stats(bn6[:, bass.ds(b * TC + c, 1), :],
                                        h[:, bass.ds(b * TC + c, 1), :])
                last.then_inc(s["stats"], 1)

            def variances(eps, tiles=slice(0, TILES)):
                m0, m1 = bn6[:, tiles, 1], bn6[:, tiles, 4]
                v0, v1_ = bn6[:, tiles, 2], bn6[:, tiles, 5]
                dve.tensor_tensor(st[:, 2, tiles], m0, m1, ALU.subtract)
                dve.tensor_tensor(st[:, 3, tiles], v0, v1_, ALU.add)
                chain(dve.tensor_tensor(mean[:, tiles], m0, m1, ALU.add))
                chain(dve.tensor_tensor(st[:, 2, tiles], st[:, 2, tiles], st[:, 2, tiles],
                                        ALU.mult))
                chain(dve.tensor_scalar(st[:, 3, tiles], st[:, 3, tiles], 1.0 / D, eps,
                                        ALU.mult, ALU.add))
                chain(dve.scalar_tensor_tensor(st[:, 0, tiles], st[:, 2, tiles], 0.25,
                                               st[:, 3, tiles], ALU.mult, ALU.add))
                dve.tensor_scalar(mean[:, tiles], mean[:, tiles], 0.5, None, ALU.mult)\
                    .then_inc(s["root"], 1)

            def inverses(k, tiles=slice(0, TILES)):
                dve.wait_ge(s["root_ready"], k)
                a, b, c = st[:, 0, tiles], st[:, 2, tiles], st[:, 3, tiles]
                chain(dve.reciprocal(b, st[:, 1, tiles]))
                chain(dve.tensor_tensor(c, b, b, ALU.mult))
                chain(dve.tensor_tensor(c, c, a, ALU.mult))
                chain(dve.tensor_scalar(c, c, -0.5, 1.5, ALU.mult, ALU.add))
                chain(dve.tensor_tensor(rstd[:, tiles], c, b, ALU.mult))

            def deviations(eps, k, tiles=slice(0, TILES)):
                variances(eps, tiles)
                inverses(k, tiles)

            def normalise(dst, b):
                for c in range(TC):
                    tile = bass.ds(b * TC + c, 1)
                    last = dve.tensor_scalar(dst[c], h[:, tile, :], mean[:, tile],
                                             rstd[:, tile], ALU.subtract, ALU.mult)
                return last

            def scaled(first):
                tiles = [bass.ds(first + c, 1) for c in range(4)]
                for x in tiles:
                    last = dve.scalar_tensor_tensor(h[:, x, :], h[:, x, :], mean[:, x],
                                                    gamma[:, None, :], ALU.subtract, ALU.mult)
                chain(last)
                for x in tiles:
                    last = dve.scalar_tensor_tensor(h[:, x, :], h[:, x, :], rstd[:, x],
                                                    beta[:, None, :], ALU.mult, ALU.add)
                chain(last)
                for x in tiles:
                    last = dve.bn_stats(bn6[:, x, :], h[:, x, :])
                last.then_inc(s["h_ready"], 4 // TC)

            def norm(g, part):
                if part == 1:
                    dve.wait_ge(s["stats"], (g + 1) * AHEAD)
                    variances(EPS_EMB, bass.ds(g * GT, GT))
                elif part == 2:
                    inverses(g + 1 if not isinstance(g, int) else GROUPS + 1, bass.ds(g * GT, GT))
                    scaled(g * GT)
                else:
                    scaled(g * GT + 4)

            def loops(i):
                if i is None:
                    chain.done(B // AHEAD - 1)
                else:
                    chain.loop(i, AHEAD * 5 + 4 + 5 + 4)

            dve.wait_ge(s["norm_in"], 32)
            phase_a(step, dve, norm, loops)
            dve.wait_ge(s["attn_in"], 16 * N_ATTN)
            chain(dve.tensor_tensor(span[:, :], rel_hd[:, :, NREL - 1], rel_hd[:, :, 0],
                                    ALU.subtract))
            for t in range(2):
                last = dve.tensor_scalar(g_sel[:, t, :, HD:ROW],
                                         g_blk[:, t, :, None].to_broadcast([P, NH, ROW - HD]),
                                         span[:, t:t + 1], None, ALU.mult)
            last.then_inc(s["g_ready"], 1)
            dve.wait_ge(s["zeroed"], 2)
            dve.tensor_copy(wk[:, :, :, 0:HD],
                            wk_d[:, :, :].rearrange("p t (h d) -> p t h d", d=HD))\
                .then_inc(s["wk_ready"], 1)
            dve.tensor_copy(relx[:, 0:REL - 1], rel32[:, 0:1].to_broadcast([P, REL - 1]))
            dve.tensor_copy(relx[:, REL - 1:REL - 1 + NREL], rel32[:, :])
            chain(dve.tensor_copy(relx[:, REL - 1 + NREL:EXT],
                                  rel32[:, NREL - 1:NREL].to_broadcast([P, EXT - REL + 1 - NREL])))
            chain(dve.tensor_scalar(relx[:, :], relx[:, :], rel32[:, 0:1], None, ALU.subtract))
            for k in range(HG):
                last = dve.tensor_scalar(rel_bd[:, :, k], relx[:, :], hmask[:, k:k + 1], None,
                                         ALU.mult)
            last.then_inc(s["relbd_ready"], 1)
            dve.wait_ge(s["h_ready"], B - AHEAD)
            deviations(EPS_LN, GROUPS, slice(0, LAST_G))

            dve.wait_ge(s["wq_psum"], 1)
            dve.memset(wq[:, 1, :], 0.0)
            chain(dve.tensor_copy(wq[:, 0, :], psum[:, S0, 0:NH * ROW]))
            dve.tensor_copy(wq[0:LAST + 1, 1, :], psum[0:LAST + 1, T0, 0:NH * ROW])\
                .then_inc(s["wq_ready"], 1)

            def xn_rows(b):
                wait(dve, s["xT_psum"], b)
                normalise([xn[:, c, :] for c in range(TC)], b).then_inc(s["xn_ready"], 1)

            def slot(b, r, k, now, before, ahead, ahead2):
                n = k + 2
                if now if n < NH else ahead:
                    unit, g, hg = b * NH + n, (n % NH) // HG, n % HG
                    if hg == 0:
                        dve.wait_ge(rel_in[g], (b + n // NH + 1) * N_RD)
                    wait(dve, s["p_ready"], unit - 1)
                    wait_alone(dve, s["s_psum"], unit + 1, s["dve_passed"])
                    for c in range(TC):
                        last = dve.tensor_tensor_reduce(
                            ssum[:, n % 2, c, :], psum[:, S0 + n % 2, c * T:(c + 1) * T],
                            rel[:, g, c, REL_AT[c]:REL_AT[c] + T, hg], 1.0, BIG,
                            ALU.add, ALU.min, smin[:, n % 2, c:c + 1])
                    last.then_inc(s["s_min"], 1)
                if now and k % DVE_COPIES == DVE_COPIES - 1:
                    dve.wait_ge(s["pT_psum"], b * NH + k + 1)
                    wait(dve, s["o_psum"], (b - 1) * GRP + k // HG + 1)
                    dve.tensor_copy(pT[:, k // HG, k % HG, :, :]
                                    .rearrange("p s t -> p (s t)"), psum[:, T0 + k % 2, :])\
                        .then_inc(s["pT_dve"], 1)
                if k in QK and (ahead2 if QK[k] < 3 else ahead):
                    u, n = (b + 2 if QK[k] < 3 else b + 1), QK[k]
                    what, g = QK_OF[n]
                    dve.wait_ge(s["qk_psum"], u * len(QK) + n + 1)
                    new = psum[:, QB, n % 2 * T:(n % 2 + 1) * T]
                    if what == "q":
                        wait(dve, s["q_parts"], u)
                        dve.tensor_tensor(qT[:, g, :], new, q_mask[:, :], ALU.mult)\
                            .then_inc(s["qk_ready"], 1)
                    else:
                        if g == 0:
                            for hg in range(HG):
                                wait(dve, k_in[hg], u * 3 * 16)
                        chain(dve.tensor_scalar(k_hi[:, g, :].bitcast(I32), new.bitcast(I32),
                                                MASK, None, ALU.bitwise_and))
                        dve.tensor_tensor(k_lo[:, g, :], new, k_hi[:, g, :], ALU.subtract)\
                            .then_inc(s["qk_ready"], 1)
                    if n == len(QK) - 1:
                        for hg in range(HG):
                            wait(dve, q_in[hg], u * 2 * 16)
                        dve.wait_ge(s["qk_ready"], (u + 1) * len(QK))
                        chain(dve.tensor_scalar(q_hi[:, :, :].bitcast(I32),
                                                qT[:, :, :].bitcast(I32), MASK, None,
                                                ALU.bitwise_and))
                        dve.tensor_tensor(q_lo[:, :, :], qT[:, :, :], q_hi[:, :, :],
                                          ALU.subtract).then_inc(s["q_parts"], 1)
                if before and k == 2:
                    outputs(b - 1, GRP - 1)
                if now and k in (6, 10):
                    outputs(b, k // 4 - 1)
                if now and k in (3, 7, 11):
                    g = k // 4
                    dve.wait_ge(s["p_ready"], b * NH + HG * (g + 1))
                    chain(dve.reciprocal(rinv[:, :, :], rsum[:, g, :, :]))
                    wait(dve, s["o_psum"], b * GRP + g)
                    dve.tensor_copy(rinvs[:, :, :, :],
                                    rinv[:, :, :, None].to_broadcast([P, TC, HG, ROW])).then_inc(
                        s["inverse"], 1)
                if before and k == 5:
                    u = b - 1
                    dve.wait_ge(s["out_psum"], u + 1)
                    rows = h[:, bass.ds(u * TC, TC), :]
                    chain(dve.tensor_tensor(rows, psum[:, QB, 0:TC * D]
                                            .rearrange("p (c d) -> p c d", c=TC), rows, ALU.add))
                    for c in range(TC):
                        last = dve.bn_stats(bn6[:, bass.ds(u * TC + c, 1), :],
                                            h[:, bass.ds(u * TC + c, 1), :])
                    last.then_inc(s["h2_ready"], 1)
                if ahead and k in TOP_SLOTS:
                    hg = TOP_SLOTS.index(k)
                    dve.tensor_copy(sQ[0:ROW, 1 - r, :, hg, :],
                                    q_hi[hg * ROW:(hg + 1) * ROW, :, :])\
                        .then_inc(s["tops_ready"], 1)
                if ahead2 and k == 0:
                    xn_rows(b + 2)

            def outputs(b, g):
                dve.wait_ge(s["o_ready"], b * GRP + g + 1)
                wait(dve, s["out_psum"], b)
                dve.tensor_tensor(oT[:, g, :], o_sb[:, :], psum[:, OB, T:2 * T], ALU.mult)\
                    .then_inc(s["oT_ready"], 1)

            def loops(i):
                if i is None:
                    chain.done(B // 2 - 2)
                else:
                    chain.loop(i, 2 * (1 + 2 * GRP + 1))

            def before_slot(b, k):
                if b == -1 and k in NORM_SLOTS:
                    norm(LAST_GROUP, NORM_SLOTS.index(k) + 1)
                if (b, k) == (-1, 10):
                    dve.wait_ge(s["h_ready"], B)
                    deviations(EPS_LN, GROUPS + 2, slice(LAST_G, TILES))

            phase_b(dve, slot, before_slot, loops)
            dve.wait_ge(s["h2_ready"], B)
            variances(EPS_LN)
            dve.wait_ge(s["ffn_in"], 48)
            dve.tensor_scalar(w1_cut.bitcast(I32), w1[:, :, :].bitcast(I32), MASK, None,
                              ALU.bitwise_and).then_inc(s["w_cuts"], 1)
            dve.wait_ge(s["w_cuts"], 1)
            dve.tensor_tensor(w1_lo[:, :, :], w1[:, :, :], w1_cut, ALU.subtract)\
                .then_inc(s["w_lows"], 1)
            inverses(GROUPS + 3)

            def rows_of(b):
                wait(dve, s["xT_psum"], B + b)
                normalise([xn[:, c, :] for c in range(TC)], b).then_inc(s["xn_ready"], 1)

            def classes(b):
                dve.wait_ge(s["xT_ready"], B + b + 1)
                dve.tensor_copy(clsT[:, 0, :, bass.ds(b, 1)], xT[:, 0, 0:NCLS, None])
                dve.tensor_copy(clsT[0:LAST, 1, :, bass.ds(b, 1)], xT[0:LAST, 1, 0:NCLS, None])\
                    .then_inc(s["sq_ready"], 1)

            def results(b):
                rows = h[:, bass.ds(b * TC, TC), :]
                dve.wait_ge(s["cls_in"], 16 * NCLS)
                dve.wait_ge(s["y_psum"], b + 1)
                chain(dve.tensor_tensor(rows, psum[:, 7, 0:TC * D]
                                        .rearrange("p (c d) -> p c d", c=TC), rows, ALU.add))
                dve.tensor_tensor(rows, rows, b2[:, None, :].to_broadcast([P, TC, D]), ALU.add)\
                    .then_inc(s["y_ready"], 1)

            def x_parts(b):
                dve.wait_ge(s["xT_ready"], B + b + 1)
                dve.tensor_scalar(x_cut[:, :, :].bitcast(I32), xT[:, :, :].bitcast(I32), MASK,
                                  None, ALU.bitwise_and).then_inc(s["x_cuts"], 1)
                dve.wait_ge(s["x_cuts"], b + 1)
                dve.tensor_tensor(x_lo[:, :, :], xT[:, :, :], x_cut[:, :, :], ALU.subtract)\
                    .then_inc(s["x_lows"], 1)

            rows_of(0)
            x_parts(0)
            classes(0)

            def step(b, r, more, before):
                if more:
                    rows_of(b + 1)
                    x_parts(b + 1)
                    classes(b + 1)
                if before:
                    results(b - 1)

            def loops(i):
                if i is None:
                    chain.done(B // 2 - 2)
                else:
                    chain.loop(i, 2)

            phase_c(step, dve, loops)
            results(B - 1)

            dve.wait_ge(s["gate_in"], 64)
            dve.wait_ge(s["sq_ready"], B)
            for t, n in ((0, P), (1, LAST)):
                c = clsT[0:n, t, :, :].rearrange("p n b -> p (n b)")
                g = gate[0:n, t, :, :].rearrange("p n r -> p (n r)")
                dve.tensor_tensor(sq[0:n, t, 0:NB], c, c, ALU.mult)
                dve.tensor_tensor(sq[0:n, t, NB:], g, g, ALU.mult)
                for r in range(2):
                    last = dve.tensor_tensor(
                        prod[0:n, t, r, :, :], clsT[0:n, t, :, :],
                        gate[0:n, t, :, r:r + 1].to_broadcast([n, NCLS, B]), ALU.mult)
            last.then_inc(s["sq_ready"], 1)
            dve.wait_ge(s["root_ready"], GROUPS + 4)
            size = psum[:, 3, 0:NB + 2 * NCLS]
            chain(dve.tensor_scalar(nrm[:, 1, :], nrm[:, 0, :], EPS_NORM, None, ALU.max))
            chain(dve.reciprocal(nrm[:, 1, :], nrm[:, 1, :]))
            chain(dve.tensor_tensor(nrm[:, 1, :], size, nrm[:, 1, :], ALU.mult))
            chain(dve.tensor_tensor(nrm[:, 1, :], nrm[:, 0, :], nrm[:, 1, :], ALU.add))
            chain(dve.tensor_scalar(nrm[:, 1, :], nrm[:, 1, :], 0.5, EPS_NORM,
                                    ALU.mult, ALU.max))
            chain(dve.reciprocal(nrm[:, 2, :], nrm[:, 1, :]))
            by_x = nrm[:, 2, 0:NB].rearrange("p (n b) -> p n b", b=B)
            by_g = nrm[:, 2, NB:].rearrange("p (n r) -> p n r", r=2)
            dots = psum[:, 3, P:P + 2 * NB].rearrange("p (r n b) -> p r n b", r=2, n=NCLS)
            for r in range(2):
                last = dve.tensor_tensor(lg[:, r, :, :], dots[:, r, :, :], by_x, ALU.mult)
            chain(last)
            for r in range(2):
                last = dve.tensor_tensor(lg[:, r, :, :], lg[:, r, :, :],
                                         by_g[:, :, r:r + 1].to_broadcast([P, NCLS, B]), ALU.mult)
            chain(last)
            for r in range(2):
                last = dve.tensor_tensor(lg[:, r, :, :], lg[:, r, :, :],
                                         bal[:, r, :, None].to_broadcast([P, NCLS, B]), ALU.add)
            chain(last)
            chain(dve.tensor_tensor(mx[:, :, :], lg[:, 0, :, :], lg[:, 1, :, :], ALU.max))
            for r in range(2):
                last = dve.tensor_tensor(lg[:, r, :, :], lg[:, r, :, :], mx[:, :, :],
                                         ALU.subtract)
            last.then_inc(s["gates"], 1)
            dve.wait_ge(s["exps"], 1)
            chain(dve.tensor_tensor(den[:, :, :], lg[:, 0, :, :], lg[:, 1, :, :], ALU.add))
            chain(dve.reciprocal(den[:, :, :], den[:, :, :]))
            for r in range(2):
                last = dve.tensor_tensor(lg[:, r, :, :], lg[:, r, :, :], den[:, :, :], ALU.mult)
            chain(last)
            chain(dve.tensor_tensor(first[:, :, :], lg[:, 0, :, :], lg[:, 1, :, :], ALU.is_ge))
            dve.tensor_tensor(lg[:, 0, :, :], lg[:, 0, :, :], first[:, :, :], ALU.mult)
            chain(dve.tensor_scalar(mx[:, :, :], first[:, :, :], -1.0, 1.0, ALU.mult, ALU.add))
            dve.tensor_tensor(lg[:, 1, :, :], lg[:, 1, :, :], mx[:, :, :], ALU.mult)\
                .then_inc(s["weights"], 1)
            dve.wait_ge(s["rows_psum"], 1)
            chain(dve.tensor_copy(by_row[:, 0:2], psum[0:NB, 7, 0:2]))
            for k in range(2):
                last = dve.tensor_tensor(by_row[:, 2 + k:3 + k], by_row[:, 0:1],
                                         parity[:, k:k + 1], ALU.mult)
            chain(last)
            dve.wait_ge(s["cls_in"], 16 * NCLS)
            for r in range(2):
                chain(dve.scalar_tensor_tensor(hcls[:, :], bout[:, r, :], by_row[:, r:r + 1],
                                               hcls[:, :], ALU.mult, ALU.add))
            dve.wait_ge(s["cand_psum"], 1)
            chain(dve.tensor_scalar(y_cls[:, :], psum[0:NB, 4, 0:D], by_row[:, 2:3], None,
                                    ALU.mult))
            for bank, k in ((5, 3), (6, 1)):
                chain(dve.scalar_tensor_tensor(y_cls[:, :], psum[0:NB, bank, 0:D],
                                               by_row[:, k:k + 1], y_cls[:, :],
                                               ALU.mult, ALU.add))
            dve.tensor_tensor(hcls[:, :], y_cls[:, :], hcls[:, :], ALU.add)\
                .then_inc(s["yc_ready"], 1)

        @block.tensor
        def _(pe):
            mm = nc.tensor.matmul

            pe.wait_ge(s["small_in"], 16 * 5)
            pe.wait_ge(s["pairs_ready"], 1)

            def step(b, e, now, before):
                r = e % 2
                if now:
                    pe.wait_ge(s["diag_ready"], b + 1)
                    wait(pe, s["one_hot_ready"], b - 1)
                    mm(psum[:, ID0 + r, 0:T], ones[:, :], diag[:, r, :], start=True, stop=True)\
                        .then_inc(s["id_psum"], 1)
                if before:
                    pe.wait_ge(s["one_hot_ready"], b)
                    pe.wait_ge(s["sines"], b)
                    wait(pe, s["summed"], b - 2)
                    last = (e - 1) % AHEAD
                    pe.wait_ge(gathered[last],
                               (b - 1 - last + AHEAD) * (16 * TC * NGATHER // AHEAD))
                    for c in range(TC):
                        out = psum[:, SUM0 + 1 - r, c * D:(c + 1) * D]
                        mm(out, one_hot[:, 1 - r, c * P:(c + 1) * P], pairs, start=True,
                           stop=False)
                        for j in range(NGATHER + 2):
                            last = mm(out, ident[:, :], emb[:, (e - 1) % AHEAD, c, j, :], start=False,
                                      stop=j == NGATHER + 1)
                    last.then_inc(s["sum_psum"], 1)

            phase_a(step, pe, lambda g, part: None)

            pe.wait_ge(s["attn_in"], 16 * N_ATTN)
            pe.wait_ge(s["g_ready"], 1)
            for bank, lo, hi in ((S0, 0, P), (T0, P, D + 1)):
                for t in range(2):
                    last = mm(psum[0:hi - lo, bank, 0:NH * ROW], wq_n[:, t, lo:hi],
                              g_sel[:, t, :, :].rearrange("p h r -> p (h r)"),
                              start=t == 0, stop=t == 1)
            last.then_inc(s["wq_psum"], 1)
            pe.wait_ge(s["wq_ready"], 1)
            pe.wait_ge(s["wk_ready"], 1)
            pe.wait_ge(s["relbd_ready"], 1)
            pe.wait_ge(s["zeroed"], 2)

            def slot(b, r, k, now, before, ahead, ahead2):
                n = k + 2
                if now if n < NH else ahead:
                    unit, g, hg = b * NH + n, (n % NH) // HG, n % HG
                    u, ru = (b, r) if n < NH else (b + 1, 1 - r)
                    if g == 0:
                        pe.wait_ge(q_in[hg], (u + 1) * 2 * 16)
                        pe.wait_ge(s["tops_ready"], u * HG + hg + 1)
                        pe.wait_ge(k_in[hg], (u + 1) * 3 * 16)
                    wait(pe, s["s_min"], unit - 1)
                    for c in range(TC):
                        last = mm(psum[:, S0 + n % 2, c * T:(c + 1) * T],
                                  sQ[:, ru, g, hg, c * P:(c + 1) * P],
                                  sK[:, ru, g, hg, :], start=True, stop=True)
                    last.then_inc(s["s_psum"], 1)
                if now:
                    pe.wait_ge(s["p_ready"], b * NH + k + 1)
                    copied(pe, b, k - 2)
                    for t in range(2):
                        for c in range(TC):
                            last = nc.tensor.transpose(
                                psum[:, T0 + k % 2, t * T + c * P:t * T + (c + 1) * P],
                                prob[:, k % 2, c, t * P:(t + 1) * P], ident[:, :])
                    last.then_inc(s["pT_psum"], 1)
                if before and k == 1:
                    outputs(b - 1, GRP - 1)
                if k in QK and (ahead2 if QK[k] < 3 else ahead):
                    u, n = (b + 2 if QK[k] < 3 else b + 1), QK[k]
                    what, g = QK_OF[n]
                    if n == 0:
                        pe.wait_ge(s["xT_ready"], u + 1)
                    if n == 0 and before:
                        pe.wait_ge(s["h2_ready"], b)
                    wait(pe, s["qk_ready"], u * len(QK) + n)
                    w = wq if what == "q" else wk[:, :, :, :].rearrange("p t h r -> p t (h r)")
                    for t in range(2):
                        last = mm(psum[:, QB, n % 2 * T:(n % 2 + 1) * T],
                                  w[:, t, g * P:(g + 1) * P], xT[:, t, :],
                                  start=t == 0, stop=t == 1)
                    last.then_inc(s["qk_psum"], 1)
                if before and k == 4:
                    u = b - 1
                    pe.wait_ge(s["oT_ready"], (u + 1) * GRP)
                    pe.wait_ge(s["qk_ready"],
                               len(QK) * (min(b + 2, B) if isinstance(b, int) else b + 2))
                    for c in range(TC):
                        for g in range(GRP):
                            last = mm(psum[:, QB, c * D:(c + 1) * D],
                                      oT[:, g, c * P:(c + 1) * P], wo[:, g, :],
                                      start=g == 0, stop=g == GRP - 1)
                    last.then_inc(s["out_psum"], 1)
                if ahead and k in R_SLOTS:
                    u, g = b + 1, R_SLOTS.index(k)
                    pe.wait_ge(s["qk_ready"], u * len(QK) + QK_OF.index(("q", g)) + 1)
                    wait(pe, s["r_ready"], u * GRP + g)
                    for c in range(TC):
                        last = mm(psum[:, RB, c * EXT * HG:(c + 1) * EXT * HG],
                                  qT[:, g, c * P:(c + 1) * P],
                                  rel_bd[:, :, :].rearrange("p e h -> p (e h)"),
                                  start=True, stop=True)
                    last.then_inc(s["r_psum"], 1)
                if now and k in (5, 9):
                    outputs(b, k // 4 - 1)
                if ahead2 and k == 5:
                    u = b + 2
                    pe.wait_ge(s["xn_ready"], u + 1)
                    wait(pe, s["v_ready"], u)
                    for c in range(TC):
                        nc.tensor.transpose(psum[:, XB, c * P:(c + 1) * P], xn[:, c, 0:P],
                                            ident[:, :])
                        last = nc.tensor.transpose(psum[0:LAST, XB, T + c * P:T + (c + 1) * P],
                                                   xn[:, c, P:D], ident[:, :])
                    last.then_inc(s["xT_psum"], 1)
                if ahead and k == 2:
                    u = b + 1
                    for c in range(TC):
                        for t in range(2):
                            last = mm(psum[:, XB, c * D:(c + 1) * D], xT[:, t, c * P:(c + 1) * P],
                                      wv[:, t, :], start=t == 0, stop=t == 1)
                    last.then_inc(s["v_psum"], 1)

            def outputs(b, g):
                for k in (HG - 2, HG - 1):
                    copied(pe, b, HG * g + k)
                if g == 0:
                    pe.wait_ge(s["v1_ready"], b + 1)
                wait(pe, s["oT_ready"], b * GRP + g)
                for t in range(2):
                    for k in range(HG):
                        mm(psum[k * ROW:(k + 1) * ROW, OB, 0:T],
                           v1[:, t, HG * g + k, :], pT[:, g, k, t, :],
                           start=t == 0, stop=t == 1, tile_position=(0, k * ROW))
                pe.wait_ge(s["inverse"], b * GRP + g + 1)
                for c in range(TC):
                    last = mm(psum[:, OB, T + c * P:T + (c + 1) * P],
                              rinvs[:, c, :, :].rearrange("p h r -> p (h r)"), ident[:, :],
                              start=True, stop=True)
                last.then_inc(s["o_psum"], 1)

            phase_b(pe, slot)

            pe.wait_ge(s["w_lows"], 1)
            pe.wait_ge(s["w_highs"], 1)

            def transposes(b):
                pe.wait_ge(s["xn_ready"], B + b + 1)
                wait(pe, s["sq_ready"], b)
                for c in range(TC):
                    nc.tensor.transpose(psum[:, 6, c * P:(c + 1) * P], xn[:, c, 0:P], ident[:, :])
                    last = nc.tensor.transpose(psum[0:LAST, 6, T + c * P:T + (c + 1) * P],
                                               xn[:, c, P:D], ident[:, :])
                last.then_inc(s["xT_psum"], 1)

            def first(b, r):
                pe.wait_ge(s["x_highs"], b + 1)
                pe.wait_ge(s["x_lows"], b + 1)
                passes = [(w, x, t) for w, x in ((w1_hi, x_hi), (w1_hi, x_lo), (w1_lo, x_hi))
                          for t in range(2)]
                for j in range(3):
                    wait(pe, s["f_ready"], (b - 2) * 3 + j + 1)
                    for k in range(2):
                        for n, (w, x, t) in enumerate(passes):
                            last = mm(psum[:, 3 * r + j, k * T:(k + 1) * T],
                                      w[:, t, (2 * j + k) * P:(2 * j + k + 1) * P], x[:, t, :],
                                      start=n == 0, stop=n == len(passes) - 1)
                    last.then_inc(s["f_psum"], 1)

            def second(b, r):
                pe.wait_ge(s["f_ready"], b * 3 + 3)
                wait(pe, s["y_ready"], b)
                for c in range(TC):
                    for n in range(HT):
                        last = mm(psum[:, 7, c * D:(c + 1) * D], gT[:, r, n, c * P:(c + 1) * P],
                                  w2[:, n, :], start=n == 0, stop=n == HT - 1)
                last.then_inc(s["y_psum"], 1)

            transposes(0)

            def step(b, r, more, before):
                first(b, r)
                if more:
                    transposes(b + 1)
                if before:
                    second(b - 1, 1 - r)

            phase_c(step, pe)
            second(B - 1, 1)

            def of_atom(columns, route, a):
                c = columns[:, route, :, :]
                if a < 3:
                    return c[:, 2 * a:2 * a + 2, :]
                return c.rearrange("p (k q) b -> p k q b", q=2)[:, :, a - 3, :]

            pe.wait_ge(s["sq_ready"], B + 1)
            pe.wait_ge(s["f_ready"], 3 * B)
            for lo, src in ((0, sq[:, :, :]),
                            (P, prod[:, :, :, :, :].rearrange("p t r n b -> p t (r n b)"))):
                for t, n in ((0, P), (1, LAST)):
                    last = mm(psum[:, 3, lo:lo + src.shape[2]], ones[0:n, :], src[0:n, t, :],
                              start=t == 0, stop=t == 1)
            last.then_inc(s["norms_psum"], 1)
            pe.wait_ge(s["win_in"], 16)
            pe.wait_ge(s["wout_in"], 16)
            pe.wait_ge(s["f_ready"], 3 * B)
            for n in range(HT):
                hid = psum[:, n // 2, (n % 2) * 2 * NB:(n % 2 + 1) * 2 * NB]\
                    .rearrange("p (r n b) -> p r n b", r=2, n=NCLS)
                for a in range(NATOM):
                    for t in range(2):
                        last = mm(of_atom(hid, a // 3, a), win[:, a, t, n * P:(n + 1) * P],
                                  of_atom(clsT[:, t:t + 1, :, :], 0, a),
                                  start=t == 0, stop=t == 1)
                if n % 2:
                    last.then_inc(s["hid_psum"], 1)
            pe.wait_ge(s["weights"], 1)
            pe.wait_ge(s["y_ready"], B)
            for r in range(2):
                last = mm(psum[0:NB, 7, r:r + 1], lg[:, r, :, :].rearrange("p n b -> p (n b)"),
                          ident[:, 0:1], start=True, stop=True)
            last.then_inc(s["rows_psum"], 1)
            pe.wait_ge(s["hid_ready"], 3)
            for a in (3, 4):
                for n in range(HT):
                    mm(psum[0:NB, a + 1, 0:D],
                       hidT[:, n, 0, :, :].rearrange("p n b -> p (n b)"), wout[:, a, n, :],
                       start=n == 0, stop=n == HT - 1)
            for n in range(HT):
                for a in range(3):
                    last = mm(psum[a * 2 * B:(a + 1) * 2 * B, 6, 0:D],
                              hidT[:, n, 1, 2 * a:2 * a + 2, :].rearrange("p n b -> p (n b)"),
                              wout[:, a, n, :], start=n == 0, stop=n == HT - 1,
                              tile_position=(0, a * 2 * B))
            last.then_inc(s["cand_psum"], 1)


INPUTS = ["x", "itok_BS_0_9999", "itok_BS_0_2047", "itok_BS_0_15", "itok_BS_0_3"]


def kernel(**inputs):
    import numpy as np
    import concourse.bacc as bacc
    from concourse.bass_utils import run_bass_kernel_spmd as run

    a = {k: np.asarray(v) for k, v in inputs.items()}
    t = {k[len("L0_tok_"):]: v for k, v in a.items() if k.startswith("L0_tok_")}
    at = {k[len("L0_attn_"):]: v for k, v in a.items() if k.startswith("L0_attn_")}
    f = {k[len("L0_ffn_"):]: v for k, v in a.items() if k.startswith("L0_ffn_")}

    def by_tile(v):
        return v.reshape(-1, P).T

    def rows(v):
        return np.broadcast_to(v, (P,) + v.shape)

    def halves(*parts):
        v = np.concatenate(parts, 0)
        full = np.zeros((2 * P,) + v.shape[1:], v.dtype)
        full[:v.shape[0]] = v
        return full.reshape((2, P) + v.shape[1:]).swapaxes(0, 1)

    def spread(v):
        full = np.zeros((GRP, HG, ROW) + v.shape[1:], v.dtype)
        full[:, :, :HD] = v.reshape((GRP, HG, HD) + v.shape[1:])
        return full.reshape((GRP, P) + v.shape[1:]).swapaxes(0, 1)

    def up(v):
        return np.concatenate([v, np.zeros((P - v.shape[0],) + v.shape[1:], v.dtype)], 0)

    part, tok = np.arange(P), np.arange(T)
    qkv_w, qkv_b = at["qkv_w"], at["qkv_b"]
    wo = spread(at["out_w"].T).copy()
    wo[HD, 0] = at["out_b"]
    rel_T = at["rel_pos_emb"].T
    place = (part % ROW - HD)[:, None]
    high = (part // ROW != 1)[:, None]
    q_mask = ((place < 0) | (place >= tok // BLK + 2)).astype(np.float32)
    k_ind = (high & (place == tok // BLK)).astype(np.float32)[:STACK]
    heads = (part[:, None] // ROW == np.arange(HG)).astype(np.float32)
    hd = np.arange(2 * P)
    same = (hd[:, None] // HD == np.arange(NH)) * np.float32(SCALE)
    g_sel = np.zeros((2 * P, NH, ROW), np.float32)
    g_sel[:, :, :HD] = same[:, :, None] * (hd[:, None, None] % HD == np.arange(HD))
    left, right = [0, 0, 1, 1, 2, 2], [3, 4, 3, 4, 3, 4]

    arrays = {
        "ids": np.stack([by_tile(a[n]) for n in INPUTS], 1),
        "tau": np.stack([by_tile(a["fside_BS_age_tau"]), by_tile(a["fside_BS_delays_tau"])], 1),
        "t2v_w": rows(np.stack([np.concatenate([t["age_w"][0], t["age_w0"][0]]),
                                np.concatenate([t["delay_w"][0], t["delay_w0"][0]])])),
        "t2v_b": rows(np.stack([np.concatenate([t["age_b"], t["age_b0"]]),
                                np.concatenate([t["delay_b"], t["delay_b0"]])])),
        "gamma": rows(t["ln_gamma"]), "beta": rows(t["ln_beta"]),
        "word": t["word_table"], 
        "modal": up(np.repeat(t["modalities_table"], TABLE_ROWS[4], 0)),
        "seg": up(np.tile(t["seg_table"], (TABLE_ROWS[3], 1))),
        "row_no": part[:, None].astype(np.float32),
        "npi": t["npi_table"], "posi": t["posi_table"],
        "ident": np.eye(P, dtype=np.float32),
        "g_sel": halves(g_sel), "g_blk": halves(same.astype(np.float32)),
        "rel_hd": halves(np.tile(rel_T, (NH, 1))),
        "wq_n": halves(np.concatenate([qkv_w[0:D], qkv_b[0:D, None]], 1)),
        "wk": halves(qkv_w[D:2 * D].T, qkv_b[None, D:2 * D]),
        "wv": halves(qkv_w[2 * D:].T, qkv_b[None, 2 * D:]),
        "wo": wo,
        "rel32": spread(np.tile(rel_T, (NH, 1)))[:, 0],
        "hmask": heads, "q_mask": q_mask, "k_ind": k_ind,
        "w1": halves(f["fc1_w"].T, f["fc1_b"][None]),
        "w2": f["fc2_w"].T.reshape(HT, P, D).swapaxes(0, 1), "b2": rows(f["fc2_b"]),
        "win": np.stack([halves(w.T, b[None]) for w, b in zip(f["atom_in_w"], f["atom_in_b"])], 1),
        "wout": f["atom_out_w"].transpose(0, 2, 1).reshape(NATOM, HT, P, D).transpose(2, 0, 1, 3),
        "bout": np.repeat(np.stack([f["atom_out_b"][right], f["atom_out_b"][left]], 1), B, 0),
        "parity": np.repeat(np.arange(NCLS)[:, None] % 2 == np.arange(2), B, 0)
        .astype(np.float32),
        "gate": halves(f["gate_pair"].transpose(2, 0, 1)),
        "bal": rows(f["balance_bias"].T),
        "ones": np.ones((P, P), np.float32),
    }
    arrays = {k: np.ascontiguousarray(v) for k, v in arrays.items()}
    nc = bacc.Bacc("TRN2", target_bir_lowering=False, num_devices=1)
    io = {k: nc.dram_tensor(f"in_{k}", v.shape, mybir.dt.from_np(v.dtype),
                            kind="ExternalInput").ap() for k, v in arrays.items()}
    io["out"] = nc.dram_tensor("out_y", (B, T, D), F32, kind="ExternalOutput").ap()
    tower(nc, io)
    r = run(nc, [{f"in_{k}": v for k, v in arrays.items()}], core_ids=[0])
    return r.results[0]["out_y"]
```
